# Optimizing a Trainium2 kernel written in Bass

```python
import numpy as np
import jax
import jax.numpy as jnp

def _softmax(x, axis=-1):
    return jax.nn.softmax(x, axis=axis)

def _gelu(x):
    return jax.nn.gelu(x, approximate=True)

def _silu(x):
    return jax.nn.silu(x)

def _sigmoid(x):
    return jax.nn.sigmoid(x)

def _layernorm(x, axis=-1, eps=1e-05):
    m = jnp.mean(x, axis=axis, keepdims=True)
    v = jnp.var(x, axis=axis, keepdims=True)
    return (x - m) / jnp.sqrt(v + eps)

def _scatter_add(tgt, idx, src, axis=0):
    return tgt.at[idx].add(src)

def _segment_sum(src, seg, n):
    return jax.ops.segment_sum(src, seg, n)
kernel_name = 'mk_macaron_d2_jaxref_r8_4e11c7'

def setup_inputs(seed: int=0):
    np.random.seed(seed)
    _w = jnp.asarray

    def _L0_attn_setup():
        import jax, jax.numpy as jnp
        import numpy as np
        HIDDEN = 512
        N_HEADS = 32
        N_KV = 8
        HEAD_DIM = HIDDEN // N_HEADS
        Q_PER_KV = N_HEADS // N_KV
        SEQ = 256
        ROPE_BASE = 1000000.0
        POS_SCALE = 1.0
        SM_SCALE = 1.0 / HEAD_DIM
        BLOCK = 64
        LOCAL_BLOCKS = 16
        VERT_STRIDE = 8

        def _blocksparse_mask(seq_len):
            nb = seq_len // BLOCK
            qb = np.arange(nb)[:, None]
            kb = np.arange(nb)[None, :]
            bmask = (kb <= qb) & ((qb - kb < LOCAL_BLOCKS) | ((kb + 1) % VERT_STRIDE == 0))
            emask = np.kron(bmask, np.ones((BLOCK, BLOCK), dtype=bool))
            i = np.arange(seq_len)
            emask &= i[:, None] >= i[None, :]
            return jnp.asarray(emask)

        def _rope(x, cos, sin):
            x1, x2 = jnp.split(x, 2, axis=-1)
            rot = jnp.concatenate([-x2, x1], axis=-1)
            return x * cos[None, :, None, :] + rot * sin[None, :, None, :]
        key = jax.random.key(seed)
        k1, k2, k3, k4, k5 = jax.random.split(key, 5)
        qkv_out = (N_HEADS + 2 * N_KV) * HEAD_DIM
        return {'hidden_states': jax.random.normal(k1, (1, SEQ, HIDDEN), dtype=jnp.float32), 'w_qkv': jax.random.normal(k2, (qkv_out, HIDDEN), dtype=jnp.float32) * 0.02, 'b_qkv': jnp.zeros((qkv_out,), dtype=jnp.float32), 'w_dense': jax.random.normal(k3, (HIDDEN, HIDDEN), dtype=jnp.float32) * 0.02, 'b_dense': jnp.zeros((HIDDEN,), dtype=jnp.float32)}
    _L0_attn_in = _L0_attn_setup()

    def _L0_ffn_setup():
        import jax, jax.numpy as jnp
        import numpy as np
        H = 512
        I = 256
        E = 16
        TOPK = 4
        SI = 256
        key = jax.random.key(seed)
        ks = jax.random.split(key, 9)
        s = 0.02
        return {'hidden_states': jax.random.normal(ks[0], (2, 256, H), dtype=jnp.float32), 'gate_w': jax.random.normal(ks[1], (E, H), dtype=jnp.float32) * s, 'bias': jnp.zeros((E,), dtype=jnp.float32), 'Wg': jax.random.normal(ks[2], (E, I, H), dtype=jnp.float32) * s, 'Wu': jax.random.normal(ks[3], (E, I, H), dtype=jnp.float32) * s, 'Wd': jax.random.normal(ks[4], (E, H, I), dtype=jnp.float32) * s, 'Sg': jax.random.normal(ks[5], (SI, H), dtype=jnp.float32) * s, 'Su': jax.random.normal(ks[6], (SI, H), dtype=jnp.float32) * s, 'Sd': jax.random.normal(ks[7], (H, SI), dtype=jnp.float32) * s}
    _L0_ffn_in = _L0_ffn_setup()

    def _L1_attn_setup():
        import jax, jax.numpy as jnp
        import numpy as np
        H = 512
        D = H // 4
        key = jax.random.key(seed)
        k1, k2, k3, k4, k5 = jax.random.split(key, 5)
        x = jax.random.normal(k1, (4, 512, H), dtype=jnp.float32)
        s_in = 1.0 / np.sqrt(H)
        Wqkv = jax.random.normal(k2, (H, 3 * D), dtype=jnp.float32) * s_in
        bqkv = jax.random.normal(k3, (3 * D,), dtype=jnp.float32) * 0.01
        Wo = jax.random.normal(k4, (D, H), dtype=jnp.float32) * (1.0 / np.sqrt(D))
        bo = jax.random.normal(k5, (H,), dtype=jnp.float32) * 0.01
        return {'x': x, 'Wqkv': Wqkv, 'bqkv': bqkv, 'Wo': Wo, 'bo': bo}
    _L1_attn_in = _L1_attn_setup()

    def _L1_ffn_setup():
        import jax, jax.numpy as jnp
        import numpy as np
        B, L, H, Dh, M = (4, 256, 16, 32, 128)
        D = H * Dh
        key = jax.random.key(seed)
        kx, ku, kd, kp = jax.random.split(key, 4)
        x = jax.random.normal(kx, (B, L, D), dtype=jnp.float32)
        up = jax.random.normal(ku, (H, Dh, M), dtype=jnp.float32)
        down = jax.random.normal(kd, (H, M, Dh), dtype=jnp.float32)
        perm = jax.random.permutation(kp, D)
        return {'x': x, 'up': up, 'down': down, 'perm': perm}
    _L1_ffn_in = _L1_ffn_setup()
    _d = {'L0_attn_hidden_states': _L0_attn_in['hidden_states'], 'L0_attn_w_qkv': _L0_attn_in['w_qkv'], 'L0_attn_b_qkv': _L0_attn_in['b_qkv'], 'L0_attn_w_dense': _L0_attn_in['w_dense'], 'L0_attn_b_dense': _L0_attn_in['b_dense'], 'L0_ffn_gate_w': _L0_ffn_in['gate_w'], 'L0_ffn_bias': _L0_ffn_in['bias'], 'L0_ffn_Wg': _L0_ffn_in['Wg'], 'L0_ffn_Wu': _L0_ffn_in['Wu'], 'L0_ffn_Wd': _L0_ffn_in['Wd'], 'L0_ffn_Sg': _L0_ffn_in['Sg'], 'L0_ffn_Su': _L0_ffn_in['Su'], 'L0_ffn_Sd': _L0_ffn_in['Sd'], 'L1_attn_Wqkv': _L1_attn_in['Wqkv'], 'L1_attn_bqkv': _L1_attn_in['bqkv'], 'L1_attn_Wo': _L1_attn_in['Wo'], 'L1_attn_bo': _L1_attn_in['bo'], 'L1_ffn_up': _L1_ffn_in['up'], 'L1_ffn_down': _L1_ffn_in['down'], 'L1_ffn_perm': _L1_ffn_in['perm']}
    _x0 = _d['L0_attn_hidden_states']
    _d['L0_attn_hidden_states'] = jax.random.normal(jax.random.fold_in(jax.random.key(seed), 1), (1, 1024, 512), dtype=_x0.dtype)
    del _x0
    return _d

def reference(L0_attn_hidden_states, L0_attn_w_qkv, L0_attn_b_qkv, L0_attn_w_dense, L0_attn_b_dense, L0_ffn_gate_w, L0_ffn_bias, L0_ffn_Wg, L0_ffn_Wu, L0_ffn_Wd, L0_ffn_Sg, L0_ffn_Su, L0_ffn_Sd, L1_attn_Wqkv, L1_attn_bqkv, L1_attn_Wo, L1_attn_bo, L1_ffn_up, L1_ffn_down, L1_ffn_perm):

    def _L0_attn_ref(hidden_states, w_qkv, b_qkv, w_dense, b_dense):
        import jax, jax.numpy as jnp
        import numpy as np
        HIDDEN = 512
        N_HEADS = 32
        N_KV = 8
        HEAD_DIM = HIDDEN // N_HEADS
        Q_PER_KV = N_HEADS // N_KV
        SEQ = 256
        ROPE_BASE = 1000000.0
        POS_SCALE = 1.0
        SM_SCALE = 1.0 / HEAD_DIM
        BLOCK = 64
        LOCAL_BLOCKS = 16
        VERT_STRIDE = 8

        def _blocksparse_mask(seq_len):
            nb = seq_len // BLOCK
            qb = np.arange(nb)[:, None]
            kb = np.arange(nb)[None, :]
            bmask = (kb <= qb) & ((qb - kb < LOCAL_BLOCKS) | ((kb + 1) % VERT_STRIDE == 0))
            emask = np.kron(bmask, np.ones((BLOCK, BLOCK), dtype=bool))
            i = np.arange(seq_len)
            emask &= i[:, None] >= i[None, :]
            return jnp.asarray(emask)

        def _rope(x, cos, sin):
            x1, x2 = jnp.split(x, 2, axis=-1)
            rot = jnp.concatenate([-x2, x1], axis=-1)
            return x * cos[None, :, None, :] + rot * sin[None, :, None, :]
        B, S, _ = hidden_states.shape
        qkv = jnp.einsum('bsh,oh->bso', hidden_states, w_qkv) + b_qkv
        qkv = qkv.reshape(B, S, N_KV, Q_PER_KV + 2, HEAD_DIM)
        q = qkv[:, :, :, :Q_PER_KV].reshape(B, S, N_HEADS, HEAD_DIM)
        k = qkv[:, :, :, Q_PER_KV]
        v = qkv[:, :, :, Q_PER_KV + 1]
        inv_freq = 1.0 / ROPE_BASE ** (jnp.arange(0, HEAD_DIM, 2, dtype=jnp.float32) / HEAD_DIM)
        t = jnp.arange(S, dtype=jnp.float32) * POS_SCALE
        freqs = jnp.outer(t, inv_freq)
        emb = jnp.concatenate([freqs, freqs], axis=-1)
        cos, sin = (jnp.cos(emb), jnp.sin(emb))
        q = _rope(q, cos, sin)
        k = _rope(k, cos, sin)
        k = jnp.repeat(k, Q_PER_KV, axis=2)
        v = jnp.repeat(v, Q_PER_KV, axis=2)
        mask = _blocksparse_mask(S)
        scores = jnp.einsum('bqhd,bkhd->bhqk', q, k) * SM_SCALE
        scores = jnp.where(mask[None, None], scores, jnp.finfo(scores.dtype).min)
        probs = jax.nn.softmax(scores, axis=-1)
        ctx = jnp.einsum('bhqk,bkhd->bqhd', probs, v).reshape(B, S, HIDDEN)
        out = jnp.einsum('bsh,oh->bso', ctx, w_dense) + b_dense
        return out

    def _L0_ffn_ref(hidden_states, gate_w, bias, Wg, Wu, Wd, Sg, Su, Sd):
        import jax, jax.numpy as jnp
        import numpy as np
        H = 512
        I = 256
        E = 16
        TOPK = 4
        SI = 256
        orig_shape = hidden_states.shape
        x = hidden_states.reshape(-1, orig_shape[-1])
        scores = jax.nn.sigmoid(x @ gate_w.T) + bias
        topk_w, topk_idx = jax.lax.top_k(scores, TOPK)
        topk_w = topk_w / (jnp.sum(topk_w, axis=-1, keepdims=True) + 1e-20)
        cw = jnp.sum(jax.nn.one_hot(topk_idx, E, dtype=x.dtype) * topk_w[..., None], axis=1)
        g = jnp.einsum('th,eih->eti', x, Wg)
        u = jnp.einsum('th,eih->eti', x, Wu)
        z = jax.nn.silu(g) * u
        zw = z * cw.T[:, :, None]
        out = jnp.einsum('eti,ehi->th', zw, Wd)
        out = out + jax.nn.silu(x @ Sg.T) * (x @ Su.T) @ Sd.T
        return out.reshape(orig_shape)

    def _L1_attn_ref(x, Wqkv, bqkv, Wo, bo):
        import jax, jax.numpy as jnp
        import numpy as np
        H = 512
        D = H // 4
        B, S, C = x.shape
        d = C // 4
        qkv = jnp.einsum('bsc,cf->bsf', x, Wqkv) + bqkv
        qkv = qkv.reshape(B, S, 3, d)
        q, k, v = (qkv[:, :, 0], qkv[:, :, 1], qkv[:, :, 2])
        scale = 1.0 / jnp.sqrt(jnp.float32(d)).astype(x.dtype)
        attn = jnp.einsum('bqd,bkd->bqk', q, k) * scale
        attn = jax.nn.softmax(attn, axis=-1)
        out = jnp.einsum('bqk,bkd->bqd', attn, v)
        return jnp.einsum('bqd,dc->bqc', out, Wo) + bo

    def _L1_ffn_ref(x, up, down, perm):
        import jax, jax.numpy as jnp
        import numpy as np
        B, L, H, Dh, M = (4, 256, 16, 32, 128)
        D = H * Dh
        b, l, Dm = x.shape
        h, d = (up.shape[0], up.shape[1])
        unperm = jnp.argsort(perm)
        t = x.reshape(b * l, Dm)
        t = t[:, perm]
        t = t.reshape(b * l, h, d)
        t = jnp.einsum('bhd,hdm->bhm', t, up)
        t = jax.nn.gelu(t, approximate=False)
        t = jnp.einsum('bhm,hmd->bhd', t, down)
        t = t.reshape(b * l, h * d)
        t = t[:, unperm]
        out = t.reshape(b, l, Dm)
        return out
    x = L0_attn_hidden_states
    x = x + 0.5 * _L0_ffn_ref(_layernorm(x, axis=-1), L0_ffn_gate_w, L0_ffn_bias, L0_ffn_Wg, L0_ffn_Wu, L0_ffn_Wd, L0_ffn_Sg, L0_ffn_Su, L0_ffn_Sd)
    x = x + _L0_attn_ref(_layernorm(x, axis=-1), L0_attn_w_qkv, L0_attn_b_qkv, L0_attn_w_dense, L0_attn_b_dense)
    x = x + 0.5 * _L0_ffn_ref(_layernorm(x, axis=-1), L0_ffn_gate_w, L0_ffn_bias, L0_ffn_Wg, L0_ffn_Wu, L0_ffn_Wd, L0_ffn_Sg, L0_ffn_Su, L0_ffn_Sd)
    x = x + 0.5 * _L1_ffn_ref(_layernorm(x, axis=-1), L1_ffn_up, L1_ffn_down, L1_ffn_perm)
    x = x + _L1_attn_ref(_layernorm(x, axis=-1), L1_attn_Wqkv, L1_attn_bqkv, L1_attn_Wo, L1_attn_bo)
    x = x + 0.5 * _L1_ffn_ref(_layernorm(x, axis=-1), L1_ffn_up, L1_ffn_down, L1_ffn_perm)
    return x

_drawn_inputs = setup_inputs


def setup_inputs(seed=0):
    import zlib

    import numpy as np

    out = dict(_drawn_inputs(seed))
    spreads = {'L0_attn_b_qkv': (0.0, 0.1), 'L0_attn_b_dense': (0.0, 0.1), 'L0_ffn_bias': (0.0, 0.616)}
    factors = {'L0_attn_w_qkv': 3.731,
     'L0_ffn_gate_w': 5.002,
     'L0_ffn_Wg': 3.767,
     'L0_ffn_Wu': 3.732,
     'L0_ffn_Wd': 3.71,
     'L1_attn_bqkv': 64.0,
     'L1_attn_bo': 64.0}
    for name, (base, spread) in spreads.items():
        noise = np.random.default_rng([zlib.crc32(name.encode()), seed]).standard_normal(out[name].shape)
        drawn = base * np.exp(spread * noise) if base else spread * noise
        out[name] = jnp.asarray(drawn.astype(out[name].dtype))
    for name, factor in factors.items():
        out[name] = (out[name] * factor).astype(out[name].dtype)
    return out
```

```python
from contextlib import ExitStack

import concourse.bass as bass
from concourse import mybir

ALU = mybir.AluOpType
ACT = mybir.ActivationFunctionType
AX = mybir.AxisListType
F32 = mybir.dt.float32
F32R = mybir.dt.float32r
BF16 = mybir.dt.bfloat16
I32 = mybir.dt.int32

P = 128
S = 1024
H = 512
T = S // P
KT = H // P
CH = 512
NCH = S // CH
EPS = 1e-5

E = 16
TOPK = 4
NE = E + 1
FI = 256
IT = FI // P
GU_COLS = KT * 2 * FI
W_COLS = GU_COLS + IT * H


class Shared:

    def semaphore(self, name):
        self.taken.append(self.nc.alloc_semaphore(name=name))
        return self.taken[-1]

    def release(self):
        with self.nc.Block() as block:
            @block.sync
            def _(sp):
                for s in self.taken:
                    sp.sem_clear(s)
        for s in self.taken:
            self.nc.release_semaphore(s)
        self.taken = []


def normalise_vector(m, dve, nm, lo_of):
    for t in range(T):
        nc = m.nc
        nc.vector.bn_stats(out=m.stats[:, t, :], in_=m.x[:, t, :]).then_inc(nm.stats, 1)
    for t in range(T):
        dve.wait_ge(nm.stats, t + 1)
        nc.vector.bn_aggr(out=m.mean_var[:, t, :], in_=m.stats[:, t, :]).then_inc(nm.moments, 1)
    dve.wait_ge(nm.rstd, 1)
    for t in range(T):
        nc.vector.tensor_scalar(m.xn[:, t, :], m.x[:, t, :], m.mean_var[:, t, 0:1], m.rstd[:, t:t + 1],
                                ALU.subtract, ALU.mult).then_inc(nm.xn, 1)
        if t >= 1:
            lo_of(t - 1)
    lo_of(T - 1)


def rstd_gpsimd(m, pool, nm):
    pool.wait_ge(nm.moments, T)
    m.nc.gpsimd.tensor_scalar(m.var_eps[:, :], m.mean_var[:, :, 1], EPS, None, ALU.add).then_inc(nm.var_eps, 1)
    pool.wait_ge(nm.var_eps, 1)
    m.nc.gpsimd.tensor_tensor(m.rstd[:, :], m.var_eps[:, :], m.minus_half[:, :], ALU.pow).then_inc(nm.rstd, 1)


class NormSems:
    def __init__(self, sem, name="norm"):
        self.stats = sem(f"{name}_stats")
        self.moments = sem(f"{name}_moments")
        self.var_eps = sem(f"{name}_var_eps")
        self.rstd = sem(f"{name}_rstd")
        self.xn = sem(f"{name}_xn")
        self.xt = sem(f"{name}_xt")
        self.xt_hi = sem(f"{name}_xt_hi")
        self.xt_lo = sem(f"{name}_xt_lo")


def transpose_tile(m, pe, nm, bank, t, ready=True):
    if ready:
        pe.wait_ge(nm.xn, t + 1)
    if t >= 2:
        pe.wait_ge(nm.xt_lo, t - 1)
    for k in range(KT):
        last = m.nc.tensor.transpose(bank[:, k * P:(k + 1) * P], m.xn[:, t, k * P:(k + 1) * P], m.ident[:, :])
    last.then_inc(nm.xt, 1)


def hi_tile(m, act, nm, bank, t):
    act.wait_ge(nm.xt, t + 1)
    m.nc.scalar.copy(m.xt_hi[:, :, t * P:(t + 1) * P],
                     bank[:, :].rearrange("p (k c) -> p k c", k=KT)).then_inc(nm.xt_hi, 1)


def lo_tile(m, dve, nm, bank, t):
    dve.wait_ge(nm.xt_hi, t + 1)
    m.nc.vector.tensor_tensor(m.xt_lo[:, :, t * P:(t + 1) * P], bank[:, :].rearrange("p (k c) -> p k c", k=KT),
                              m.xt_hi[:, :, t * P:(t + 1) * P].bitcast(F32), ALU.subtract).then_inc(nm.xt_lo, 1)


def product(nc, out, pairs):
    n = 0
    for a_hi, a_lo, b_hi, b_lo in pairs:
        for a, b in ((a_hi, b_hi), (a_hi, b_lo), (a_lo, b_hi)):
            last = nc.tensor.matmul(out, a, b, start=(n == 0), stop=(n == 3 * len(pairs) - 1))
            n += 1
    return last


def moe_layer(m, name):
    nc = m.nc
    with ExitStack() as ctx:
        def sb(what, shape, dt=F32):
            return ctx.enter_context(nc.sbuf_tensor(f"{name}_{what}", shape, dt))

        def pb(what, shape, dt=F32):
            return ctx.enter_context(nc.psum_tensor(f"{name}_{what}", shape, dt))

        def sem(what):
            return m.semaphore(f"{name}_{what}")

        acc = sb("acc", [P, T, H])
        raw = [sb(f"raw{s}", [P, W_COLS]) for s in range(2)]
        w_hi = [sb(f"w_hi{s}", [P, W_COLS], F32R) for s in range(2)]
        w_lo = [sb(f"w_lo{s}", [P, W_COLS], F32R) for s in range(2)]
        gate_raw = sb("gate_raw", [P, KT, P])
        gate_hi = sb("gate_hi", [P, KT, P], F32R)
        gate_lo = sb("gate_lo", [P, KT, P], F32R)
        gate_bias = sb("gate_bias", [E, 1])
        tie = sb("tie", [P, E * E])
        score_t = sb("score_t", [E, S])
        score_tb = sb("score_tb", [E, S])
        score = sb("score", [P, T, E])
        beats = sb("beats", [P, T, E, E])
        equal = sb("equal", [P, T, E, E])
        rank = sb("rank", [P, T, E])
        chosen = sb("chosen", [P, T, E])
        total = sb("total", [P, T])
        inv_total = sb("inv_total", [P, T])
        cw = sb("cw", [P, T, NE])
        silu = [sb(f"silu{s}", [P, FI]) for s in range(2)]
        z = [sb(f"z{s}", [P, FI]) for s in range(2)]
        zt_hi = [sb(f"zt_hi{s}", [P, FI], F32R) for s in range(2)]
        zt_lo = [sb(f"zt_lo{s}", [P, FI], F32R) for s in range(2)]

        turn = [pb(f"turn{s}", [P, CH]) for s in range(2)]
        gu = [pb(f"gu{s}", [P, CH]) for s in range(2)]
        y = [pb(f"y{s}", [P, CH]) for s in range(2)]
        logits = [pb(f"logits{c}", [P, CH]) for c in range(NCH)]

        nm = NormSems(sem)
        gate_in, gate_w = sem("gate_in"), sem("gate_w")
        raw_in = [sem(f"raw_in{s}") for s in range(2)]
        w_hi_done, w_ready = sem("w_hi_done"), sem("w_ready")
        logits_done, sig_done, score_b, score_turned, score_done = (
            sem("logits_done"), sem("sig_done"), sem("score_b"), sem("score_turned"), sem("score_done"))
        compared, tied, route, init_done = sem("compared"), sem("tied"), sem("route"), sem("init_done")
        gu_done, silu_done, z_done = sem("gu_done"), sem("silu_done"), sem("z_done")
        zt_done, zt_hi_done, zt_lo_done = sem("zt_done"), sem("zt_hi_done"), sem("zt_lo_done")
        y_done, acc_done, x_done = sem("y_done"), sem("acc_done"), sem("x_done")

        def gu_w(w, k):
            return w[:, k * 2 * FI:(k + 1) * 2 * FI]

        def down_w(w, i):
            return w[:, GU_COLS + i * H:GU_COLS + (i + 1) * H]

        block = ctx.enter_context(nc.Block())


        @block.sync
        def _(sp):
            sp.dma_start(gate_raw[:, :, :], m.dram["gate_w"]).then_inc(gate_in, 16)
            sp.dma_start(gate_bias[:, :], m.dram["gate_bias"]).then_inc(gate_in, 16)
            sp.dma_start(tie[:, :], m.dram["tie"]).then_inc(gate_in, 16)

            def load(slot, e):
                sp.dma_start(raw[slot][:, 0:GU_COLS], m.dram["w_gu"][e]).then_inc(raw_in[slot], 16)
                sp.dma_start(raw[slot][:, GU_COLS:W_COLS], m.dram["w_down"][e]).then_inc(raw_in[slot], 16)

            load(0, 0)
            with sp.Fori(0, E // 2) as i:
                sp.wait_ge(w_ready, i * 2 + 1)
                load(1, i * 2 + 1)
                load(0, i * 2 + 2)

        @block.gpsimd
        def _(pool):
            def split(slot, uses, e):
                pool.wait_ge(raw_in[slot], uses * 32 + 32)
                nc.gpsimd.tensor_tensor(w_hi[slot][:, :], raw[slot][:, :], m.zero[:, 0:1].broadcast_to([P, W_COLS]),
                                        ALU.add).then_inc(w_hi_done, 1)
                pool.wait_ge(w_hi_done, e + 1)
                nc.gpsimd.tensor_tensor(w_lo[slot][:, :], raw[slot][:, :], w_hi[slot][:, :].bitcast(F32),
                                        ALU.subtract).then_inc(w_ready, 1)

            rstd_gpsimd(m, pool, nm)
            split(0, 0, 0)
            pool.wait_ge(gate_in, 48)
            nc.gpsimd.tensor_copy(gate_hi[:, :, :], gate_raw[:, :, :]).then_inc(gate_w, 1)
            pool.wait_ge(gate_w, 1)
            nc.gpsimd.tensor_tensor(gate_lo[:, :, :], gate_raw[:, :, :], gate_hi[:, :, :].bitcast(F32),
                                    ALU.subtract).then_inc(gate_w, 1)
            pool.wait_ge(sig_done, NCH)
            nc.gpsimd.tensor_scalar(score_tb[:, :], score_t[:, :], gate_bias[:, 0:1], None, ALU.add).then_inc(score_b, 1)
            first = tie[:, :].rearrange("p (a b) -> p a b", a=E).unsqueeze(1).broadcast_to([P, T, E, E])
            pool.wait_ge(compared, 2)
            nc.gpsimd.tensor_tensor(equal[:, :, :, :], equal[:, :, :, :], first, ALU.mult).then_inc(tied, 1)
            pool.wait_ge(tied, 1)
            nc.gpsimd.tensor_tensor(beats[:, :, :, :], beats[:, :, :, :], equal[:, :, :, :], ALU.add).then_inc(tied, 1)
            with pool.Fori(0, E // 2) as i:
                pool.wait_ge(y_done, i * (2 * T) + 1)
                split(1, i, i * 2 + 1)
                pool.wait_ge(y_done, i * (2 * T) + T)
                split(0, i + 1, i * 2 + 2)

        @block.tensor
        def _(pe):
            def turn_z(b, s):
                pe.wait_ge(z_done, b + 1)
                for j in range(IT):
                    last = nc.tensor.transpose(turn[s][:, j * P:(j + 1) * P], z[s][:, j * P:(j + 1) * P], m.ident[:, :])
                last.then_inc(zt_done, 1)

            def gate_up(s, slot, t):
                product(nc, gu[s][:, :], [(m.xt_hi[:, k, t * P:(t + 1) * P], m.xt_lo[:, k, t * P:(t + 1) * P],
                                           gu_w(w_hi[slot], k), gu_w(w_lo[slot], k)) for k in range(KT)]).then_inc(gu_done, 1)

            def down(b, s, slot):
                pe.wait_ge(zt_lo_done, b + 1)
                last = product(nc, y[s][:, :], [(zt_hi[s][:, j * P:(j + 1) * P], zt_lo[s][:, j * P:(j + 1) * P],
                                                 down_w(w_hi[slot], j), down_w(w_lo[slot], j)) for j in range(IT)])
                last.then_inc(y_done, 1)

            for t in range(T):
                transpose_tile(m, pe, nm, turn[t % 2], t)
            pe.wait_ge(nm.xt_lo, T)
            pe.wait_ge(gate_w, 2)
            for c in range(NCH):
                cols = slice(c * CH, (c + 1) * CH)
                product(nc, logits[c][:, :], [(gate_hi[:, k, :], gate_lo[:, k, :], m.xt_hi[:, k, cols], m.xt_lo[:, k, cols])
                                              for k in range(KT)]).then_inc(logits_done, 1)

            pe.wait_ge(w_ready, 1)
            for t in range(T):
                if t >= 1:
                    turn_z(t - 1, (t - 1) % 2)
                if t == 2:
                    pe.wait_ge(score_b, 1)
                    for u in range(T):
                        last = nc.tensor.transpose(logits[0][:, u * E:(u + 1) * E], score_tb[:, u * P:(u + 1) * P],
                                                   m.ident[0:E, 0:E])
                    last.then_inc(score_turned, 1)
                gate_up(t % 2, 0, t)
                if t >= 1:
                    if t >= 3:
                        pe.wait_ge(acc_done, t - 2)
                    down(t - 1, (t - 1) % 2, 0)
            with pe.Fori(0, E // 2) as i:
                for half in range(2):
                    slot = 1 - half
                    pe.wait_ge(w_ready, i * 2 + half + 2)
                    for t in range(T):
                        b = i * (2 * T) + ((1 + half) * T + t)
                        turn_z(b - 1, (t - 1) % 2)
                        gate_up(t % 2, slot, t)
                        pe.wait_ge(acc_done, b - 2)
                        down(b - 1, (t - 1) % 2, slot if t else 1 - slot)
            b = NE * T
            turn_z(b - 1, (b - 1) % 2)
            pe.wait_ge(acc_done, b - 2)
            down(b - 1, (b - 1) % 2, 0)

        @block.scalar
        def _(act):
            def silu_of(b, s):
                act.wait_ge(gu_done, b + 1)
                nc.scalar.activation(silu[s][:, :], gu[s][:, 0:FI], ACT.Silu).then_inc(silu_done, 1)

            def zt_hi_of(b, s):
                act.wait_ge(zt_done, b + 1)
                nc.scalar.copy(zt_hi[s][:, :], turn[s][:, 0:FI]).then_inc(zt_hi_done, 1)

            for t in range(T):
                hi_tile(m, act, nm, turn[t % 2], t)
            for c in range(NCH):
                act.wait_ge(logits_done, c + 1)
                nc.scalar.activation(score_t[:, c * CH:(c + 1) * CH], logits[c][0:E, :], ACT.Sigmoid).then_inc(sig_done, 1)
            for t in range(T):
                if t >= 1:
                    if t >= 3:
                        act.wait_ge(y_done, t - 2)
                    zt_hi_of(t - 1, (t - 1) % 2)
                if t >= 2:
                    act.wait_ge(z_done, t - 1)
                silu_of(t, t % 2)
                if t == 3:
                    act.wait_ge(score_turned, 1)
                    nc.scalar.copy(score[:, :, :], logits[0][:, 0:T * E].rearrange("p (t e) -> p t e", t=T)).then_inc(score_done, 1)
            with act.Fori(0, E // 2) as i:
                for half in range(2):
                    for t in range(T):
                        b = i * (2 * T) + ((1 + half) * T + t)
                        act.wait_ge(y_done, b - 2)
                        zt_hi_of(b - 1, (t - 1) % 2)
                        act.wait_ge(z_done, b - 1)
                        silu_of(b, t % 2)
            b = NE * T
            act.wait_ge(y_done, b - 2)
            zt_hi_of(b - 1, (b - 1) % 2)

        @block.vector
        def _(dve):
            def z_of(b, s):
                dve.wait_ge(silu_done, b + 1)
                nc.vector.tensor_tensor(z[s][:, :], silu[s][:, :], gu[s][:, FI:2 * FI], ALU.mult).then_inc(z_done, 1)

            def zt_lo_of(b, s):
                dve.wait_ge(zt_hi_done, b + 1)
                nc.vector.tensor_tensor(zt_lo[s][:, :], turn[s][:, 0:FI], zt_hi[s][:, :].bitcast(F32),
                                        ALU.subtract).then_inc(zt_lo_done, 1)

            def add(b, s, t, weight):
                dve.wait_ge(y_done, b + 1)
                nc.vector.scalar_tensor_tensor(out=acc[:, t, :], in0=y[s][:, :], scalar=weight, in1=acc[:, t, :],
                                               op0=ALU.mult, op1=ALU.add).then_inc(acc_done, 1)

            nc.vector.memset(acc[:, :, :], 0.0).then_inc(init_done, 1)
            nc.vector.memset(cw[:, :, 0:1], 1.0).then_inc(init_done, 1)
            normalise_vector(m, dve, nm, lambda t: lo_tile(m, dve, nm, turn[t % 2], t))
            dve.wait_ge(init_done, 2)
            for t in range(T):
                if t >= 1:
                    zt_lo_of(t - 1, (t - 1) % 2)
                z_of(t, t % 2)
                if t >= 1:
                    add(t - 1, (t - 1) % 2, t - 1, cw[:, t - 1, 0:1])
                if t == 4:
                    dve.wait_ge(score_done, 1)
                    mine = score[:, :, :].unsqueeze(3).broadcast_to([P, T, E, E])
                    other = score[:, :, :].unsqueeze(2).broadcast_to([P, T, E, E])
                    nc.vector.tensor_tensor(beats[:, :, :, :], other, mine, ALU.is_gt).then_inc(compared, 1)
                    nc.vector.tensor_tensor(equal[:, :, :, :], other, mine, ALU.is_equal).then_inc(compared, 1)
                if t == 7:
                    dve.wait_ge(tied, 2)
                    nc.vector.tensor_reduce(rank[:, :, :], beats[:, :, :, :], AX.X, ALU.add).then_inc(route, 1)
                    dve.wait_ge(route, 1)
                    nc.vector.scalar_tensor_tensor(out=chosen[:, :, :], in0=rank[:, :, :], scalar=float(TOPK) - 0.5,
                                                   in1=score[:, :, :], op0=ALU.is_lt, op1=ALU.mult).then_inc(route, 1)
                    dve.wait_ge(route, 2)
                    nc.vector.tensor_reduce(total[:, :], chosen[:, :, :], AX.X, ALU.add).then_inc(route, 1)
                    dve.wait_ge(route, 3)
                    nc.vector.tensor_scalar(total[:, :], total[:, :], 1e-20, None, ALU.add).then_inc(route, 1)
                    dve.wait_ge(route, 4)
                    nc.vector.reciprocal(inv_total[:, :], total[:, :]).then_inc(route, 1)
                    dve.wait_ge(route, 5)
                    nc.vector.tensor_tensor(cw[:, :, 1:NE], chosen[:, :, :],
                                            inv_total[:, :].unsqueeze(2).broadcast_to([P, T, E]), ALU.mult).then_inc(route, 1)
            dve.wait_ge(route, 6)
            with dve.Fori(0, E // 2) as i:
                for half in range(2):
                    for t in range(T):
                        b = i * (2 * T) + ((1 + half) * T + t)
                        zt_lo_of(b - 1, (t - 1) % 2)
                        z_of(b, t % 2)
                        before = (t - 1) % T
                        e = i * 2 + (half if t == 0 else half + 1)
                        dve.wait_ge(acc_done, b - T + 1)
                        add(b - 1, (t - 1) % 2, before, cw[:, before, bass.ds(e, 1)])
            b = NE * T
            zt_lo_of(b - 1, (b - 1) % 2)
            dve.wait_ge(acc_done, b - T + 1)
            add(b - 1, (b - 1) % 2, T - 1, cw[:, T - 1, E:NE])
            for t in range(T):
                dve.wait_ge(acc_done, b - T + t + 1)
                nc.vector.scalar_tensor_tensor(out=m.x[:, t, :], in0=acc[:, t, :], scalar=0.5, in1=m.x[:, t, :],
                                               op0=ALU.mult, op1=ALU.add).then_inc(x_done, 1)



def butterfly_layer(m, name):
    nc = m.nc
    HEADS, DH, M = 16, 32, 128
    QH = P // DH
    TC = CH // P
    with ExitStack() as ctx:
        def sb(what, shape, dt=F32):
            return ctx.enter_context(nc.sbuf_tensor(f"{name}_{what}", shape, dt))

        def pb(what, shape, dt=F32):
            return ctx.enter_context(nc.psum_tensor(f"{name}_{what}", shape, dt))

        def sem(what):
            return m.semaphore(f"{name}_{what}")

        perm_row_i = sb("perm_row_i", [P, H], I32)
        perm_row = sb("perm_row", [P, H])
        perm_col_i = sb("perm_col_i", [P, KT], I32)
        perm_col = sb("perm_col", [P, KT])
        index_row = sb("index_row", [P, H])
        index_col = sb("index_col", [P, KT])
        gather = sb("gather", [P, KT, H], F32R)
        spread = sb("spread", [P, KT, H], F32R)
        up = sb("up", [P, KT, M])
        down = sb("down", [P, HEADS, DH])
        t_in = sb("t_in", [P, KT, S])
        hid = [sb(f"hid{s}", [P, QH, CH]) for s in range(2)]
        d_hi = sb("d_hi", [P, KT, S], F32R)
        d_lo = sb("d_lo", [P, KT, S], F32R)
        ups = [pb(f"ups{s}", [P, 2, CH]) for s in range(2)]
        io = [pb(f"io{s}", [P, CH]) for s in range(2)]
        dn = [pb(f"dn{s}", [P, CH]) for s in range(2)]

        nm = NormSems(sem)
        perm_in, w_in, perm_f, maps = sem("perm_in"), sem("w_in"), sem("perm_f"), sem("maps")
        io_done, io_read = sem("io_done"), sem("io_read")
        up_done, gelu_done, dn_done, d_hi_done, d_lo_done = (
            sem("up_done"), sem("gelu_done"), sem("dn_done"), sem("d_hi_done"), sem("d_lo_done"))

        UNITS = NCH * KT

        def around(u):
            return KT + u - 1 if 1 <= u <= 2 * KT else None

        block = ctx.enter_context(nc.Block())

        @block.sync
        def _(sp):
            sp.dma_start(perm_row_i[:, :], m.dram["perm"].rearrange("(a h) -> a h", a=1).broadcast_to([P, H])).then_inc(perm_in, 16)
            sp.dma_start(perm_col_i[:, :], m.dram["perm_col"]).then_inc(perm_in, 16)
            sp.dma_start(index_row[:, :], m.dram["index_row"].rearrange("(a h) -> a h", a=1).broadcast_to([P, H])).then_inc(perm_in, 16)
            sp.dma_start(index_col[:, :], m.dram["index_col"]).then_inc(perm_in, 16)
            sp.dma_start(up[:, :, :], m.dram["up"]).then_inc(w_in, 16)
            sp.dma_start(down[:, :, :], m.dram["down"]).then_inc(w_in, 16)

        @block.gpsimd
        def _(pool):
            rstd_gpsimd(m, pool, nm)

        @block.tensor
        def _(pe):
            def columns(n):
                c, j = divmod(n, KT)
                if n >= 2:
                    pe.wait_ge(io_read, n - 1)
                for k in range(KT):
                    for half in (m.xt_hi, m.xt_lo):
                        last = nc.tensor.matmul(io[n % 2][:, :], gather[:, k, j * P:(j + 1) * P],
                                                half[:, k, c * CH:(c + 1) * CH],
                                                start=(k == 0 and half is m.xt_hi), stop=(k == KT - 1 and half is m.xt_lo))
                last.then_inc(io_done, 1)

            def outputs(n):
                t = n - UNITS
                pe.wait_ge(io_read, n - 1)
                pe.wait_ge(d_lo_done, (t // TC + 1) * KT)
                for k in range(KT):
                    for half in (d_hi, d_lo):
                        last = nc.tensor.matmul(io[n % 2][:, :], half[:, k, t * P:(t + 1) * P], spread[:, k, :],
                                                start=(k == 0 and half is d_hi), stop=(k == KT - 1 and half is d_lo))
                last.then_inc(io_done, 1)

            for t in range(T):
                transpose_tile(m, pe, nm, dn[t % 2], t)
            pe.wait_ge(nm.xt_lo, T)
            pe.wait_ge(maps, 2)
            pe.wait_ge(w_in, 32)
            for n in range(KT):
                columns(n)
            for u in range(UNITS + 1):
                n = around(u)
                if n is not None:
                    columns(n) if n < UNITS else outputs(n)
                if u < UNITS:
                    c, j = divmod(u, KT)
                    pe.wait_ge(io_read, u + 1)
                    for r in range(QH):
                        if u >= 1 and r % 2 == 0:
                            pe.wait_ge(gelu_done, 2 * u - 1 + r // 2)
                        rows = slice(DH * r, DH * (r + 1))
                        last = nc.tensor.matmul(ups[r // 2][:, r % 2, :], up[rows, j, :], t_in[rows, j, c * CH:(c + 1) * CH],
                                                start=True, stop=True)
                        if r % 2:
                            last.then_inc(up_done, 1)
                if u >= 1:
                    v = u - 1
                    pe.wait_ge(gelu_done, 2 * v + 2)
                    if v >= 2:
                        pe.wait_ge(d_lo_done, v - 1)
                    for r in range(QH):
                        last = nc.tensor.matmul(dn[v % 2][DH * r:DH * (r + 1), :], down[:, QH * (v % KT) + r, :],
                                                hid[v % 2][:, r, :], start=True, stop=True)
                    last.then_inc(dn_done, 1)
            for n in range(UNITS + TC, UNITS + T):
                outputs(n)

        @block.scalar
        def _(act):
            for t in range(T):
                hi_tile(m, act, nm, dn[t % 2], t)
            for u in range(UNITS + 1):
                if u < UNITS:
                    for a in range(2):
                        act.wait_ge(up_done, 2 * u + a + 1)
                        if u >= 2:
                            act.wait_ge(dn_done, u - 1)
                        nc.scalar.activation(hid[u % 2][:, 2 * a:2 * a + 2, :], ups[a][:, :, :], ACT.Gelu).then_inc(gelu_done, 1)
                if u >= 1:
                    c, j = divmod(u - 1, KT)
                    act.wait_ge(dn_done, u)
                    nc.scalar.copy(d_hi[:, j, c * CH:(c + 1) * CH], dn[(u - 1) % 2][:, :]).then_inc(d_hi_done, 1)

        @block.vector
        def _(dve):
            def read(n):
                dve.wait_ge(io_done, n + 1)
                if n < UNITS:
                    c, j = divmod(n, KT)
                    nc.vector.tensor_copy(t_in[:, j, c * CH:(c + 1) * CH], io[n % 2][:, :]).then_inc(io_read, 1)
                else:
                    t = n - UNITS
                    nc.vector.scalar_tensor_tensor(out=m.x[:, t, :], in0=io[n % 2][:, :], scalar=0.5, in1=m.x[:, t, :],
                                                   op0=ALU.mult, op1=ALU.add).then_inc(io_read, 1)

            dve.wait_ge(perm_in, 64)
            nc.vector.tensor_copy(perm_row[:, :], perm_row_i[:, :]).then_inc(perm_f, 1)
            nc.vector.tensor_copy(perm_col[:, :], perm_col_i[:, :]).then_inc(perm_f, 1)
            dve.wait_ge(perm_f, 2)
            for k in range(KT):
                g = nc.vector.tensor_scalar(gather[:, k, :], perm_row[:, :], index_col[:, k:k + 1], None, ALU.is_equal)
                s = nc.vector.tensor_scalar(spread[:, k, :], index_row[:, :], perm_col[:, k:k + 1], None, ALU.is_equal)
            g.then_inc(maps, 1)
            s.then_inc(maps, 1)
            normalise_vector(m, dve, nm, lambda t: lo_tile(m, dve, nm, dn[t % 2], t))
            for n in range(KT):
                read(n)
            for u in range(UNITS + 1):
                n = around(u)
                if n is not None:
                    read(n)
                if u >= 1:
                    c, j = divmod(u - 1, KT)
                    dve.wait_ge(d_hi_done, u)
                    nc.vector.tensor_tensor(d_lo[:, j, c * CH:(c + 1) * CH], dn[(u - 1) % 2][:, :],
                                            d_hi[:, j, c * CH:(c + 1) * CH].bitcast(F32), ALU.subtract).then_inc(d_lo_done, 1)
            for n in range(UNITS + TC, UNITS + T):
                read(n)


def full_attention_layer(m, name):
    nc = m.nc
    D = H // 4
    SCALE = float(D) ** -0.5
    with ExitStack() as ctx:
        def sb(what, shape, dt=F32):
            return ctx.enter_context(nc.sbuf_tensor(f"{name}_{what}", shape, dt))

        def pb(what, shape, dt=F32):
            return ctx.enter_context(nc.psum_tensor(f"{name}_{what}", shape, dt))

        def sem(what):
            return m.semaphore(f"{name}_{what}")

        w_raw = sb("w_raw", [P, KT, 3 * D])
        w_hi = sb("w_hi", [P, KT, 3 * D], F32R)
        w_lo = sb("w_lo", [P, KT, 3 * D], F32R)
        wo_raw = sb("wo_raw", [P, H])
        wo_hi = sb("wo_hi", [P, H], F32R)
        wo_lo = sb("wo_lo", [P, H], F32R)
        b_qkv = sb("b_qkv", [P, 3])
        b_out = sb("b_out", [P, H])
        qk_hi = [sb(f"{a}_hi", [P, S], F32R) for a in "qk"]
        qk_lo = [sb(f"{a}_lo", [P, S], F32R) for a in "qk"]
        vt = sb("vt", [P, S])
        v_hi = sb("v_hi", [P, S], F32R)
        v_lo = sb("v_lo", [P, S], F32R)
        top = sb("top", [P, T])
        bias = sb("bias", [P, T])
        total = sb("total", [P, T])
        inv_total = sb("inv_total", [P, T])
        prob = [sb(f"prob{s}", [P, S]) for s in range(2)]
        pt_hi = sb("pt_hi", [P, T, S], F32R)
        pt_lo = sb("pt_lo", [P, T, S], F32R)
        o_hi = sb("o_hi", [P, S], F32R)
        o_lo = sb("o_lo", [P, S], F32R)

        sc = [pb(f"sc{s}", [P, S]) for s in range(2)]
        pt = pb("pt", [P, S])
        pj = [pb(f"pj{s}", [P, CH]) for s in range(2)]

        nm = NormSems(sem)
        w_in, b_in, w_half, w_ready, x_biased = sem("w_in"), sem("b_in"), sem("w_half"), sem("w_ready"), sem("x_biased")
        pj_done, qk_hi_done, qk_read, vt_read = sem("pj_done"), sem("qk_hi_done"), sem("qk_read"), sem("vt_read")
        o_hi_done, o_read, x_done = sem("o_hi_done"), sem("o_read"), sem("x_done")
        vt_done, v_hi_done, v_lo_done = sem("vt_done"), sem("v_hi_done"), sem("v_lo_done")
        sc_done, top_done, bias_done, prob_done = sem("sc_done"), sem("top_done"), sem("bias_done"), sem("prob_done")
        pt_done, pt_hi_done, pt_lo_done = sem("pt_done"), sem("pt_hi_done"), sem("pt_lo_done")
        inv_done = sem("inv_done")
        PROJ = 3 * NCH

        block = ctx.enter_context(nc.Block())

        @block.sync
        def _(sp):
            sp.dma_start(w_raw[:, :, :], m.dram["w1_qkv"]).then_inc(w_in, 16)
            sp.dma_start(wo_raw[:, :], m.dram["w1_out"]).then_inc(w_in, 16)
            sp.dma_start(b_qkv[:, :], m.dram["b1_qkv"]).then_inc(b_in, 16)
            sp.dma_start(b_out[:, :], m.dram["b1_out"].rearrange("(a h) -> a h", a=1).broadcast_to([P, H])).then_inc(b_in, 16)

        @block.gpsimd
        def _(pool):
            pool.wait_ge(w_in, 32)
            nc.gpsimd.tensor_copy(w_hi[:, :, :], w_raw[:, :, :]).then_inc(w_half, 1)
            nc.gpsimd.tensor_copy(wo_hi[:, :], wo_raw[:, :]).then_inc(w_half, 1)
            rstd_gpsimd(m, pool, nm)
            pool.wait_ge(w_half, 2)
            nc.gpsimd.tensor_tensor(w_lo[:, :, :], w_raw[:, :, :], w_hi[:, :, :].bitcast(F32), ALU.subtract).then_inc(w_ready, 1)
            nc.gpsimd.tensor_tensor(wo_lo[:, :], wo_raw[:, :], wo_hi[:, :].bitcast(F32), ALU.subtract).then_inc(w_ready, 1)
            pool.wait_ge(b_in, 32)
            pool.wait_ge(nm.xn, T)
            nc.gpsimd.tensor_tensor(m.x[:, :, :], m.x[:, :, :], b_out[:, :].unsqueeze(1).broadcast_to([P, T, H]),
                                    ALU.add).then_inc(x_biased, 1)

        @block.tensor
        def _(pe):
            for t in range(T):
                transpose_tile(m, pe, nm, sc[t % 2][:, 0:CH], t)
            pe.wait_ge(nm.xt_lo, T)
            pe.wait_ge(w_ready, 2)
            for u in range(PROJ):
                a, c = divmod(u, NCH)
                if u >= 2:
                    pe.wait_ge(qk_read, u - 1)
                cols = slice(c * CH, (c + 1) * CH)
                product(nc, pj[u % 2][:, :], [(w_hi[:, k, a * D:(a + 1) * D], w_lo[:, k, a * D:(a + 1) * D],
                                               m.xt_hi[:, k, cols], m.xt_lo[:, k, cols]) for k in range(KT)]).then_inc(pj_done, 1)

            def scores(t):
                if t >= 2:
                    pe.wait_ge(prob_done, t - 1)
                rows = slice(t * P, (t + 1) * P)
                for c in range(NCH):
                    cols = slice(c * CH, (c + 1) * CH)
                    last = product(nc, sc[t % 2][:, cols], [(qk_hi[0][:, rows], qk_lo[0][:, rows],
                                                             qk_hi[1][:, cols], qk_lo[1][:, cols])])
                last.then_inc(sc_done, 1)

            def turn_prob(t):
                pe.wait_ge(prob_done, t + 1)
                if t >= 1:
                    pe.wait_ge(pt_lo_done, t)
                for k in range(T):
                    last = nc.tensor.transpose(pt[:, k * P:(k + 1) * P], prob[t % 2][:, k * P:(k + 1) * P], m.ident[:, :])
                last.then_inc(pt_done, 1)

            pe.wait_ge(qk_read, 2 * NCH)
            scores(0)
            pe.wait_ge(vt_read, NCH)
            for t in range(T):
                last = nc.tensor.transpose(pt[:, t * P:(t + 1) * P], vt[:, t * P:(t + 1) * P], m.ident[:, :])
            last.then_inc(vt_done, 1)
            for t in range(1, T):
                scores(t)
                if t == 1:
                    pe.wait_ge(v_lo_done, 1)
                turn_prob(t - 1)
            turn_prob(T - 1)
            for c in range(NCH):
                pe.wait_ge(pt_lo_done, (c + 1) * (CH // P))
                cols = slice(c * CH, (c + 1) * CH)
                product(nc, pj[c][:, :], [(v_hi[:, k * D:(k + 1) * D], v_lo[:, k * D:(k + 1) * D],
                                           pt_hi[:, k, cols], pt_lo[:, k, cols]) for k in range(T)]).then_inc(pj_done, 1)
            for t in range(T):
                if t == 0:
                    pe.wait_ge(o_read, NCH)
                if t >= 2:
                    pe.wait_ge(x_done, t - 1)
                rows = slice(t * P, (t + 1) * P)
                product(nc, pj[t % 2][:, :], [(o_hi[:, rows], o_lo[:, rows], wo_hi[:, :], wo_lo[:, :])]).then_inc(pj_done, 1)

        @block.scalar
        def _(act):
            for t in range(T):
                hi_tile(m, act, nm, sc[t % 2][:, 0:CH], t)
            act.wait_ge(b_in, 32)
            for u in range(PROJ):
                a, c = divmod(u, NCH)
                act.wait_ge(pj_done, u + 1)
                cols = slice(c * CH, (c + 1) * CH)
                if a < 2:
                    nc.scalar.activation(qk_hi[a][:, cols], pj[u % 2][:, :], ACT.Identity, bias=b_qkv[:, a:a + 1]).then_inc(qk_hi_done, 1)
                else:
                    nc.scalar.activation(vt[:, cols], pj[u % 2][:, :], ACT.Identity, bias=b_qkv[:, a:a + 1]).then_inc(vt_read, 1)

            def probabilities(t):
                act.wait_ge(bias_done, t + 1)
                if t >= 2:
                    act.wait_ge(pt_done, t - 1)
                nc.scalar.activation(prob[t % 2][:, :], sc[t % 2][:, :], ACT.Exp, bias=bias[:, t:t + 1], scale=SCALE,
                                     accum_out=total[:, t:t + 1]).then_inc(prob_done, 1)

            def upper(t):
                act.wait_ge(pt_done, t + 1)
                nc.scalar.copy(pt_hi[:, :, t * P:(t + 1) * P], pt[:, :].rearrange("p (k c) -> p k c", k=T)).then_inc(pt_hi_done, 1)

            act.wait_ge(vt_done, 1)
            nc.scalar.copy(v_hi[:, :], pt[:, :]).then_inc(v_hi_done, 1)
            probabilities(0)
            for t in range(1, T):
                probabilities(t)
                upper(t - 1)
            upper(T - 1)
            for c in range(NCH):
                act.wait_ge(pj_done, PROJ + c + 1)
                nc.scalar.copy(o_hi[:, c * CH:(c + 1) * CH], pj[c][:, :]).then_inc(o_hi_done, 1)

        @block.vector
        def _(dve):
            normalise_vector(m, dve, nm, lambda t: lo_tile(m, dve, nm, sc[t % 2][:, 0:CH], t))
            for u in range(2 * NCH):
                a, c = divmod(u, NCH)
                dve.wait_ge(qk_hi_done, u + 1)
                cols = slice(c * CH, (c + 1) * CH)
                nc.vector.scalar_tensor_tensor(out=qk_lo[a][:, cols], in0=pj[u % 2][:, :], scalar=b_qkv[:, a:a + 1],
                                               in1=qk_hi[a][:, cols].bitcast(F32), op0=ALU.add, op1=ALU.subtract).then_inc(qk_read, 1)

            def maximum(t):
                dve.wait_ge(sc_done, t + 1)
                nc.vector.tensor_reduce(top[:, t:t + 1], sc[t % 2][:, :], AX.X, ALU.max).then_inc(top_done, 1)
                dve.wait_ge(top_done, t + 1)
                nc.vector.tensor_scalar(bias[:, t:t + 1], top[:, t:t + 1], -SCALE, None, ALU.mult).then_inc(bias_done, 1)

            def lower(t):
                dve.wait_ge(pt_hi_done, t + 1)
                cols = slice(t * P, (t + 1) * P)
                nc.vector.tensor_tensor(pt_lo[:, :, cols], pt[:, :].rearrange("p (k c) -> p k c", k=T),
                                        pt_hi[:, :, cols].bitcast(F32), ALU.subtract).then_inc(pt_lo_done, 1)

            maximum(0)
            dve.wait_ge(v_hi_done, 1)
            nc.vector.tensor_tensor(v_lo[:, :], pt[:, :], v_hi[:, :].bitcast(F32), ALU.subtract).then_inc(v_lo_done, 1)
            for t in range(1, T):
                maximum(t)
                lower(t - 1)
            lower(T - 1)
            dve.wait_ge(prob_done, T)
            nc.vector.reciprocal(inv_total[:, :], total[:, :]).then_inc(inv_done, 1)
            for c in range(NCH):
                dve.wait_ge(o_hi_done, c + 1)
                cols = slice(c * CH, (c + 1) * CH)
                nc.vector.tensor_tensor(o_lo[:, cols], pj[c][:, :], o_hi[:, cols].bitcast(F32), ALU.subtract).then_inc(o_read, 1)
            dve.wait_ge(inv_done, 1)
            dve.wait_ge(x_biased, 1)
            for t in range(T):
                dve.wait_ge(pj_done, PROJ + NCH + t + 1)
                nc.vector.scalar_tensor_tensor(out=m.x[:, t, :], in0=pj[t % 2][:, :], scalar=inv_total[:, t:t + 1],
                                               in1=m.x[:, t, :], op0=ALU.mult, op1=ALU.add).then_inc(x_done, 1)


def causal_attention_layer(m, name):
    nc = m.nc
    HD, KV, QPK = 16, 8, 4
    HEADS = KV * QPK
    SCALE = 1.0 / HD
    QK_ROWS = (KV + HEADS) * HD
    Q_PART = (0, 0, 1, 0, 1, 2)
    K_PART = (0, 1, 0, 2, 1, 0)
    STACK = len(Q_PART) * HD
    MROWS = 3
    with ExitStack() as outer:
        def sem(what):
            return m.semaphore(f"{name}_{what}")

        parts_dram = nc.dram_tensor(f"{name}_parts", [3, QK_ROWS, S], BF16, kind="Internal").ap()
        v_all = outer.enter_context(nc.sbuf_tensor(f"{name}_v_all", [P, T, KV, 2 * HD], F32))
        ks = outer.enter_context(nc.sbuf_tensor(f"{name}_ks", [P, KV * S], BF16))

        with ExitStack() as ctx:
            def sb(what, shape, dt=F32):
                return ctx.enter_context(nc.sbuf_tensor(f"{name}_{what}", shape, dt))

            def pb(what, shape, dt=F32):
                return ctx.enter_context(nc.psum_tensor(f"{name}_{what}", shape, dt))

            WQ = (HEADS + 2 * KV) * HD
            w_raw = sb("w_raw", [P, KT, WQ])
            w_hi = sb("w_hi", [P, KT, WQ], F32R)
            w_lo = sb("w_lo", [P, KT, WQ], F32R)
            b_qkv = sb("b_qkv", [P, WQ // P])
            cos = sb("cos", [P, S])
            sin = sb("sin", [P, S])
            swap_raw = sb("swap_raw", [P, P])
            swap = sb("swap", [P, P], F32R)
            q_hi = [sb(f"q_hi{s}", [P, CH], F32R) for s in range(2)]
            q_lo = [sb(f"q_lo{s}", [P, CH], F32R) for s in range(2)]
            with_cos = [sb(f"with_cos{s}", [P, CH]) for s in range(2)]
            with_sin = [sb(f"with_sin{s}", [P, CH]) for s in range(2)]
            turned = [sb(f"turned{s}", [P, CH]) for s in range(2)]
            rest = [sb(f"rest{s}", [P, CH]) for s in range(2)]
            NPB = 4
            part = [sb(f"part{s}", [P, 3, CH], BF16) for s in range(NPB)]
            vt = sb("vt", [P, S])
            xp = [pb(f"xp{s}", [P, CH]) for s in range(2)]
            pj = [pb(f"pj{s}", [P, CH]) for s in range(2)]
            rot = [pb(f"rot{s}", [P, CH]) for s in range(2)]

            nm = NormSems(sem)
            w_in, c_in, w_half, w_ready, v_init = sem("w_in"), sem("c_in"), sem("w_half"), sem("w_ready"), sem("v_init")
            pj_done, hi_done, lo_done, cos_done, rot_done, sin_done = (
                sem("pj_done"), sem("hi_done"), sem("lo_done"), sem("cos_done"), sem("rot_done"), sem("sin_done"))
            turned_done, p1_done, rest_done, p2_done, p3_done = (
                sem("turned_done"), sem("p1_done"), sem("rest_done"), sem("p2_done"), sem("p3_done"))
            v_read, vt_done, v_done = sem("v_read"), sem("vt_done"), sem("v_done")
            part_out = [sem(f"part_out{s}") for s in range(NPB)]

            UNITS = WQ // P * NCH
            V_UNITS = (NCH, 2 * NCH)
            TURN = [n for n in range(UNITS) if not V_UNITS[0] <= n < V_UNITS[1]]
            number = {n: r for r, n in enumerate(TURN)}

            with nc.Block() as block:
                @block.sync
                def _(sp):
                    sp.dma_start(w_raw[:, :, :], m.dram["w_qkv"]).then_inc(w_in, 16)
                    sp.dma_start(swap_raw[:, :], m.dram["swap"]).then_inc(w_in, 16)
                    sp.dma_start(b_qkv[:, :], m.dram["b_qkv"]).then_inc(c_in, 16)
                    sp.dma_start(cos[:, :], m.dram["cos"]).then_inc(c_in, 16)
                    sp.dma_start(sin[:, :], m.dram["sin"]).then_inc(c_in, 16)
                    for n in TURN:
                        j, c = divmod(n, NCH)
                        r = number[n]
                        row = (j if j == 0 else j - 1) * P
                        sp.wait_ge(p3_done, r + 1)
                        sp.dma_start(parts_dram[:, row:row + P, c * CH:(c + 1) * CH].rearrange("a p s -> p a s"),
                                     part[r % NPB][:, :, :]).then_inc(part_out[r % NPB], 16)
                    for s in range(NPB):
                        sp.wait_ge(part_out[s], 16 * len(range(s, len(TURN), NPB)))

                @block.gpsimd
                def _(pool):
                    nc.gpsimd.memset(v_all[:, :, :, :], 0.0).then_inc(v_init, 1)
                    pool.wait_ge(w_in, 32)
                    nc.gpsimd.tensor_copy(w_hi[:, :, :], w_raw[:, :, :]).then_inc(w_half, 1)
                    nc.gpsimd.tensor_copy(swap[:, :], swap_raw[:, :]).then_inc(w_half, 1)
                    rstd_gpsimd(m, pool, nm)
                    pool.wait_ge(w_half, 2)
                    nc.gpsimd.tensor_tensor(w_lo[:, :, :], w_raw[:, :, :], w_hi[:, :, :].bitcast(F32),
                                            ALU.subtract).then_inc(w_ready, 1)
                    pool.wait_ge(v_init, 1)
                    nc.gpsimd.memset(v_all[:, :, :, HD:HD + 1], 1.0).then_inc(v_init, 1)
                    pool.wait_ge(v_init, 2)
                    nc.gpsimd.memset(ks[STACK:STACK + MROWS, :], 1.0).then_inc(v_init, 1)
                    pool.wait_ge(v_init, 3)
                    for n in range(UNITS + 4):
                        if n - 1 in number:
                            r = number[n - 1]
                            pool.wait_ge(sin_done, r + 1)
                            if r >= 2:
                                pool.wait_ge(rest_done, r - 1)
                            nc.gpsimd.tensor_tensor(turned[r % 2][:, :], with_cos[r % 2][:, :], with_sin[r % 2][:, :],
                                                    ALU.add).then_inc(turned_done, 1)
                        if n - 2 in number:
                            r = number[n - 2]
                            pool.wait_ge(p1_done, r + 1)
                            if r >= 2:
                                pool.wait_ge(p3_done, r - 1)
                            nc.gpsimd.tensor_tensor(rest[r % 2][:, :], turned[r % 2][:, :], part[r % NPB][:, 0, :],
                                                    ALU.subtract).then_inc(rest_done, 1)
                        if n - 3 in number:
                            r = number[n - 3]
                            pool.wait_ge(p2_done, r + 1)
                            nc.gpsimd.tensor_tensor(part[r % NPB][:, 2, :], rest[r % 2][:, :], part[r % NPB][:, 1, :],
                                                    ALU.subtract).then_inc(p3_done, 1)

                @block.tensor
                def _(pe):
                    for t in range(T):
                        transpose_tile(m, pe, nm, xp[t % 2], t)
                    pe.wait_ge(nm.xt_lo, T)
                    pe.wait_ge(w_ready, 1)
                    for n in range(UNITS + 1):
                        if n < UNITS:
                            j, c = divmod(n, NCH)
                            if n - 2 in number:
                                pe.wait_ge(cos_done, number[n - 2] + 1)
                            elif n >= 2:
                                pe.wait_ge(v_read, n - 2 - V_UNITS[0] + 1)
                            cols = slice(c * CH, (c + 1) * CH)
                            feats = slice(j * P, (j + 1) * P)
                            product(nc, pj[n % 2][:, :], [(w_hi[:, k, feats], w_lo[:, k, feats], m.xt_hi[:, k, cols],
                                                           m.xt_lo[:, k, cols]) for k in range(KT)]).then_inc(pj_done, 1)
                        if n - 1 in number:
                            r = number[n - 1]
                            pe.wait_ge(lo_done, r + 1)
                            if r >= 2:
                                pe.wait_ge(sin_done, r - 1)
                            nc.tensor.matmul(rot[r % 2][:, :], swap[:, :], q_hi[r % 2][:, :], start=True, stop=False)
                            nc.tensor.matmul(rot[r % 2][:, :], swap[:, :], q_lo[r % 2][:, :], start=False,
                                             stop=True).then_inc(rot_done, 1)
                        elif n == V_UNITS[1]:
                            pe.wait_ge(v_read, NCH)
                            for t in range(T):
                                last = nc.tensor.transpose(xp[t * P // CH][:, t * P % CH:t * P % CH + P],
                                                           vt[:, t * P:(t + 1) * P], m.ident[:, :])
                            last.then_inc(vt_done, 1)

                @block.scalar
                def _(act):
                    for t in range(T):
                        hi_tile(m, act, nm, xp[t % 2], t)
                    act.wait_ge(c_in, 48)
                    for n in range(UNITS + 4):
                        if n < UNITS:
                            j, c = divmod(n, NCH)
                            act.wait_ge(pj_done, n + 1)
                            if n in number:
                                r = number[n]
                                if r >= 2:
                                    act.wait_ge(rot_done, r - 1)
                                nc.scalar.activation(q_hi[r % 2][:, :], pj[n % 2][:, :], ACT.Identity,
                                                     bias=b_qkv[:, j:j + 1]).then_inc(hi_done, 1)
                            else:
                                nc.scalar.activation(vt[:, c * CH:(c + 1) * CH], pj[n % 2][:, :], ACT.Identity,
                                                     bias=b_qkv[:, j:j + 1]).then_inc(v_read, 1)
                        if n - 2 in number:
                            r = number[n - 2]
                            act.wait_ge(turned_done, r + 1)
                            if r >= NPB:
                                act.wait_ge(part_out[r % NPB], 16 * (r // NPB))
                            nc.scalar.copy(part[r % NPB][:, 0, :], turned[r % 2][:, :]).then_inc(p1_done, 1)
                        if n - 3 in number:
                            r = number[n - 3]
                            act.wait_ge(rest_done, r + 1)
                            nc.scalar.copy(part[r % NPB][:, 1, :], rest[r % 2][:, :]).then_inc(p2_done, 1)

                @block.vector
                def _(dve):
                    normalise_vector(m, dve, nm, lambda t: lo_tile(m, dve, nm, xp[t % 2], t))
                    dve.wait_ge(c_in, 48)
                    for n in range(UNITS + 1):
                        j, c = divmod(n, NCH)
                        cols = slice(c * CH, (c + 1) * CH)
                        if n in number:
                            r = number[n]
                            dve.wait_ge(hi_done, r + 1)
                            nc.vector.scalar_tensor_tensor(out=q_lo[r % 2][:, :], in0=pj[n % 2][:, :], scalar=b_qkv[:, j:j + 1],
                                                           in1=q_hi[r % 2][:, :].bitcast(F32), op0=ALU.add,
                                                           op1=ALU.subtract).then_inc(lo_done, 1)
                            if r >= 2:
                                dve.wait_ge(turned_done, r - 1)
                            nc.vector.scalar_tensor_tensor(out=with_cos[r % 2][:, :], in0=pj[n % 2][:, :],
                                                           scalar=b_qkv[:, j:j + 1], in1=cos[:, cols], op0=ALU.add,
                                                           op1=ALU.mult).then_inc(cos_done, 1)
                        if n - 1 in number:
                            r = number[n - 1]
                            c = (n - 1) % NCH
                            dve.wait_ge(rot_done, r + 1)
                            nc.vector.tensor_tensor(with_sin[r % 2][:, :], rot[r % 2][:, :], sin[:, c * CH:(c + 1) * CH],
                                                    ALU.mult).then_inc(sin_done, 1)
                        if n == V_UNITS[1] + 1:
                            dve.wait_ge(vt_done, 1)
                            dve.wait_ge(v_init, 2)
                            for c in range(NCH):
                                nc.vector.tensor_copy(v_all[:, c * (CH // P):(c + 1) * (CH // P), :, 0:HD],
                                                      xp[c][:, :].rearrange("p (t g d) -> p t g d", t=CH // P, g=KV)).then_inc(v_done, 1)

        with ExitStack() as ctx:
            def sb(what, shape, dt=F32):
                return ctx.enter_context(nc.sbuf_tensor(f"{name}_{what}", shape, dt))

            def pb(what, shape, dt=F32):
                return ctx.enter_context(nc.psum_tensor(f"{name}_{what}", shape, dt))

            QG = QPK * S
            TC = CH // P
            qs = sb("qs", [P, HEADS * S], BF16)
            v_now = sb("v_now", [P, T, 2 * HD])
            masks = sb("masks", [P, 2, P])
            mask_qk = sb("mask_qk", [P, P], BF16)
            mask_kq = sb("mask_kq", [P, P], BF16)
            ident = sb("ident", [P, P], BF16)
            warm = sb("warm", [1, 1])
            top = sb("top", [P, NCH, T, QPK])
            best = sb("best", [P, TC, QPK])
            neg = sb("neg", [P, TC, QPK])
            left = sb("left", [P, TC, QPK])
            neg_parts = [sb(f"neg_parts{h}", [P, TC, MROWS, QPK], BF16) for h in range(NCH)]
            neg_turned = [sb(f"neg_turned{h}", [MROWS * QPK, CH], BF16) for h in range(NCH)]
            prob = [sb(f"prob{s}", [P, QPK, CH]) for s in range(2)]
            out_t = sb("out_t", [P, CH])
            inv = sb("inv", [P, TC, QPK])
            sc = [pb(f"sc{s}", [P, CH]) for s in range(2)]
            mx = [pb(f"mx{s}", [P, 2, CH]) for s in range(2)]
            po = pb("po", [P, CH])
            small = pb("small", [P, 2 * CH], BF16)
            small_f = small[:, :].bitcast(F32)

            c_in2, consts, stack_in = sem("c_in2"), sem("consts"), sem("stack_in")
            mx_done, mx_read, neg_chain, neg_done, neg_turn, neg_read = (
                sem("mx_done"), sem("mx_read"), sem("neg_chain"), sem("neg_done"), sem("neg_turn"), sem("neg_read"))
            neg_in = [sem(f"neg_in{h}") for h in range(NCH)]
            sc_done, exp_done, v_ready, pv_done = sem("sc_done"), sem("exp_done"), sem("v_ready"), sem("pv_done")
            po_read, out_turn, inv_done, ctx_done = sem("po_read"), sem("out_turn"), sem("inv_done"), sem("ctx_done")

            MAX_UNITS = [(t, kc, a) for t in range(T) for kc in range(t * P // CH + 1) for a in range(QPK // 2)]
            NMU = len(MAX_UNITS)
            HALF0 = sum(t < TC for t, _, _ in MAX_UNITS)
            STEPS = [(c, kb) for c in range(NCH) for kb in range((c + 1) * TC)]
            NS = len(STEPS)
            C0 = TC
            NEG_OPS = (4, 5)
            LOADS = 2 * len(Q_PART)

            with nc.Block() as block:
                @block.sync
                def _(sp):
                    sp.dma_start(masks[:, :, :], m.dram["masks"]).then_inc(c_in2, 16)

                    def load(g):
                        for a in range(len(Q_PART)):
                            rows = slice(a * HD, (a + 1) * HD)
                            sp.dma_start(ks[rows, bass.ds(g * S, S)],
                                         parts_dram[K_PART[a], bass.ds(g * HD, HD), :]).then_inc(stack_in, 16)
                            sp.dma_start(qs[rows, bass.ds(g * QG, QG)].rearrange("d (h s) -> d h s", h=QPK),
                                         parts_dram[Q_PART[a], bass.ds(g * (QPK * HD) + KV * HD, QPK * HD), :].rearrange(
                                             "(h d) s -> d h s", h=QPK)).then_inc(stack_in, 16)

                    load(0)
                    with sp.Fori(1, KV) as g:
                        sp.wait_ge(stack_in, g * (16 * LOADS))
                        load(g)

                @block.gpsimd
                def _(pool):
                    def put_maxima(gn, h):
                        pool.wait_ge(neg_read, gn * NCH + h + 1)
                        for a in range(MROWS):
                            pool.dma_start(qs[STACK + a:STACK + a + 1, bass.ds(gn * QG, QG)].rearrange(
                                "a (h s) -> a h s", h=QPK)[:, :, h * CH:(h + 1) * CH],
                                neg_turned[h][a * QPK:(a + 1) * QPK, :]).then_inc(neg_in[h], 16)

                    def values(g):
                        pool.wait_ge(pv_done, g * NS + 1)
                        nc.gpsimd.tensor_copy(v_now[:, :, :], v_all[:, :, bass.ds(g, 1), :].rearrange(
                            "p t a d -> p t (a d)")).then_inc(v_ready, 1)

                    for h in range(NCH):
                        put_maxima(0, h)
                    with pool.Fori(0, KV - 1) as g:
                        values(g)
                        for h in range(NCH):
                            put_maxima(g + 1, h)
                    values(KV - 1)

                @block.tensor
                def _(pe):
                    def maximum(gn, i):
                        t, kc, a = MAX_UNITS[i]
                        mu = gn * NMU + i
                        if i == 0:
                            pe.wait_ge(stack_in, gn * (16 * LOADS) + 16 * LOADS)
                        if not isinstance(mu, int) or mu >= 2:
                            pe.wait_ge(mx_read, mu - 1)
                        w = min(CH, (t + 1) * P - kc * CH)
                        diagonal = t * P < (kc + 1) * CH
                        for b in range(2):
                            at = gn * QG + ((2 * a + b) * S + t * P)
                            last = nc.tensor.matmul(mx[i % 2][:, b, 0:w], qs[0:STACK, bass.ds(at, P)],
                                                    ks[0:STACK, bass.ds(gn * S + kc * CH, w)], start=True, stop=not diagonal)
                            if diagonal:
                                last = nc.tensor.matmul(mx[i % 2][:, b, w - P:w], ident[:, :], mask_qk[:, :], start=False, stop=True)
                        last.then_inc(mx_done, 1)

                    def turn_maxima(gn, h):
                        pe.wait_ge(neg_done, gn * NCH + h + 1)
                        if not isinstance(gn, int) or gn * NCH + h >= 1:
                            pe.wait_ge(neg_read, gn * NCH + h)
                        for u in range(TC):
                            last = nc.tensor.transpose(small[0:MROWS * QPK, u * P:(u + 1) * P],
                                                       neg_parts[h][:, u, :, :].rearrange("p a h -> p (a h)"), ident[:, :])
                        last.then_inc(neg_turn, 1)

                    def scores(g, u, h):
                        c, kb = STEPS[u]
                        pe.wait_ge(exp_done, g * (NS * QPK) + (u * QPK + h + 1))
                        o = max(0, kb * P - c * CH)
                        diagonal = kb * P >= c * CH
                        b = (u * QPK + h) % 2
                        nc_last = nc.tensor.matmul(sc[b][:, o:CH], ks[0:STACK + MROWS, bass.ds(g * S + kb * P, P)],
                                                   qs[0:STACK + MROWS, bass.ds(g * QG + (h * S + c * CH + o), CH - o)],
                                                   start=True, stop=not diagonal)
                        if diagonal:
                            nc_last = nc.tensor.matmul(sc[b][:, o:o + P], ident[:, :], mask_kq[:, :], start=False, stop=True)
                        nc_last.then_inc(sc_done, 1)

                    def values(g, u):
                        c, kb = STEPS[u]
                        pe.wait_ge(exp_done, g * (NS * QPK) + ((u + 1) * QPK + 2))
                        if u == 0:
                            pe.wait_ge(v_ready, g + 1)
                        if kb == 0:
                            pe.wait_ge(po_read, g * NCH + (c + 1))
                        o = max(0, kb * P - c * CH)
                        for h in range(QPK):
                            last = nc.tensor.matmul(po[2 * HD * h:2 * HD * (h + 1), o:CH], v_now[:, kb, :],
                                                    prob[u % 2][:, h, o:CH], start=(kb == 0), stop=(kb == (c + 1) * TC - 1))
                        last.then_inc(pv_done, 1)

                    def turn_output(g, c):
                        pe.wait_ge(po_read, g * NCH + (c + 2))
                        for u in range(TC):
                            last = nc.tensor.transpose(small_f[:, u * P:(u + 1) * P], out_t[:, u * P:(u + 1) * P], m.ident[:, :])
                        last.then_inc(out_turn, 1)

                    def group(g, more):
                        for u in range(NS):
                            if u == 0 or u == C0:
                                pe.wait_ge(neg_in[STEPS[u][0]], g * (16 * MROWS) + 16 * MROWS)
                            scores(g, u, 0)
                            scores(g, u, 1)
                            if more:
                                maximum(g + 1, 2 * u)
                            scores(g, u, 2)
                            if u >= 1:
                                values(g, u - 1)
                            scores(g, u, 3)
                            if more:
                                maximum(g + 1, 2 * u + 1)
                            if u == C0 + 1 and more:
                                pe.wait_ge(ctx_done, g * NCH + 1)
                                turn_maxima(g + 1, 0)
                            if u == C0 + 4:
                                if more:
                                    pe.wait_ge(neg_read, g * NCH + NCH + 1)
                                turn_output(g, 0)
                        values(g, NS - 1)
                        pe.wait_ge(ctx_done, g * NCH + 2)
                        if more:
                            turn_maxima(g + 1, 1)
                            pe.wait_ge(neg_read, g * NCH + NCH + 2)
                        turn_output(g, 1)

                    pe.sem_inc(pv_done, 1)
                    pe.sem_inc(out_turn, 1)
                    pe.wait_ge(consts, 3)
                    for i in range(NMU):
                        maximum(0, i)
                        if i == HALF0 + 1:
                            turn_maxima(0, 0)
                    turn_maxima(0, 1)
                    with pe.Fori(0, KV - 1) as g:
                        group(g, True)
                    group(KV - 1, False)

                @block.scalar
                def _(act):
                    def read_maxima(gn, h):
                        act.wait_ge(neg_turn, gn * NCH + h + 1)
                        if not isinstance(gn, int) or gn:
                            act.wait_ge(neg_in[h], gn * (16 * MROWS))
                        nc.scalar.copy(neg_turned[h][:, :], small[0:MROWS * QPK, 0:CH]).then_inc(neg_read, 1)

                    def group(g, more):
                        for u in range(NS):
                            c, kb = STEPS[u]
                            o = max(0, kb * P - c * CH)
                            act.wait_ge(pv_done, g * NS + (max(0, u - 1) + 1))
                            for h in range(QPK):
                                act.wait_ge(sc_done, g * (NS * QPK) + (u * QPK + h + 1))
                                nc.scalar.activation(prob[u % 2][:, h, o:CH], sc[(u * QPK + h) % 2][:, o:CH], ACT.Exp,
                                                     scale=SCALE).then_inc(exp_done, 1)
                            if u == C0 + 2 and more:
                                read_maxima(g + 1, 0)
                        if more:
                            read_maxima(g + 1, 1)

                    nc.scalar.activation(warm[:, :], m.ident[0:1, 0:1], ACT.Exp).then_inc(exp_done, 2)
                    for h in range(NCH):
                        read_maxima(0, h)
                    with act.Fori(0, KV - 1) as g:
                        group(g, True)
                    group(KV - 1, False)

                @block.vector
                def _(dve):
                    def maximum(gn, i):
                        t, kc, a = MAX_UNITS[i]
                        w = min(CH, (t + 1) * P - kc * CH)
                        dve.wait_ge(mx_done, gn * NMU + (i + 1))
                        nc.vector.tensor_reduce(top[:, kc, t, 2 * a:2 * a + 2], mx[i % 2][:, :, 0:w], AX.X,
                                                ALU.max).then_inc(mx_read, 1)

                    def split_maxima(gn, h, units):
                        base = gn * sum(NEG_OPS) + sum(NEG_OPS[:h])
                        dve.wait_ge(mx_read, gn * NMU + units)
                        k = 0
                        source = top[:, 0, 0:TC, :]
                        if h:
                            nc.vector.tensor_tensor(best[:, :, :], top[:, 0, TC:T, :], top[:, 1, TC:T, :], ALU.max).then_inc(neg_chain, 1)
                            k += 1
                            dve.wait_ge(neg_chain, base + k)
                            source = best[:, :, :]
                        nc.vector.tensor_scalar(neg[:, :, :], source, -1.0, None, ALU.mult).then_inc(neg_chain, 1)
                        k += 1
                        dve.wait_ge(neg_chain, base + k)
                        if not isinstance(gn, int):
                            dve.wait_ge(neg_turn, gn * NCH + h - 1)
                        nc.vector.tensor_copy(neg_parts[h][:, :, 0, :], neg[:, :, :]).then_inc(neg_chain, 1)
                        k += 1
                        dve.wait_ge(neg_chain, base + k)
                        nc.vector.tensor_tensor(left[:, :, :], neg[:, :, :], neg_parts[h][:, :, 0, :], ALU.subtract).then_inc(neg_chain, 1)
                        k += 1
                        dve.wait_ge(neg_chain, base + k)
                        nc.vector.tensor_copy(neg_parts[h][:, :, 1, :], left[:, :, :]).then_inc(neg_chain, 1)
                        k += 1
                        dve.wait_ge(neg_chain, base + k)
                        nc.vector.tensor_tensor(neg_parts[h][:, :, 2, :], left[:, :, :], neg_parts[h][:, :, 1, :],
                                                ALU.subtract).then_inc(neg_done, 1)

                    def read_output(g, c):
                        dve.wait_ge(pv_done, g * NS + ((C0, NS)[c] + 1))
                        dve.wait_ge(out_turn, g * NCH + (c + 1))
                        nc.vector.tensor_copy(out_t[:, :], po[:, :]).then_inc(po_read, 1)

                    def normalise(g, c):
                        dve.wait_ge(out_turn, g * NCH + (c + 2))
                        o = small_f.rearrange("p (t h d) -> p t h d", t=TC, h=QPK)
                        nc.vector.reciprocal(inv[:, :, :], o[:, :, :, HD]).then_inc(inv_done, 1)
                        dve.wait_ge(inv_done, g * NCH + c + 1)
                        nc.vector.tensor_tensor(m.xn[:, c * TC:(c + 1) * TC, bass.ds(g * (QPK * HD), QPK * HD)].rearrange(
                            "p t (h d) -> p t h d", h=QPK), o[:, :, :, 0:HD],
                            inv[:, :, :].unsqueeze(3).broadcast_to([P, TC, QPK, HD]), ALU.mult).then_inc(ctx_done, 1)

                    def group(g, more):
                        for u in range(NS):
                            if more:
                                maximum(g + 1, 2 * u)
                            if u == C0:
                                read_output(g, 0)
                            if more:
                                maximum(g + 1, 2 * u + 1)
                                if 2 * u + 2 == HALF0:
                                    split_maxima(g + 1, 0, HALF0)
                            if u == C0 + 5:
                                normalise(g, 0)
                        if more:
                            split_maxima(g + 1, 1, NMU)
                        read_output(g, 1)
                        normalise(g, 1)

                    dve.sem_inc(po_read, 1)
                    dve.sem_inc(ctx_done, 1)
                    dve.wait_ge(c_in2, 16)
                    nc.vector.tensor_copy(mask_qk[:, :], masks[:, 0, :]).then_inc(consts, 1)
                    nc.vector.tensor_copy(mask_kq[:, :], masks[:, 1, :]).then_inc(consts, 1)
                    nc.vector.tensor_copy(ident[:, :], m.ident[:, :]).then_inc(consts, 1)
                    for i in range(NMU):
                        maximum(0, i)
                        if i + 1 == HALF0:
                            split_maxima(0, 0, HALF0)
                    split_maxima(0, 1, NMU)
                    with dve.Fori(0, KV - 1) as g:
                        group(g, True)
                    group(KV - 1, False)

        with ExitStack() as ctx:
            def sb(what, shape, dt=F32):
                return ctx.enter_context(nc.sbuf_tensor(f"{name}_{what}", shape, dt))

            def pb(what, shape, dt=F32):
                return ctx.enter_context(nc.psum_tensor(f"{name}_{what}", shape, dt))

            wd_raw = sb("wd_raw", [P, KT, H])
            wd_hi = sb("wd_hi", [P, KT, H], F32R)
            wd_lo = sb("wd_lo", [P, KT, H], F32R)
            b_out = sb("b_out", [P, H])
            xp = [pb(f"xpd{s}", [P, CH]) for s in range(2)]
            yp = [pb(f"yp{s}", [P, CH]) for s in range(2)]
            cm = NormSems(sem, "ctx")
            wd_in, wd_half, wd_ready, x_biased, y_done, x_done = (
                sem("wd_in"), sem("wd_half"), sem("wd_ready"), sem("x_biased"), sem("y_done"), sem("x_done"))

            with nc.Block() as block:
                @block.sync
                def _(sp):
                    sp.dma_start(wd_raw[:, :, :], m.dram["w_dense"]).then_inc(wd_in, 16)
                    sp.dma_start(b_out[:, :], m.dram["b_dense"].rearrange("(a h) -> a h", a=1).broadcast_to([P, H])).then_inc(wd_in, 16)

                @block.gpsimd
                def _(pool):
                    pool.wait_ge(wd_in, 32)
                    nc.gpsimd.tensor_copy(wd_hi[:, :, :], wd_raw[:, :, :]).then_inc(wd_half, 1)
                    pool.wait_ge(wd_half, 1)
                    nc.gpsimd.tensor_tensor(wd_lo[:, :, :], wd_raw[:, :, :], wd_hi[:, :, :].bitcast(F32),
                                            ALU.subtract).then_inc(wd_ready, 1)
                    nc.gpsimd.tensor_tensor(m.x[:, :, :], m.x[:, :, :], b_out[:, :].unsqueeze(1).broadcast_to([P, T, H]),
                                            ALU.add).then_inc(x_biased, 1)

                @block.tensor
                def _(pe):
                    for t in range(T):
                        transpose_tile(m, pe, cm, xp[t % 2], t, ready=False)
                    pe.wait_ge(wd_ready, 1)
                    for t in range(T):
                        pe.wait_ge(cm.xt_lo, t + 1)
                        if t >= 2:
                            pe.wait_ge(x_done, t - 1)
                        rows = slice(t * P, (t + 1) * P)
                        product(nc, yp[t % 2][:, :], [(m.xt_hi[:, k, rows], m.xt_lo[:, k, rows], wd_hi[:, k, :], wd_lo[:, k, :])
                                                      for k in range(KT)]).then_inc(y_done, 1)

                @block.scalar
                def _(act):
                    for t in range(T):
                        hi_tile(m, act, cm, xp[t % 2], t)

                @block.vector
                def _(dve):
                    for t in range(T):
                        lo_tile(m, dve, cm, xp[t % 2], t)
                    dve.wait_ge(x_biased, 1)
                    for t in range(T):
                        dve.wait_ge(y_done, t + 1)
                        nc.vector.tensor_tensor(m.x[:, t, :], yp[t % 2][:, :], m.x[:, t, :], ALU.add).then_inc(x_done, 1)



def program(nc, m_in, out, stages):
    m = Shared()
    m.nc = nc
    m.taken = []
    m.dram = m_in
    layers = {"moe": moe_layer, "causal": causal_attention_layer, "butter": butterfly_layer, "full": full_attention_layer}
    with ExitStack() as ctx:
        def sb(what, shape, dt=F32):
            return ctx.enter_context(nc.sbuf_tensor(what, shape, dt))

        m.x = sb("x", [P, T, H])
        m.xn = sb("xn", [P, T, H])
        m.xt_hi = sb("xt_hi", [P, KT, S], F32R)
        m.xt_lo = sb("xt_lo", [P, KT, S], F32R)
        m.ident = sb("ident", [P, P])
        m.stats = sb("stats", [P, T, 6])
        m.mean_var = sb("mean_var", [P, T, 2])
        m.var_eps = sb("var_eps", [P, T])
        m.minus_half = sb("minus_half", [P, T])
        m.zero = sb("zero", [P, 1])
        m.rstd = sb("rstd", [P, T])
        x_in = ctx.enter_context(nc.semaphore("x_in"))
        x_out = ctx.enter_context(nc.semaphore("x_out"))
        with nc.Block() as block:
            @block.gpsimd
            def _(pool):
                nc.gpsimd.memset(m.minus_half[:, :], -0.5)
                nc.gpsimd.memset(m.zero[:, :], 0.0)

            @block.sync
            def _(sp):
                sp.dma_start(m.x[:, :, :], m.dram["hidden"].rearrange("(t p) h -> p t h", p=P)).then_inc(x_in, 16)
                sp.dma_start(m.ident[:, :], m.dram["identity"]).then_inc(x_in, 16)
                sp.wait_ge(x_in, 32)
        for n, stage in enumerate(stages):
            layers[stage](m, f"{stage}{n}")
            m.release()
        with nc.Block() as block:
            @block.sync
            def _(sp):
                sp.dma_start(out.rearrange("(t p) h -> p t h", p=P), m.x[:, :, :]).then_inc(x_out, 16)
                sp.wait_ge(x_out, 16)


STAGES = ("moe", "causal", "moe", "butter", "full", "butter")


def layout(inputs):
    import numpy as np

    f = np.ascontiguousarray
    i = {k: np.asarray(v) for k, v in inputs.items()}
    d = {}

    def by_partition(w):
        return f(w.reshape(w.shape[0] // P, P, w.shape[1]).transpose(1, 0, 2))

    d["hidden"] = f(i["L0_attn_hidden_states"].reshape(S, H))
    gate = np.concatenate([i["L0_ffn_Sg"][None], i["L0_ffn_Wg"]])
    up = np.concatenate([i["L0_ffn_Su"][None], i["L0_ffn_Wu"]])
    down = np.concatenate([i["L0_ffn_Sd"][None], i["L0_ffn_Wd"]])
    gu = np.concatenate([gate, up], axis=1).transpose(0, 2, 1)
    d["w_gu"] = f(gu.reshape(NE, KT, P, 2 * FI).transpose(0, 2, 1, 3).reshape(NE, P, GU_COLS))
    d["w_down"] = f(down.transpose(0, 2, 1).reshape(NE, IT, P, H).transpose(0, 2, 1, 3).reshape(NE, P, IT * H))
    router = np.zeros((H, P), np.float32)
    router[:, :E] = i["L0_ffn_gate_w"].T
    d["gate_w"] = by_partition(router)
    d["gate_bias"] = f(i["L0_ffn_bias"].reshape(E, 1))
    kv, hd, qpk = 8, 16, 4
    w = i["L0_attn_w_qkv"].reshape(kv, qpk + 2, hd, H)
    b = i["L0_attn_b_qkv"].reshape(kv, qpk + 2, hd)
    w = np.concatenate([w[:, qpk].reshape(-1, H), w[:, qpk + 1].reshape(-1, H), w[:, :qpk].reshape(-1, H)])
    b = np.concatenate([b[:, qpk].reshape(-1), b[:, qpk + 1].reshape(-1), b[:, :qpk].reshape(-1)])
    d["w_qkv"] = by_partition(w.T)
    d["b_qkv"] = f(b.reshape(-1, P).T)
    d["w_dense"] = by_partition(i["L0_attn_w_dense"].T)
    d["b_dense"] = f(i["L0_attn_b_dense"])
    d["perm"] = f(i["L1_ffn_perm"])
    d["perm_col"] = f(d["perm"].reshape(KT, P).T)
    d["up"] = f(i["L1_ffn_up"].reshape(KT, P, -1).transpose(1, 0, 2))
    d["down"] = f(i["L1_ffn_down"].transpose(1, 0, 2))
    d["w1_qkv"] = by_partition(i["L1_attn_Wqkv"])
    d["w1_out"] = f(i["L1_attn_Wo"])
    d["b1_qkv"] = f(i["L1_attn_bqkv"].reshape(-1, P).T)
    d["b1_out"] = f(i["L1_attn_bo"])
    d["identity"] = np.eye(P, dtype=np.float32)
    lower = (np.arange(E)[None, :] < np.arange(E)[:, None]).astype(np.float32)
    d["tie"] = f(np.broadcast_to(lower.reshape(1, -1), (P, E * E)))
    d["index_row"] = np.arange(H, dtype=np.float32)
    d["index_col"] = f(np.arange(H, dtype=np.float32).reshape(KT, P).T)
    inv_freq = np.float32(1) / np.power(np.float32(1e6), np.arange(0, hd, 2, dtype=np.float32) / np.float32(hd))
    angle = inv_freq.astype(np.float32)[:, None] * np.arange(S, dtype=np.float32)[None, :]
    d["cos"] = f(np.tile(np.cos(angle), (2 * P // hd, 1)).astype(np.float32))
    d["sin"] = f(np.tile(np.sin(angle), (2 * P // hd, 1)).astype(np.float32))
    swap = np.zeros((P, P), np.float32)
    for o in range(P):
        if o % hd < hd // 2:
            swap[o + hd // 2, o] = -1
        else:
            swap[o - hd // 2, o] = 1
    d["swap"] = swap
    later = np.where(np.arange(P)[None, :] > np.arange(P)[:, None], np.float32(-1e30), np.float32(0))
    d["masks"] = f(np.stack([later, later.T], axis=1).astype(np.float32))
    return d


def kernel(**inputs):
    import numpy as _np
    import concourse.bacc as _bacc
    from concourse import mybir as _mybir
    from concourse.bass_utils import run_bass_kernel_spmd as _run

    nc = _bacc.Bacc("TRN2", target_bir_lowering=False, num_devices=1)
    arrays, aps = {}, {}
    for name, a in layout(inputs).items():
        arrays[f"in_{name}"] = a
        aps[name] = nc.dram_tensor(f"in_{name}", a.shape, _mybir.dt.from_np(a.dtype), kind="ExternalInput").ap()
    out = nc.dram_tensor("out", (S, H), _mybir.dt.from_np(_np.dtype("float32")), kind="ExternalOutput").ap()
    program(nc, aps, out, STAGES)
    r = _run(nc, [arrays], core_ids=[0])
    return r.results[0]["out"].reshape(1, S, H)
```

```python
from contextlib import ExitStack

import concourse.bass as bass
from concourse import mybir

ALU = mybir.AluOpType
ACT = mybir.ActivationFunctionType
AX = mybir.AxisListType
F32 = mybir.dt.float32
F32R = mybir.dt.float32r
BF16 = mybir.dt.bfloat16
I32 = mybir.dt.int32
U32 = mybir.dt.uint32

P = 128
S = 1024
H = 512
T = S // P
KT = H // P
CH = 512
NCH = S // CH
EPS = 1e-5

E = 16
TOPK = 4
NE = E + 1
FI = 256
IT = FI // P
GU_COLS = KT * 2 * FI
W_COLS = GU_COLS + IT * H
RING = 4
NB = (S * TOPK + E * (P - 1)) // P // RING * RING + RING
RAW = 3
DVE_COLS = GU_COLS * 5 // 8
ROW = H + E
ROUTE_COLS = 2 * T - 1 + TOPK + E
COUNT_STEP = T - 1


class Shared:

    def semaphore(self, name):
        self.taken.append(self.nc.alloc_semaphore(name=name))
        return self.taken[-1]

    def gpsimd_dma_semaphore(self, name, adds):
        if name not in self.kept:
            self.kept[name] = self.nc.alloc_semaphore(name=name)
            self.counted[name] = 0
        start = self.counted[name]
        self.counted[name] += adds
        return self.kept[name], start

    def release(self):
        with self.nc.Block() as block:
            @block.sync
            def _(sp):
                for s in self.taken:
                    sp.sem_clear(s)
        for s in self.taken:
            self.nc.release_semaphore(s)
        self.taken = []


def normalise_vector(m, dve, nm, lo_of):
    for t in range(T):
        nc = m.nc
        nc.vector.bn_stats(out=m.stats[:, t, :], in_=m.x[:, t, :]).then_inc(nm.stats, 1)
    for t in range(T):
        dve.wait_ge(nm.stats, t + 1)
        nc.vector.bn_aggr(out=m.mean_var[:, t, :], in_=m.stats[:, t, :]).then_inc(nm.moments, 1)
    dve.wait_ge(nm.rstd, 1)
    for t in range(T):
        nc.vector.tensor_scalar(m.xn[:, t, :], m.x[:, t, :], m.mean_var[:, t, 0:1], m.rstd[:, t:t + 1],
                                ALU.subtract, ALU.mult).then_inc(nm.xn, 1)
        if t >= 1:
            lo_of(t - 1)
    lo_of(T - 1)


def rstd_gpsimd(m, pool, nm):
    pool.wait_ge(nm.moments, T)
    m.nc.gpsimd.tensor_scalar(m.var_eps[:, :], m.mean_var[:, :, 1], EPS, None, ALU.add).then_inc(nm.var_eps, 1)
    pool.wait_ge(nm.var_eps, 1)
    m.nc.gpsimd.tensor_tensor(m.rstd[:, :], m.var_eps[:, :], m.minus_half[:, :], ALU.pow).then_inc(nm.rstd, 1)


class NormSems:
    def __init__(self, sem, name="norm"):
        self.stats = sem(f"{name}_stats")
        self.moments = sem(f"{name}_moments")
        self.var_eps = sem(f"{name}_var_eps")
        self.rstd = sem(f"{name}_rstd")
        self.xn = sem(f"{name}_xn")
        self.xt = sem(f"{name}_xt")
        self.xt_hi = sem(f"{name}_xt_hi")
        self.xt_lo = sem(f"{name}_xt_lo")


def transpose_tile(m, pe, nm, bank, t, ready=True):
    if ready:
        pe.wait_ge(nm.xn, t + 1)
    if t >= 2:
        pe.wait_ge(nm.xt_lo, t - 1)
    for k in range(KT):
        last = m.nc.tensor.transpose(bank[:, k * P:(k + 1) * P], m.xn[:, t, k * P:(k + 1) * P], m.ident[:, :])
    last.then_inc(nm.xt, 1)


def hi_tile(m, act, nm, bank, t):
    act.wait_ge(nm.xt, t + 1)
    m.nc.scalar.copy(m.xt_hi[:, :, t * P:(t + 1) * P],
                     bank[:, :].rearrange("p (k c) -> p k c", k=KT)).then_inc(nm.xt_hi, 1)


def lo_tile(m, dve, nm, bank, t):
    dve.wait_ge(nm.xt_hi, t + 1)
    m.nc.vector.tensor_tensor(m.xt_lo[:, :, t * P:(t + 1) * P], bank[:, :].rearrange("p (k c) -> p k c", k=KT),
                              m.xt_hi[:, :, t * P:(t + 1) * P].bitcast(F32), ALU.subtract).then_inc(nm.xt_lo, 1)


def product(nc, out, pairs):
    n = 0
    for a_hi, a_lo, b_hi, b_lo in pairs:
        for a, b in ((a_hi, b_hi), (a_hi, b_lo), (a_lo, b_hi)):
            last = nc.tensor.matmul(out, a, b, start=(n == 0), stop=(n == 3 * len(pairs) - 1))
            n += 1
    return last


def some(count):
    return not isinstance(count, int) or count > 0


def moe_layer(m, name):
    nc = m.nc
    xn_rows = nc.dram_tensor(f"{name}_xn_rows", (S + P, ROW), F32).ap()
    acc_rows = nc.dram_tensor(f"{name}_acc_rows", (S + P, H), F32).ap()
    with ExitStack() as ctx:
        def sb(what, shape, dt=F32):
            return ctx.enter_context(nc.sbuf_tensor(f"{name}_{what}", shape, dt))

        def sem(what):
            return m.semaphore(f"{name}_{what}")

        def gu_w(w, k):
            return w[:, k * 2 * FI:(k + 1) * 2 * FI]

        def down_w(w, i):
            return w[:, GU_COLS + i * H:GU_COLS + (i + 1) * H]

        raw = sb("raw", [P, RAW * W_COLS])
        w_hi = [sb(f"w_hi{s}", [P, W_COLS], F32R) for s in range(2)]
        w_lo = [sb(f"w_lo{s}", [P, W_COLS], F32R) for s in range(2)]
        silu = [sb(f"silu{s}", [P, FI]) for s in range(2)]
        z = [sb(f"z{s}", [P, FI]) for s in range(2)]
        zt_hi = [sb(f"zt_hi{s}", [P, FI], F32R) for s in range(2)]
        zt_lo = [sb(f"zt_lo{s}", [P, FI], F32R) for s in range(2)]
        token_of = sb("token_of", [P, NB], I32)
        expert_of = sb("expert_of", [1, NB], I32)
        raw_at = sb("raw_at", [1, NB], I32)
        first_of = sb("first_of", [1, E], I32)
        raw_in = [sem(f"raw_in{s}") for s in range(RAW)]

        def load_raw(eng, slot, e):
            at = slot * W_COLS
            eng.dma_start(raw[:, at:at + GU_COLS], m.dram["w_gu"][e]).then_inc(raw_in[slot], 16)
            eng.dma_start(raw[:, at + GU_COLS:at + W_COLS], m.dram["w_down"][e]).then_inc(raw_in[slot], 16)

        with ExitStack() as part:
            def sb(what, shape, dt=F32):
                return part.enter_context(nc.sbuf_tensor(f"{name}_{what}", shape, dt))

            def pb(what, shape, dt=F32):
                return part.enter_context(nc.psum_tensor(f"{name}_{what}", shape, dt))

            gate_raw = sb("gate_raw", [P, KT, P])
            gate_hi = sb("gate_hi", [P, KT, P], F32R)
            gate_lo = sb("gate_lo", [P, KT, P], F32R)
            gate_bias = sb("gate_bias", [E, 1])
            tie = sb("tie", [P, E * E])
            consts = sb("consts", [P, ROUTE_COLS])
            index_row = sb("index_row", [P, P])
            index_col = sb("index_col", [P, KT])
            score_t = sb("score_t", [E, S])
            score = sb("score", [P, T, E])
            beats = sb("beats", [P, T, E, E], BF16)
            equal = sb("equal", [P, T, E, E], BF16)
            rank = sb("rank", [P, T, E])
            mask = sb("mask", [P, T, E], BF16)
            chosen = sb("chosen", [P, T, E])
            total = sb("total", [P, T])
            inv_total = sb("inv_total", [P, T])
            cw = sb("cw", [P, T, E])
            before = sb("before", [P, P], BF16)
            ones = sb("ones", [P, P], BF16)
            over = sb("over", [P, E, T - 1])
            blocks = sb("blocks", [P, E])
            ahead = sb("ahead", [P, E, E])
            first = sb("first", [P, E])
            place = sb("place", [P, T, E])
            pick = sb("pick", [P, T, TOPK, E])
            slot = sb("slot", [P, T, TOPK])
            slot_i = sb("slot_i", [P, T, TOPK], I32)
            block_i = sb("block_i", [P, T, TOPK], I32)
            block_f = sb("block_f", [P, T, TOPK])
            within = sb("within", [P, T, TOPK])
            at_place = sb("at_place", [P, T, TOPK, P], BF16)
            in_block = sb("in_block", [P, T, TOPK, NB], BF16)
            in_block_p = sb("in_block_p", [P, T, TOPK, NB], BF16)
            in_block_t = sb("in_block_t", [P, T, TOPK, NB], BF16)
            padding = sb("padding", [P, NB])
            begun = sb("begun", [1, NB, E], BF16)
            begun_at = sb("begun_at", [1, NB, E], BF16)
            expert_f = sb("expert_f", [1, NB])
            raw_f = sb("raw_f", [1, NB])

            turn = [pb(f"turn{s}", [P, CH]) for s in range(2)]
            gu = [pb(f"gu{s}", [P, CH]) for s in range(2)]
            y = [pb(f"y{s}", [P, CH]) for s in range(2)]
            logits = [pb(f"logits{c}", [P, CH]) for c in range(NCH)]
            counts = logits[1]

            nm = NormSems(sem)
            gate_in, gate_w, const_in = sem("gate_in"), sem("gate_w"), sem("const_in")
            w_hi_done, w_ready = sem("w_hi_done"), sem("w_ready")
            logits_done, sig_done, score_b, score_turned, score_done = (
                sem("logits_done"), sem("sig_done"), sem("score_b"), sem("score_turned"), sem("score_done"))
            compared, tied, route, ready = sem("compared"), sem("tied"), sem("route"), sem("ready")
            mask_done, cw_done, counted, maps_done, mapped = (
                sem("mask_done"), sem("cw_done"), sem("counted"), sem("maps_done"), sem("mapped"))
            gu_done, silu_done, z_done = sem("gu_done"), sem("silu_done"), sem("z_done")
            zt_done, zt_hi_done, zt_lo_done = sem("zt_done"), sem("zt_hi_done"), sem("zt_lo_done")
            y_done, x_done, rows_out = sem("y_done"), sem("x_done"), sem("rows_out")
            table_done = sem("table_done")
            SHARED = 1
            SHARED_RAW = RAW - 1

            block = part.enter_context(nc.Block())

            @block.sync
            def _(sp):
                sp.dma_start(gate_raw[:, :, :], m.dram["gate_w"]).then_inc(gate_in, 16)
                load_raw(sp, SHARED_RAW, 0)
                sp.dma_start(gate_bias[:, :], m.dram["gate_bias"]).then_inc(const_in, 16)
                sp.dma_start(tie[:, :], m.dram["tie"]).then_inc(const_in, 16)
                sp.dma_start(index_row[:, :], m.dram["index_row"][0:P].rearrange("(a h) -> a h", a=1).broadcast_to([P, P])).then_inc(const_in, 16)
                sp.dma_start(index_col[:, :], m.dram["index_col"]).then_inc(const_in, 16)
                sp.dma_start(consts[:, :], m.dram["route"].rearrange("(a h) -> a h", a=1).broadcast_to([P, ROUTE_COLS])).then_inc(const_in, 16)
                for e in range(RAW - 1):
                    load_raw(sp, e, e + 1)
                sp.wait_ge(nm.xn, T)
                sp.dma_start(xn_rows[0:S, 0:H].rearrange("(t p) h -> p t h", p=P), m.xn[:, :, :]).then_inc(rows_out, 16)
                sp.dma_start(xn_rows[S:S + P, 0:H], m.xn[:, 0, :]).then_inc(rows_out, 16)
                sp.wait_ge(w_ready, 1)
                load_raw(sp, SHARED_RAW, RAW)
                sp.wait_ge(cw_done, 1)
                sp.dma_start(xn_rows[0:S, H:ROW].rearrange("(t p) e -> p t e", p=P), cw[:, :, :]).then_inc(rows_out, 16)
                sp.dma_start(xn_rows[S:S + P, H:ROW], cw[:, 0, :]).then_inc(rows_out, 16)
                for t in range(T):
                    sp.wait_ge(x_done, t + 1)
                    sp.dma_start(acc_rows[t * P:(t + 1) * P, :], m.x[:, t, :]).then_inc(rows_out, 16)
                sp.dma_start(acc_rows[S:S + P, :], m.x[:, 0, :]).then_inc(rows_out, 16)
                sp.wait_ge(rows_out, 16 * (T + 5))

            @block.gpsimd
            def _(pool):
                pool.wait_ge(gate_in, 16)
                nc.gpsimd.tensor_copy(gate_hi[:, :, :], gate_raw[:, :, :]).then_inc(gate_w, 1)
                pool.wait_ge(gate_w, 1)
                nc.gpsimd.tensor_tensor(gate_lo[:, :, :], gate_raw[:, :, :], gate_hi[:, :, :].bitcast(F32),
                                        ALU.subtract).then_inc(gate_w, 1)
                rstd_gpsimd(m, pool, nm)
                shared = raw[:, SHARED_RAW * W_COLS:(SHARED_RAW + 1) * W_COLS]
                pool.wait_ge(w_hi_done, 1)
                nc.gpsimd.tensor_tensor(w_lo[SHARED][:, :], shared, w_hi[SHARED][:, :].bitcast(F32),
                                        ALU.subtract).then_inc(w_ready, 1)
                pool.wait_ge(const_in, 80)
                pool.wait_ge(sig_done, NCH)
                nc.gpsimd.tensor_scalar(score_t[:, :], score_t[:, :], gate_bias[:, 0:1], None, ALU.add).then_inc(score_b, 1)
                lower = tie[:, :].rearrange("p (a b) -> p a b", a=E).unsqueeze(1).broadcast_to([P, T, E, E])
                pool.wait_ge(compared, 2)
                nc.gpsimd.tensor_tensor(equal[:, :, :, :], equal[:, :, :, :], lower, ALU.mult).then_inc(tied, 1)
                pool.wait_ge(tied, 1)
                nc.gpsimd.tensor_tensor(beats[:, :, :, :], beats[:, :, :, :], equal[:, :, :, :], ALU.add).then_inc(tied, 1)

            @block.tensor
            def _(pe):
                def turn_z(b, s):
                    pe.wait_ge(z_done, b + 1)
                    for j in range(IT):
                        last = nc.tensor.transpose(turn[s][:, j * P:(j + 1) * P], z[s][:, j * P:(j + 1) * P], m.ident[:, :])
                    last.then_inc(zt_done, 1)

                def gate_up(s, t):
                    product(nc, gu[s][:, :], [(m.xt_hi[:, k, t * P:(t + 1) * P], m.xt_lo[:, k, t * P:(t + 1) * P],
                                               gu_w(w_hi[SHARED], k), gu_w(w_lo[SHARED], k)) for k in range(KT)]).then_inc(gu_done, 1)

                def down(b, s):
                    pe.wait_ge(zt_lo_done, b + 1)
                    if b >= 2:
                        pe.wait_ge(x_done, b - 1)
                    product(nc, y[s][:, :], [(zt_hi[s][:, j * P:(j + 1) * P], zt_lo[s][:, j * P:(j + 1) * P],
                                              down_w(w_hi[SHARED], j), down_w(w_lo[SHARED], j)) for j in range(IT)]).then_inc(y_done, 1)

                for t in range(T):
                    transpose_tile(m, pe, nm, turn[t % 2], t)
                pe.wait_ge(nm.xt_lo, T)
                pe.wait_ge(gate_w, 2)
                for c in range(NCH):
                    cols = slice(c * CH, (c + 1) * CH)
                    product(nc, logits[c][:, :], [(gate_hi[:, k, :], gate_lo[:, k, :], m.xt_hi[:, k, cols], m.xt_lo[:, k, cols])
                                                  for k in range(KT)]).then_inc(logits_done, 1)

                def count():
                    pe.wait_ge(ready, 2)
                    pe.wait_ge(mask_done, 1)
                    taken = mask[:, :, :].rearrange("p t e -> p (t e)")
                    nc.tensor.matmul(counts[:, 0:T * E], before[:, :], taken, start=True, stop=False)
                    for d in range(1, T):
                        nc.tensor.matmul(counts[:, d * E:T * E], ones[:, :], taken[:, 0:(T - d) * E], start=False, stop=(d == T - 1))
                    for t in range(T):
                        last = nc.tensor.matmul(counts[:, T * E:(T + 1) * E], ones[:, :], mask[:, t, :], start=(t == 0), stop=(t == T - 1))
                    last.then_inc(counted, 1)

                pe.wait_ge(w_ready, 1)
                for t in range(T + 1):
                    if t >= 1:
                        turn_z(t - 1, (t - 1) % 2)
                    if t == 1:
                        pe.wait_ge(score_b, 1)
                        for u in range(T):
                            last = nc.tensor.transpose(logits[0][:, u * E:(u + 1) * E], score_t[:, u * P:(u + 1) * P],
                                                       m.ident[0:E, 0:E])
                        last.then_inc(score_turned, 1)
                    if t < T:
                        gate_up(t % 2, t)
                    if t == COUNT_STEP:
                        count()
                    if t >= 1:
                        down(t - 1, (t - 1) % 2)
                pe.wait_ge(maps_done, 3)
                for n in range(T * TOPK):
                    t, r = divmod(n, TOPK)
                    for half in (in_block_p, in_block_t):
                        last = nc.tensor.matmul(logits[0][:, 0:NB], at_place[:, t, r, :], half[:, t, r, :],
                                                start=(n == 0 and half is in_block_p),
                                                stop=(n == T * TOPK - 1 and half is in_block_t))
                last.then_inc(mapped, 1)

            @block.scalar
            def _(act):
                def silu_of(b, s):
                    act.wait_ge(gu_done, b + 1)
                    if b >= 2:
                        act.wait_ge(z_done, b - 1)
                    nc.scalar.activation(silu[s][:, :], gu[s][:, 0:FI], ACT.Silu).then_inc(silu_done, 1)

                def zt_hi_of(b, s):
                    act.wait_ge(zt_done, b + 1)
                    if b >= 2:
                        act.wait_ge(y_done, b - 1)
                    nc.scalar.copy(zt_hi[s][:, :], turn[s][:, 0:FI]).then_inc(zt_hi_done, 1)

                act.wait_ge(raw_in[SHARED_RAW], 32)
                nc.scalar.copy(w_hi[SHARED][:, :], raw[:, SHARED_RAW * W_COLS:(SHARED_RAW + 1) * W_COLS]).then_inc(w_hi_done, 1)
                for t in range(T):
                    hi_tile(m, act, nm, turn[t % 2], t)
                for c in range(NCH):
                    act.wait_ge(logits_done, c + 1)
                    nc.scalar.activation(score_t[:, c * CH:(c + 1) * CH], logits[c][0:E, :], ACT.Sigmoid).then_inc(sig_done, 1)
                for t in range(T + 1):
                    if t >= 1:
                        zt_hi_of(t - 1, (t - 1) % 2)
                    if t == 1:
                        act.wait_ge(score_turned, 1)
                        nc.scalar.copy(score[:, :, :], logits[0][:, 0:T * E].rearrange("p (t e) -> p t e", t=T)).then_inc(score_done, 1)
                    if t < T:
                        silu_of(t, t % 2)

            @block.vector
            def _(dve):
                def z_of(b, s):
                    dve.wait_ge(silu_done, b + 1)
                    if b >= 2:
                        dve.wait_ge(zt_done, b - 1)
                    nc.vector.tensor_tensor(z[s][:, :], silu[s][:, :], gu[s][:, FI:2 * FI], ALU.mult).then_inc(z_done, 1)

                def zt_lo_of(b, s):
                    dve.wait_ge(zt_hi_done, b + 1)
                    nc.vector.tensor_tensor(zt_lo[s][:, :], turn[s][:, 0:FI], zt_hi[s][:, :].bitcast(F32),
                                            ALU.subtract).then_inc(zt_lo_done, 1)

                def add(t, s):
                    dve.wait_ge(y_done, t + 1)
                    nc.vector.scalar_tensor_tensor(out=m.x[:, t, :], in0=y[s][:, :], scalar=0.5, in1=m.x[:, t, :],
                                                   op0=ALU.mult, op1=ALU.add).then_inc(x_done, 1)

                row = index_row[:, :]
                thresholds = consts[:, 0:T - 1]
                tile_start = consts[:, T - 1:2 * T - 1]
                ranks = consts[:, 2 * T - 1:2 * T - 1 + TOPK]
                raw_step = consts[0:1, 2 * T - 1 + TOPK:2 * T - 1 + TOPK + E]

                def compare():
                    dve.wait_ge(score_done, 1)
                    mine = score[:, :, :].unsqueeze(3).broadcast_to([P, T, E, E])
                    other = score[:, :, :].unsqueeze(2).broadcast_to([P, T, E, E])
                    nc.vector.tensor_tensor(equal[:, :, :, :], other, mine, ALU.is_equal).then_inc(compared, 1)
                    nc.vector.tensor_tensor(beats[:, :, :, :], other, mine, ALU.is_gt).then_inc(compared, 1)

                def choose():
                    dve.wait_ge(tied, 2)
                    nc.vector.tensor_reduce(rank[:, :, :], beats[:, :, :, :], AX.X, ALU.add).then_inc(route, 1)
                    dve.wait_ge(route, 1)
                    nc.vector.tensor_scalar(mask[:, :, :], rank[:, :, :], float(TOPK) - 0.5, None, ALU.is_lt).then_inc(mask_done, 1)
                    nc.vector.scalar_tensor_tensor(out=chosen[:, :, :], in0=rank[:, :, :], scalar=float(TOPK) - 0.5,
                                                   in1=score[:, :, :], op0=ALU.is_lt, op1=ALU.mult).then_inc(route, 1)
                    nc.vector.tensor_tensor(pick[:, :, :, :], rank[:, :, :].unsqueeze(2).broadcast_to([P, T, TOPK, E]),
                                            ranks.unsqueeze(1).unsqueeze(3).broadcast_to([P, T, TOPK, E]),
                                            ALU.is_equal).then_inc(route, 1)
                    dve.wait_ge(route, 2)
                    nc.vector.tensor_reduce(total[:, :], chosen[:, :, :], AX.X, ALU.add).then_inc(route, 1)
                    dve.wait_ge(route, 4)
                    nc.vector.tensor_scalar(total[:, :], total[:, :], 1e-20, None, ALU.add).then_inc(route, 1)
                    dve.wait_ge(route, 5)
                    nc.vector.reciprocal(inv_total[:, :], total[:, :]).then_inc(route, 1)
                    dve.wait_ge(route, 6)
                    nc.vector.scalar_tensor_tensor(out=cw[:, :, :], in0=chosen[:, :, :], scalar=0.5,
                                                   in1=inv_total[:, :].unsqueeze(2).broadcast_to([P, T, E]),
                                                   op0=ALU.mult, op1=ALU.mult).then_inc(cw_done, 1)

                def place_tokens():
                    dve.wait_ge(counted, 1)
                    nc.vector.tensor_tensor(over[:, :, :], counts[:, T * E:(T + 1) * E].unsqueeze(2).broadcast_to([P, E, T - 1]),
                                            thresholds.unsqueeze(1).broadcast_to([P, E, T - 1]), ALU.is_gt).then_inc(route, 1)
                    dve.wait_ge(route, 7)
                    nc.vector.tensor_reduce(blocks[:, :], over[:, :, :], AX.X, ALU.add).then_inc(route, 1)
                    dve.wait_ge(route, 8)
                    nc.vector.scalar_tensor_tensor(out=ahead[:, :, :], in0=blocks[:, :].unsqueeze(1).broadcast_to([P, E, E]), scalar=1.0,
                                                   in1=tie[:, :].rearrange("p (a b) -> p a b", a=E),
                                                   op0=ALU.add, op1=ALU.mult).then_inc(route, 1)
                    dve.wait_ge(route, 9)
                    nc.vector.tensor_reduce(first[:, :], ahead[:, :, :], AX.X, ALU.add).then_inc(route, 1)
                    dve.wait_ge(route, 10)
                    nc.vector.scalar_tensor_tensor(out=place[:, :, :], in0=first[:, :].unsqueeze(1).broadcast_to([P, T, E]), scalar=float(P),
                                                   in1=counts[:, 0:T * E].rearrange("p (t e) -> p t e", t=T),
                                                   op0=ALU.mult, op1=ALU.add).then_inc(route, 1)
                    dve.wait_ge(route, 11)
                    nc.vector.tensor_tensor(pick[:, :, :, :], pick[:, :, :, :], place[:, :, :].unsqueeze(2).broadcast_to([P, T, TOPK, E]),
                                            ALU.mult).then_inc(route, 1)
                    dve.wait_ge(route, 12)
                    nc.vector.tensor_reduce(slot[:, :, :], pick[:, :, :, :], AX.X, ALU.add).then_inc(route, 1)
                    dve.wait_ge(route, 13)
                    nc.vector.tensor_copy(slot_i[:, :, :], slot[:, :, :]).then_inc(route, 1)
                    dve.wait_ge(route, 14)
                    nc.vector.tensor_scalar(block_i[:, :, :], slot_i[:, :, :], P.bit_length() - 1, None,
                                            ALU.logical_shift_right).then_inc(route, 1)
                    dve.wait_ge(route, 15)
                    nc.vector.tensor_copy(block_f[:, :, :], block_i[:, :, :]).then_inc(route, 1)
                    dve.wait_ge(route, 16)
                    nc.vector.scalar_tensor_tensor(out=within[:, :, :], in0=block_f[:, :, :], scalar=-float(P), in1=slot[:, :, :],
                                                   op0=ALU.mult, op1=ALU.add).then_inc(route, 1)
                    nc.vector.tensor_tensor(in_block[:, :, :, :], block_f[:, :, :].unsqueeze(3).broadcast_to([P, T, TOPK, NB]),
                                            row[:, 0:NB].unsqueeze(1).unsqueeze(1).broadcast_to([P, T, TOPK, NB]),
                                            ALU.is_equal).then_inc(route, 1)
                    dve.wait_ge(route, 17)
                    nc.vector.tensor_tensor(at_place[:, :, :, :], within[:, :, :].unsqueeze(3).broadcast_to([P, T, TOPK, P]),
                                            row.unsqueeze(1).unsqueeze(1).broadcast_to([P, T, TOPK, P]),
                                            ALU.is_equal).then_inc(maps_done, 1)
                    dve.wait_ge(route, 18)
                    nc.vector.tensor_scalar(in_block_p[:, :, :, :], in_block[:, :, :, :], index_col[:, 0:1], None, ALU.mult).then_inc(maps_done, 1)
                    nc.vector.tensor_tensor(in_block_t[:, :, :, :], in_block[:, :, :, :],
                                            tile_start.unsqueeze(2).unsqueeze(3).broadcast_to([P, T, TOPK, NB]),
                                            ALU.mult).then_inc(maps_done, 1)

                def tables():
                    nc.vector.tensor_copy(first_of[:, :], first[0:1, :]).then_inc(table_done, 1)
                    nc.vector.tensor_tensor(begun[:, :, :], first[0:1, :].unsqueeze(1).broadcast_to([1, NB, E]),
                                            row[0:1, 0:NB].unsqueeze(2).broadcast_to([1, NB, E]), ALU.is_le).then_inc(route, 1)
                    dve.wait_ge(route, 19)
                    nc.vector.tensor_reduce(expert_f[:, :], begun[:, :, :], AX.X, ALU.add).then_inc(route, 1)
                    nc.vector.tensor_tensor(begun_at[:, :, :], begun[:, :, :], raw_step.unsqueeze(1).broadcast_to([1, NB, E]),
                                            ALU.mult).then_inc(route, 1)
                    dve.wait_ge(route, 20)
                    nc.vector.tensor_copy(expert_of[:, :], expert_f[:, :]).then_inc(table_done, 1)
                    dve.wait_ge(route, 21)
                    nc.vector.tensor_reduce(raw_f[:, :], begun_at[:, :, :], AX.X, ALU.add).then_inc(route, 1)
                    dve.wait_ge(route, 22)
                    nc.vector.tensor_copy(raw_at[:, :], raw_f[:, :]).then_inc(table_done, 1)

                nc.vector.memset(ones[:, :], 1.0).then_inc(ready, 1)
                normalise_vector(m, dve, nm, lambda t: lo_tile(m, dve, nm, turn[t % 2], t))
                dve.wait_ge(const_in, 80)
                nc.vector.tensor_scalar(before[:, :], row, index_col[:, 0:1], None, ALU.is_gt).then_inc(ready, 1)
                for t in range(T + 1):
                    if t >= 1:
                        zt_lo_of(t - 1, (t - 1) % 2)
                    if t < T:
                        z_of(t, t % 2)
                    if t >= 1:
                        add(t - 1, (t - 1) % 2)
                    if t == 2:
                        compare()
                    if t == COUNT_STEP - 1:
                        choose()
                    if t == COUNT_STEP:
                        place_tokens()
                tables()
                dve.wait_ge(mapped, 1)
                nc.vector.tensor_scalar(padding[:, :], logits[0][:, 0:NB], 0.0, index_col[:, 0:1], ALU.is_equal, ALU.mult).then_inc(route, 1)
                dve.wait_ge(route, 23)
                nc.vector.scalar_tensor_tensor(out=token_of[:, :], in0=logits[0][:, 0:NB], scalar=float(S), in1=padding[:, :],
                                               op0=ALU.add, op1=ALU.add).then_inc(route, 1)

        routed_blocks(m, name, sb, sem, xn_rows, acc_rows, raw, raw_in, load_raw, w_hi, w_lo, gu_w, down_w,
                      silu, z, zt_hi, zt_lo, token_of, expert_of, raw_at, first_of)


def routed_blocks(m, name, sb, sem, xn_rows, acc_rows, raw, raw_in, load_raw, w_hi, w_lo, gu_w, down_w,
                  silu, z, zt_hi, zt_lo, token_of, expert_of, raw_at, first_of):
    nc = m.nc
    with ExitStack() as ctx:
        def sb(what, shape, dt=F32):
            return ctx.enter_context(nc.sbuf_tensor(f"{name}_{what}", shape, dt))

        def pb(what, shape, dt=F32):
            return ctx.enter_context(nc.psum_tensor(f"{name}_{what}", shape, dt))

        rows = [sb(f"rows{s}", [P, ROW]) for s in range(RING)]
        out_rows = [sb(f"out_rows{s}", [P, H]) for s in range(2)]
        from_row = [sb(f"from_row{s}", [P, 1], I32) for s in range(RING)]
        to_row = sb("to_row", [P, 1], I32)
        gu = [pb(f"gu_{s}", [P, CH]) for s in range(2)]
        y = [pb(f"y_{s}", [P, CH]) for s in range(2)]
        tx = [pb(f"tx{s}", [P, CH]) for s in range(2)]
        tz = [pb(f"tz{s}", [P, CH]) for s in range(2)]

        raw_ready, act_go, pool_go = sem("raw_ready"), sem("act_go"), sem("pool_go")
        hi_gu, hi_down, lo_gu, lo_gu_pool, lo_down = sem("hi_gu"), sem("hi_down"), sem("lo_gu"), sem("lo_gu_pool"), sem("lo_down")
        from_ready, to_ready = sem("from_ready"), sem("to_ready")
        gathered = [m.gpsimd_dma_semaphore(f"gathered{s}", NB // RING * 16) for s in range(RING)]
        gathered, gathered_start = [g for g, _ in gathered], gathered[0][1]
        scattered, scattered_start = m.gpsimd_dma_semaphore("scattered", NB * 16)
        tx_done, tx_hi, tx_lo = sem("tx_done"), sem("tx_hi"), sem("tx_lo")
        gu_done, silu_done, z_done = sem("b_gu_done"), sem("b_silu_done"), sem("b_z_done")
        tz_done, tz_hi, tz_lo = sem("tz_done"), sem("tz_hi"), sem("tz_lo")
        y_done, y_out, x_in = sem("b_y_done"), sem("y_out"), sem("x_in")

        def there(b):
            return not isinstance(b, int) or 0 <= b < NB

        def run(eng, step):
            for b in range(-3, 2 * RING):
                step(b, b)
            with eng.Fori(2, NB // RING - 1) as i:
                for c in range(RING):
                    step(i * RING + c, c)
            for b in range(NB - RING, NB + 3):
                step(b, b)

        def xt(half, s, k):
            return half[:, k, s * P:(s + 1) * P]

        block = ctx.enter_context(nc.Block())

        @block.sync
        def _(sp):
            def announce(slot, loads):
                sp.wait_ge(raw_in[slot], loads)
                sp.sem_inc(raw_ready, 1)

            def refill(e, slot, loads):
                end = sp.value_load(first_of[0:1, bass.ds(e - RAW + 1, 1)], min_val=0, max_val=NB)
                sp.wait_ge(lo_down, end)
                sp.wait_ge(lo_gu_pool, end)
                load_raw(sp, slot, e + 1)
                announce(slot, loads)

            for e in range(RAW):
                announce(e, 64 if e == RAW - 1 else 32)
            with sp.Fori(1, E // RAW) as i:
                for s in range(RAW):
                    refill(i * RAW + s, s, i * 32 + (64 if s == RAW - 1 else 32))
            for e in range(E // RAW * RAW, E):
                refill(e, e % RAW, 32 * (e // RAW + 1))
            sp.wait_ge(scattered, 16 * NB + scattered_start)
            sp.dma_start(m.x[:, :, :], acc_rows[0:S, :].rearrange("(t p) h -> p t h", p=P)).then_inc(x_in, 16)
            sp.wait_ge(x_in, 16)

        @block.gpsimd
        def _(pool):
            def step(b, c):
                if there(b + 1):
                    at = pool.value_load(raw_at[0:1, bass.ds(b + 1, 1)], min_val=0, max_val=(RAW - 1) * W_COLS)
                if there(b + 3):
                    if some(b):
                        pool.wait_ge(z_done, b)
                    pool.sem_inc(pool_go, 1)
                    s = (c + 3) % RING
                    nc.gpsimd.tensor_copy(from_row[s][:, :], token_of[:, bass.ds(b + 3, 1)]).then_inc(from_ready, 1)
                    pool.wait_ge(from_ready, b + 4)
                    pool.sem_inc(pool_go, 1)
                    pool.indirect_dma_start(rows[s][:, :], None, xn_rows, bass.IndirectOffsetOnAxis(
                        ap=from_row[s][:, :].bitcast(U32), axis=0)).then_inc(gathered[s], 16)
                if there(b - 3):
                    if some(b - 3):
                        pool.wait_ge(scattered, (b - 3) * 16 + scattered_start)
                    pool.sem_inc(pool_go, 1)
                    nc.gpsimd.tensor_copy(to_row[:, :], token_of[:, bass.ds(b - 3, 1)]).then_inc(to_ready, 1)
                    pool.wait_ge(to_ready, b - 2)
                    pool.wait_ge(y_out, b - 2)
                    pool.sem_inc(pool_go, 1)
                    pool.indirect_dma_start(acc_rows, bass.IndirectOffsetOnAxis(ap=to_row[:, :].bitcast(U32), axis=0),
                                            out_rows[(c - 3) % 2][:, :], None, compute_op=ALU.add).then_inc(scattered, 16)
                if there(b + 1):
                    pool.wait_ge(hi_gu, b + 2)
                    pool.sem_inc(pool_go, 1)
                    s = (c + 1) % 2
                    nc.gpsimd.tensor_tensor(w_lo[s][:, DVE_COLS:GU_COLS], raw[:, bass.ds(at + DVE_COLS, GU_COLS - DVE_COLS)],
                                            w_hi[s][:, DVE_COLS:GU_COLS].bitcast(F32), ALU.subtract).then_inc(lo_gu_pool, 1)

            run(pool, step)

        @block.tensor
        def _(pe):
            def step(b, c):
                s = c % 2
                if there(b):
                    pe.wait_ge(tx_lo, b + 1)
                    pe.wait_ge(lo_gu, b + 1)
                    pe.wait_ge(lo_gu_pool, b + 1)
                    if some(b - 1):
                        pe.wait_ge(z_done, b - 1)
                    product(nc, gu[s][:, :], [(xt(m.xt_hi, s, k), xt(m.xt_lo, s, k), gu_w(w_hi[s], k), gu_w(w_lo[s], k))
                                              for k in range(KT)]).then_inc(gu_done, 1)
                if there(b + 2):
                    r = (c + 2) % RING
                    pe.wait_ge(gathered[r], gather_count(b, c))
                    if some(b + 1):
                        pe.wait_ge(tx_lo, b + 1)
                    for k in range(KT):
                        last = nc.tensor.transpose(tx[s][:, k * P:(k + 1) * P], rows[r][:, k * P:(k + 1) * P], m.ident[:, :])
                    last.then_inc(tx_done, 1)
                if there(b - 1):
                    pe.wait_ge(z_done, b)
                    if some(b - 2):
                        pe.wait_ge(tz_lo, b - 2)
                    for j in range(IT):
                        last = nc.tensor.transpose(tz[1 - s][:, j * P:(j + 1) * P], z[1 - s][:, j * P:(j + 1) * P], m.ident[:, :])
                    last.then_inc(tz_done, 1)
                if there(b - 2):
                    pe.wait_ge(tz_lo, b - 1)
                    pe.wait_ge(lo_down, b - 1)
                    if some(b - 3):
                        pe.wait_ge(y_out, b - 3)
                    product(nc, y[s][:, :], [(zt_hi[s][:, j * P:(j + 1) * P], zt_lo[s][:, j * P:(j + 1) * P],
                                              down_w(w_hi[s], j), down_w(w_lo[s], j)) for j in range(IT)]).then_inc(y_done, 1)

            def gather_count(b, c):
                return (b + 2 - (c + 2) % RING) * (16 // RING) + (16 + gathered_start)

            run(pe, step)

        @block.scalar
        def _(act):
            def step(b, c):
                s = c % 2
                if there(b + 1):
                    expert = act.value_load(expert_of[0:1, bass.ds(b + 1, 1)], min_val=1, max_val=E)
                    at = act.value_load(raw_at[0:1, bass.ds(b + 1, 1)], min_val=0, max_val=(RAW - 1) * W_COLS)
                if there(b - 1):
                    at_down = act.value_load(raw_at[0:1, bass.ds(b - 1, 1)], min_val=0, max_val=(RAW - 1) * W_COLS)
                if there(b + 1):
                    act.wait_ge(raw_ready, expert)
                    if some(b):
                        act.wait_ge(gu_done, b)
                    act.sem_inc(act_go, 1)
                    nc.scalar.copy(w_hi[1 - s][:, 0:GU_COLS], raw[:, bass.ds(at, GU_COLS)]).then_inc(hi_gu, 1)
                if there(b - 1):
                    if some(b - 2):
                        act.wait_ge(y_done, b - 2)
                    act.sem_inc(act_go, 1)
                    nc.scalar.copy(w_hi[1 - s][:, GU_COLS:W_COLS], raw[:, bass.ds(at_down + GU_COLS, W_COLS - GU_COLS)]).then_inc(hi_down, 1)
                if there(b):
                    act.wait_ge(gu_done, b + 1)
                    if some(b - 1):
                        act.wait_ge(z_done, b - 1)
                    nc.scalar.activation(silu[s][:, :], gu[s][:, 0:FI], ACT.Silu).then_inc(silu_done, 1)
                if there(b + 2):
                    act.wait_ge(tx_done, b + 3)
                    if some(b + 1):
                        act.wait_ge(gu_done, b + 1)
                    nc.scalar.copy(m.xt_hi[:, :, s * P:(s + 1) * P], tx[s][:, :].rearrange("p (k c) -> p k c", k=KT)).then_inc(tx_hi, 1)
                if there(b - 1):
                    act.wait_ge(tz_done, b)
                    if some(b - 2):
                        act.wait_ge(y_done, b - 2)
                    nc.scalar.copy(zt_hi[1 - s][:, :], tz[1 - s][:, 0:FI]).then_inc(tz_hi, 1)

            run(act, step)

        @block.vector
        def _(dve):
            def step(b, c):
                s = c % 2
                if there(b):
                    column = dve.value_load(expert_of[0:1, bass.ds(b, 1)], min_val=1, max_val=E)
                if there(b + 1):
                    at = dve.value_load(raw_at[0:1, bass.ds(b + 1, 1)], min_val=0, max_val=(RAW - 1) * W_COLS)
                if there(b - 1):
                    at_down = dve.value_load(raw_at[0:1, bass.ds(b - 1, 1)], min_val=0, max_val=(RAW - 1) * W_COLS)
                if there(b - 3):
                    dve.wait_ge(y_done, b - 2)
                    if some(b - 4):
                        dve.wait_ge(scattered, (b - 4) * 16 + scattered_start)
                    nc.vector.tensor_copy(out_rows[1 - s][:, :], y[1 - s][:, :]).then_inc(y_out, 1)
                if there(b + 1):
                    dve.wait_ge(hi_gu, b + 2)
                    nc.vector.tensor_tensor(w_lo[1 - s][:, 0:DVE_COLS], raw[:, bass.ds(at, DVE_COLS)],
                                            w_hi[1 - s][:, 0:DVE_COLS].bitcast(F32), ALU.subtract).then_inc(lo_gu, 1)
                if there(b - 1):
                    dve.wait_ge(hi_down, b)
                    nc.vector.tensor_tensor(w_lo[1 - s][:, GU_COLS:W_COLS], raw[:, bass.ds(at_down + GU_COLS, W_COLS - GU_COLS)],
                                            w_hi[1 - s][:, GU_COLS:W_COLS].bitcast(F32), ALU.subtract).then_inc(lo_down, 1)
                if there(b):
                    dve.wait_ge(silu_done, b + 1)
                    if some(b - 1):
                        dve.wait_ge(tz_done, b - 1)
                    nc.vector.scalar_tensor_tensor(out=z[s][:, :], in0=silu[s][:, :], scalar=rows[c % RING][:, bass.ds(column + (H - 1), 1)],
                                                   in1=gu[s][:, FI:2 * FI], op0=ALU.mult, op1=ALU.mult).then_inc(z_done, 1)
                if there(b + 2):
                    dve.wait_ge(tx_hi, b + 3)
                    nc.vector.tensor_tensor(m.xt_lo[:, :, s * P:(s + 1) * P], tx[s][:, :].rearrange("p (k c) -> p k c", k=KT),
                                            m.xt_hi[:, :, s * P:(s + 1) * P].bitcast(F32), ALU.subtract).then_inc(tx_lo, 1)
                if there(b - 1):
                    dve.wait_ge(tz_hi, b)
                    nc.vector.tensor_tensor(zt_lo[1 - s][:, :], tz[1 - s][:, 0:FI], zt_hi[1 - s][:, :].bitcast(F32),
                                            ALU.subtract).then_inc(tz_lo, 1)

            run(dve, step)


def butterfly_layer(m, name):
    nc = m.nc
    HEADS, DH, M = 16, 32, 128
    QH = P // DH
    TC = CH // P
    with ExitStack() as ctx:
        def sb(what, shape, dt=F32):
            return ctx.enter_context(nc.sbuf_tensor(f"{name}_{what}", shape, dt))

        def pb(what, shape, dt=F32):
            return ctx.enter_context(nc.psum_tensor(f"{name}_{what}", shape, dt))

        def sem(what):
            return m.semaphore(f"{name}_{what}")

        perm_row_i = sb("perm_row_i", [P, H], I32)
        perm_row = sb("perm_row", [P, H])
        perm_col_i = sb("perm_col_i", [P, KT], I32)
        perm_col = sb("perm_col", [P, KT])
        index_row = sb("index_row", [P, H])
        index_col = sb("index_col", [P, KT])
        gather = sb("gather", [P, KT, H], F32R)
        spread = sb("spread", [P, KT, H], F32R)
        up = sb("up", [P, KT, M])
        down = sb("down", [P, HEADS, DH])
        t_in = sb("t_in", [P, KT, S])
        hid = [sb(f"hid{s}", [P, QH, CH]) for s in range(2)]
        d_hi = sb("d_hi", [P, KT, S], F32R)
        d_lo = sb("d_lo", [P, KT, S], F32R)
        ups = [pb(f"ups{s}", [P, 2, CH]) for s in range(2)]
        io = [pb(f"io{s}", [P, CH]) for s in range(2)]
        dn = [pb(f"dn{s}", [P, CH]) for s in range(2)]

        nm = NormSems(sem)
        perm_in, w_in, perm_f, maps = sem("perm_in"), sem("w_in"), sem("perm_f"), sem("maps")
        io_done, io_read = sem("io_done"), sem("io_read")
        up_done, gelu_done, dn_done, d_hi_done, d_lo_done = (
            sem("up_done"), sem("gelu_done"), sem("dn_done"), sem("d_hi_done"), sem("d_lo_done"))

        UNITS = NCH * KT

        def around(u):
            return KT + u - 1 if 1 <= u <= 2 * KT else None

        block = ctx.enter_context(nc.Block())

        @block.sync
        def _(sp):
            sp.dma_start(perm_row_i[:, :], m.dram["perm"].rearrange("(a h) -> a h", a=1).broadcast_to([P, H])).then_inc(perm_in, 16)
            sp.dma_start(perm_col_i[:, :], m.dram["perm_col"]).then_inc(perm_in, 16)
            sp.dma_start(index_row[:, :], m.dram["index_row"].rearrange("(a h) -> a h", a=1).broadcast_to([P, H])).then_inc(perm_in, 16)
            sp.dma_start(index_col[:, :], m.dram["index_col"]).then_inc(perm_in, 16)
            sp.dma_start(up[:, :, :], m.dram["up"]).then_inc(w_in, 16)
            sp.dma_start(down[:, :, :], m.dram["down"]).then_inc(w_in, 16)

        @block.gpsimd
        def _(pool):
            rstd_gpsimd(m, pool, nm)

        @block.tensor
        def _(pe):
            def columns(n):
                c, j = divmod(n, KT)
                if n >= 2:
                    pe.wait_ge(io_read, n - 1)
                for k in range(KT):
                    for half in (m.xt_hi, m.xt_lo):
                        last = nc.tensor.matmul(io[n % 2][:, :], gather[:, k, j * P:(j + 1) * P],
                                                half[:, k, c * CH:(c + 1) * CH],
                                                start=(k == 0 and half is m.xt_hi), stop=(k == KT - 1 and half is m.xt_lo))
                last.then_inc(io_done, 1)

            def outputs(n):
                t = n - UNITS
                pe.wait_ge(io_read, n - 1)
                pe.wait_ge(d_lo_done, (t // TC + 1) * KT)
                for k in range(KT):
                    for half in (d_hi, d_lo):
                        last = nc.tensor.matmul(io[n % 2][:, :], half[:, k, t * P:(t + 1) * P], spread[:, k, :],
                                                start=(k == 0 and half is d_hi), stop=(k == KT - 1 and half is d_lo))
                last.then_inc(io_done, 1)

            for t in range(T):
                transpose_tile(m, pe, nm, dn[t % 2], t)
            pe.wait_ge(nm.xt_lo, T)
            pe.wait_ge(maps, 2)
            pe.wait_ge(w_in, 32)
            for n in range(KT):
                columns(n)
            for u in range(UNITS + 1):
                n = around(u)
                if n is not None:
                    columns(n) if n < UNITS else outputs(n)
                if u < UNITS:
                    c, j = divmod(u, KT)
                    pe.wait_ge(io_read, u + 1)
                    for r in range(QH):
                        if u >= 1 and r % 2 == 0:
                            pe.wait_ge(gelu_done, 2 * u - 1 + r // 2)
                        rows = slice(DH * r, DH * (r + 1))
                        last = nc.tensor.matmul(ups[r // 2][:, r % 2, :], up[rows, j, :], t_in[rows, j, c * CH:(c + 1) * CH],
                                                start=True, stop=True)
                        if r % 2:
                            last.then_inc(up_done, 1)
                if u >= 1:
                    v = u - 1
                    pe.wait_ge(gelu_done, 2 * v + 2)
                    if v >= 2:
                        pe.wait_ge(d_lo_done, v - 1)
                    for r in range(QH):
                        last = nc.tensor.matmul(dn[v % 2][DH * r:DH * (r + 1), :], down[:, QH * (v % KT) + r, :],
                                                hid[v % 2][:, r, :], start=True, stop=True)
                    last.then_inc(dn_done, 1)
            for n in range(UNITS + TC, UNITS + T):
                outputs(n)

        @block.scalar
        def _(act):
            for t in range(T):
                hi_tile(m, act, nm, dn[t % 2], t)
            for u in range(UNITS + 1):
                if u < UNITS:
                    for a in range(2):
                        act.wait_ge(up_done, 2 * u + a + 1)
                        if u >= 2:
                            act.wait_ge(dn_done, u - 1)
                        nc.scalar.activation(hid[u % 2][:, 2 * a:2 * a + 2, :], ups[a][:, :, :], ACT.Gelu).then_inc(gelu_done, 1)
                if u >= 1:
                    c, j = divmod(u - 1, KT)
                    act.wait_ge(dn_done, u)
                    nc.scalar.copy(d_hi[:, j, c * CH:(c + 1) * CH], dn[(u - 1) % 2][:, :]).then_inc(d_hi_done, 1)

        @block.vector
        def _(dve):
            def read(n):
                dve.wait_ge(io_done, n + 1)
                if n < UNITS:
                    c, j = divmod(n, KT)
                    nc.vector.tensor_copy(t_in[:, j, c * CH:(c + 1) * CH], io[n % 2][:, :]).then_inc(io_read, 1)
                else:
                    t = n - UNITS
                    nc.vector.scalar_tensor_tensor(out=m.x[:, t, :], in0=io[n % 2][:, :], scalar=0.5, in1=m.x[:, t, :],
                                                   op0=ALU.mult, op1=ALU.add).then_inc(io_read, 1)

            dve.wait_ge(perm_in, 64)
            nc.vector.tensor_copy(perm_row[:, :], perm_row_i[:, :]).then_inc(perm_f, 1)
            nc.vector.tensor_copy(perm_col[:, :], perm_col_i[:, :]).then_inc(perm_f, 1)
            dve.wait_ge(perm_f, 2)
            for k in range(KT):
                g = nc.vector.tensor_scalar(gather[:, k, :], perm_row[:, :], index_col[:, k:k + 1], None, ALU.is_equal)
                s = nc.vector.tensor_scalar(spread[:, k, :], index_row[:, :], perm_col[:, k:k + 1], None, ALU.is_equal)
            g.then_inc(maps, 1)
            s.then_inc(maps, 1)
            normalise_vector(m, dve, nm, lambda t: lo_tile(m, dve, nm, dn[t % 2], t))
            for n in range(KT):
                read(n)
            for u in range(UNITS + 1):
                n = around(u)
                if n is not None:
                    read(n)
                if u >= 1:
                    c, j = divmod(u - 1, KT)
                    dve.wait_ge(d_hi_done, u)
                    nc.vector.tensor_tensor(d_lo[:, j, c * CH:(c + 1) * CH], dn[(u - 1) % 2][:, :],
                                            d_hi[:, j, c * CH:(c + 1) * CH].bitcast(F32), ALU.subtract).then_inc(d_lo_done, 1)
            for n in range(UNITS + TC, UNITS + T):
                read(n)


def full_attention_layer(m, name):
    nc = m.nc
    D = H // 4
    SCALE = float(D) ** -0.5
    with ExitStack() as ctx:
        def sb(what, shape, dt=F32):
            return ctx.enter_context(nc.sbuf_tensor(f"{name}_{what}", shape, dt))

        def pb(what, shape, dt=F32):
            return ctx.enter_context(nc.psum_tensor(f"{name}_{what}", shape, dt))

        def sem(what):
            return m.semaphore(f"{name}_{what}")

        w_raw = sb("w_raw", [P, KT, 3 * D])
        w_hi = sb("w_hi", [P, KT, 3 * D], F32R)
        w_lo = sb("w_lo", [P, KT, 3 * D], F32R)
        wo_raw = sb("wo_raw", [P, H])
        wo_hi = sb("wo_hi", [P, H], F32R)
        wo_lo = sb("wo_lo", [P, H], F32R)
        b_qkv = sb("b_qkv", [P, 3])
        b_out = sb("b_out", [P, H])
        qk_hi = [sb(f"{a}_hi", [P, S], F32R) for a in "qk"]
        qk_lo = [sb(f"{a}_lo", [P, S], F32R) for a in "qk"]
        vt = sb("vt", [P, S])
        v_hi = sb("v_hi", [P, S], F32R)
        v_lo = sb("v_lo", [P, S], F32R)
        top = sb("top", [P, T])
        bias = sb("bias", [P, T])
        total = sb("total", [P, T])
        inv_total = sb("inv_total", [P, T])
        prob = [sb(f"prob{s}", [P, S]) for s in range(2)]
        pt_hi = sb("pt_hi", [P, T, S], F32R)
        pt_lo = sb("pt_lo", [P, T, S], F32R)
        o_hi = sb("o_hi", [P, S], F32R)
        o_lo = sb("o_lo", [P, S], F32R)

        sc = [pb(f"sc{s}", [P, S]) for s in range(2)]
        pt = pb("pt", [P, S])
        pj = [pb(f"pj{s}", [P, CH]) for s in range(2)]

        nm = NormSems(sem)
        w_in, b_in, w_half, w_ready, x_biased = sem("w_in"), sem("b_in"), sem("w_half"), sem("w_ready"), sem("x_biased")
        pj_done, qk_hi_done, qk_read, vt_read = sem("pj_done"), sem("qk_hi_done"), sem("qk_read"), sem("vt_read")
        o_hi_done, o_read, x_done = sem("o_hi_done"), sem("o_read"), sem("x_done")
        vt_done, v_hi_done, v_lo_done = sem("vt_done"), sem("v_hi_done"), sem("v_lo_done")
        sc_done, top_done, bias_done, prob_done = sem("sc_done"), sem("top_done"), sem("bias_done"), sem("prob_done")
        pt_done, pt_hi_done, pt_lo_done = sem("pt_done"), sem("pt_hi_done"), sem("pt_lo_done")
        inv_done = sem("inv_done")
        PROJ = 3 * NCH

        block = ctx.enter_context(nc.Block())

        @block.sync
        def _(sp):
            sp.dma_start(w_raw[:, :, :], m.dram["w1_qkv"]).then_inc(w_in, 16)
            sp.dma_start(wo_raw[:, :], m.dram["w1_out"]).then_inc(w_in, 16)
            sp.dma_start(b_qkv[:, :], m.dram["b1_qkv"]).then_inc(b_in, 16)
            sp.dma_start(b_out[:, :], m.dram["b1_out"].rearrange("(a h) -> a h", a=1).broadcast_to([P, H])).then_inc(b_in, 16)

        @block.gpsimd
        def _(pool):
            pool.wait_ge(w_in, 32)
            nc.gpsimd.tensor_copy(w_hi[:, :, :], w_raw[:, :, :]).then_inc(w_half, 1)
            nc.gpsimd.tensor_copy(wo_hi[:, :], wo_raw[:, :]).then_inc(w_half, 1)
            rstd_gpsimd(m, pool, nm)
            pool.wait_ge(w_half, 2)
            nc.gpsimd.tensor_tensor(w_lo[:, :, :], w_raw[:, :, :], w_hi[:, :, :].bitcast(F32), ALU.subtract).then_inc(w_ready, 1)
            nc.gpsimd.tensor_tensor(wo_lo[:, :], wo_raw[:, :], wo_hi[:, :].bitcast(F32), ALU.subtract).then_inc(w_ready, 1)
            pool.wait_ge(b_in, 32)
            pool.wait_ge(nm.xn, T)
            nc.gpsimd.tensor_tensor(m.x[:, :, :], m.x[:, :, :], b_out[:, :].unsqueeze(1).broadcast_to([P, T, H]),
                                    ALU.add).then_inc(x_biased, 1)

        @block.tensor
        def _(pe):
            for t in range(T):
                transpose_tile(m, pe, nm, sc[t % 2][:, 0:CH], t)
            pe.wait_ge(nm.xt_lo, T)
            pe.wait_ge(w_ready, 2)
            for u in range(PROJ):
                a, c = divmod(u, NCH)
                if u >= 2:
                    pe.wait_ge(qk_read, u - 1)
                cols = slice(c * CH, (c + 1) * CH)
                product(nc, pj[u % 2][:, :], [(w_hi[:, k, a * D:(a + 1) * D], w_lo[:, k, a * D:(a + 1) * D],
                                               m.xt_hi[:, k, cols], m.xt_lo[:, k, cols]) for k in range(KT)]).then_inc(pj_done, 1)

            def scores(t):
                if t >= 2:
                    pe.wait_ge(prob_done, t - 1)
                rows = slice(t * P, (t + 1) * P)
                for c in range(NCH):
                    cols = slice(c * CH, (c + 1) * CH)
                    last = product(nc, sc[t % 2][:, cols], [(qk_hi[0][:, rows], qk_lo[0][:, rows],
                                                             qk_hi[1][:, cols], qk_lo[1][:, cols])])
                last.then_inc(sc_done, 1)

            def turn_prob(t):
                pe.wait_ge(prob_done, t + 1)
                if t >= 1:
                    pe.wait_ge(pt_lo_done, t)
                for k in range(T):
                    last = nc.tensor.transpose(pt[:, k * P:(k + 1) * P], prob[t % 2][:, k * P:(k + 1) * P], m.ident[:, :])
                last.then_inc(pt_done, 1)

            pe.wait_ge(qk_read, 2 * NCH)
            scores(0)
            pe.wait_ge(vt_read, NCH)
            for t in range(T):
                last = nc.tensor.transpose(pt[:, t * P:(t + 1) * P], vt[:, t * P:(t + 1) * P], m.ident[:, :])
            last.then_inc(vt_done, 1)
            for t in range(1, T):
                scores(t)
                if t == 1:
                    pe.wait_ge(v_lo_done, 1)
                turn_prob(t - 1)
            turn_prob(T - 1)
            for c in range(NCH):
                pe.wait_ge(pt_lo_done, (c + 1) * (CH // P))
                cols = slice(c * CH, (c + 1) * CH)
                product(nc, pj[c][:, :], [(v_hi[:, k * D:(k + 1) * D], v_lo[:, k * D:(k + 1) * D],
                                           pt_hi[:, k, cols], pt_lo[:, k, cols]) for k in range(T)]).then_inc(pj_done, 1)
            for t in range(T):
                if t == 0:
                    pe.wait_ge(o_read, NCH)
                if t >= 2:
                    pe.wait_ge(x_done, t - 1)
                rows = slice(t * P, (t + 1) * P)
                product(nc, pj[t % 2][:, :], [(o_hi[:, rows], o_lo[:, rows], wo_hi[:, :], wo_lo[:, :])]).then_inc(pj_done, 1)

        @block.scalar
        def _(act):
            for t in range(T):
                hi_tile(m, act, nm, sc[t % 2][:, 0:CH], t)
            act.wait_ge(b_in, 32)
            for u in range(PROJ):
                a, c = divmod(u, NCH)
                act.wait_ge(pj_done, u + 1)
                cols = slice(c * CH, (c + 1) * CH)
                if a < 2:
                    nc.scalar.activation(qk_hi[a][:, cols], pj[u % 2][:, :], ACT.Identity, bias=b_qkv[:, a:a + 1]).then_inc(qk_hi_done, 1)
                else:
                    nc.scalar.activation(vt[:, cols], pj[u % 2][:, :], ACT.Identity, bias=b_qkv[:, a:a + 1]).then_inc(vt_read, 1)

            def probabilities(t):
                act.wait_ge(bias_done, t + 1)
                if t >= 2:
                    act.wait_ge(pt_done, t - 1)
                nc.scalar.activation(prob[t % 2][:, :], sc[t % 2][:, :], ACT.Exp, bias=bias[:, t:t + 1], scale=SCALE,
                                     accum_out=total[:, t:t + 1]).then_inc(prob_done, 1)

            def upper(t):
                act.wait_ge(pt_done, t + 1)
                nc.scalar.copy(pt_hi[:, :, t * P:(t + 1) * P], pt[:, :].rearrange("p (k c) -> p k c", k=T)).then_inc(pt_hi_done, 1)

            act.wait_ge(vt_done, 1)
            nc.scalar.copy(v_hi[:, :], pt[:, :]).then_inc(v_hi_done, 1)
            probabilities(0)
            for t in range(1, T):
                probabilities(t)
                upper(t - 1)
            upper(T - 1)
            for c in range(NCH):
                act.wait_ge(pj_done, PROJ + c + 1)
                nc.scalar.copy(o_hi[:, c * CH:(c + 1) * CH], pj[c][:, :]).then_inc(o_hi_done, 1)

        @block.vector
        def _(dve):
            normalise_vector(m, dve, nm, lambda t: lo_tile(m, dve, nm, sc[t % 2][:, 0:CH], t))
            for u in range(2 * NCH):
                a, c = divmod(u, NCH)
                dve.wait_ge(qk_hi_done, u + 1)
                cols = slice(c * CH, (c + 1) * CH)
                nc.vector.scalar_tensor_tensor(out=qk_lo[a][:, cols], in0=pj[u % 2][:, :], scalar=b_qkv[:, a:a + 1],
                                               in1=qk_hi[a][:, cols].bitcast(F32), op0=ALU.add, op1=ALU.subtract).then_inc(qk_read, 1)

            def maximum(t):
                dve.wait_ge(sc_done, t + 1)
                nc.vector.tensor_reduce(top[:, t:t + 1], sc[t % 2][:, :], AX.X, ALU.max).then_inc(top_done, 1)
                dve.wait_ge(top_done, t + 1)
                nc.vector.tensor_scalar(bias[:, t:t + 1], top[:, t:t + 1], -SCALE, None, ALU.mult).then_inc(bias_done, 1)

            def lower(t):
                dve.wait_ge(pt_hi_done, t + 1)
                cols = slice(t * P, (t + 1) * P)
                nc.vector.tensor_tensor(pt_lo[:, :, cols], pt[:, :].rearrange("p (k c) -> p k c", k=T),
                                        pt_hi[:, :, cols].bitcast(F32), ALU.subtract).then_inc(pt_lo_done, 1)

            maximum(0)
            dve.wait_ge(v_hi_done, 1)
            nc.vector.tensor_tensor(v_lo[:, :], pt[:, :], v_hi[:, :].bitcast(F32), ALU.subtract).then_inc(v_lo_done, 1)
            for t in range(1, T):
                maximum(t)
                lower(t - 1)
            lower(T - 1)
            dve.wait_ge(prob_done, T)
            nc.vector.reciprocal(inv_total[:, :], total[:, :]).then_inc(inv_done, 1)
            for c in range(NCH):
                dve.wait_ge(o_hi_done, c + 1)
                cols = slice(c * CH, (c + 1) * CH)
                nc.vector.tensor_tensor(o_lo[:, cols], pj[c][:, :], o_hi[:, cols].bitcast(F32), ALU.subtract).then_inc(o_read, 1)
            dve.wait_ge(inv_done, 1)
            dve.wait_ge(x_biased, 1)
            for t in range(T):
                dve.wait_ge(pj_done, PROJ + NCH + t + 1)
                nc.vector.scalar_tensor_tensor(out=m.x[:, t, :], in0=pj[t % 2][:, :], scalar=inv_total[:, t:t + 1],
                                               in1=m.x[:, t, :], op0=ALU.mult, op1=ALU.add).then_inc(x_done, 1)


def causal_attention_layer(m, name):
    nc = m.nc
    HD, KV, QPK = 16, 8, 4
    HEADS = KV * QPK
    SCALE = 1.0 / HD
    QK_ROWS = (KV + HEADS) * HD
    Q_PART = (0, 0, 1, 0, 1, 2)
    K_PART = (0, 1, 0, 2, 1, 0)
    STACK = len(Q_PART) * HD
    MROWS = 3
    with ExitStack() as outer:
        def sem(what):
            return m.semaphore(f"{name}_{what}")

        parts_dram = nc.dram_tensor(f"{name}_parts", [3, QK_ROWS, S], BF16, kind="Internal").ap()
        v_all = outer.enter_context(nc.sbuf_tensor(f"{name}_v_all", [P, T, KV, 2 * HD], F32))
        ks = outer.enter_context(nc.sbuf_tensor(f"{name}_ks", [P, KV * S], BF16))

        with ExitStack() as ctx:
            def sb(what, shape, dt=F32):
                return ctx.enter_context(nc.sbuf_tensor(f"{name}_{what}", shape, dt))

            def pb(what, shape, dt=F32):
                return ctx.enter_context(nc.psum_tensor(f"{name}_{what}", shape, dt))

            WQ = (HEADS + 2 * KV) * HD
            w_raw = sb("w_raw", [P, KT, WQ])
            w_hi = sb("w_hi", [P, KT, WQ], F32R)
            w_lo = sb("w_lo", [P, KT, WQ], F32R)
            b_qkv = sb("b_qkv", [P, WQ // P])
            cos = sb("cos", [P, S])
            sin = sb("sin", [P, S])
            swap_raw = sb("swap_raw", [P, P])
            swap = sb("swap", [P, P], F32R)
            q_hi = [sb(f"q_hi{s}", [P, CH], F32R) for s in range(2)]
            q_lo = [sb(f"q_lo{s}", [P, CH], F32R) for s in range(2)]
            with_cos = [sb(f"with_cos{s}", [P, CH]) for s in range(2)]
            with_sin = [sb(f"with_sin{s}", [P, CH]) for s in range(2)]
            turned = [sb(f"turned{s}", [P, CH]) for s in range(2)]
            rest = [sb(f"rest{s}", [P, CH]) for s in range(2)]
            NPB = 4
            part = [sb(f"part{s}", [P, 3, CH], BF16) for s in range(NPB)]
            vt = sb("vt", [P, S])
            xp = [pb(f"xp{s}", [P, CH]) for s in range(2)]
            pj = [pb(f"pj{s}", [P, CH]) for s in range(2)]
            rot = [pb(f"rot{s}", [P, CH]) for s in range(2)]

            nm = NormSems(sem)
            w_in, c_in, w_half, w_ready, v_init = sem("w_in"), sem("c_in"), sem("w_half"), sem("w_ready"), sem("v_init")
            pj_done, hi_done, lo_done, cos_done, rot_done, sin_done = (
                sem("pj_done"), sem("hi_done"), sem("lo_done"), sem("cos_done"), sem("rot_done"), sem("sin_done"))
            turned_done, p1_done, rest_done, p2_done, p3_done = (
                sem("turned_done"), sem("p1_done"), sem("rest_done"), sem("p2_done"), sem("p3_done"))
            v_read, vt_done, v_done = sem("v_read"), sem("vt_done"), sem("v_done")
            part_out = [sem(f"part_out{s}") for s in range(NPB)]

            UNITS = WQ // P * NCH
            V_UNITS = (NCH, 2 * NCH)
            TURN = [n for n in range(UNITS) if not V_UNITS[0] <= n < V_UNITS[1]]
            number = {n: r for r, n in enumerate(TURN)}

            with nc.Block() as block:
                @block.sync
                def _(sp):
                    sp.dma_start(w_raw[:, :, :], m.dram["w_qkv"]).then_inc(w_in, 16)
                    sp.dma_start(swap_raw[:, :], m.dram["swap"]).then_inc(w_in, 16)
                    sp.dma_start(b_qkv[:, :], m.dram["b_qkv"]).then_inc(c_in, 16)
                    sp.dma_start(cos[:, :], m.dram["cos"]).then_inc(c_in, 16)
                    sp.dma_start(sin[:, :], m.dram["sin"]).then_inc(c_in, 16)
                    for n in TURN:
                        j, c = divmod(n, NCH)
                        r = number[n]
                        row = (j if j == 0 else j - 1) * P
                        sp.wait_ge(p3_done, r + 1)
                        sp.dma_start(parts_dram[:, row:row + P, c * CH:(c + 1) * CH].rearrange("a p s -> p a s"),
                                     part[r % NPB][:, :, :]).then_inc(part_out[r % NPB], 16)
                    for s in range(NPB):
                        sp.wait_ge(part_out[s], 16 * len(range(s, len(TURN), NPB)))

                @block.gpsimd
                def _(pool):
                    nc.gpsimd.memset(v_all[:, :, :, :], 0.0).then_inc(v_init, 1)
                    pool.wait_ge(w_in, 32)
                    nc.gpsimd.tensor_copy(w_hi[:, :, :], w_raw[:, :, :]).then_inc(w_half, 1)
                    nc.gpsimd.tensor_copy(swap[:, :], swap_raw[:, :]).then_inc(w_half, 1)
                    rstd_gpsimd(m, pool, nm)
                    pool.wait_ge(w_half, 2)
                    nc.gpsimd.tensor_tensor(w_lo[:, :, :], w_raw[:, :, :], w_hi[:, :, :].bitcast(F32),
                                            ALU.subtract).then_inc(w_ready, 1)
                    pool.wait_ge(v_init, 1)
                    nc.gpsimd.memset(v_all[:, :, :, HD:HD + 1], 1.0).then_inc(v_init, 1)
                    pool.wait_ge(v_init, 2)
                    nc.gpsimd.memset(ks[STACK:STACK + MROWS, :], 1.0).then_inc(v_init, 1)
                    pool.wait_ge(v_init, 3)
                    for n in range(UNITS + 4):
                        if n - 1 in number:
                            r = number[n - 1]
                            pool.wait_ge(sin_done, r + 1)
                            if r >= 2:
                                pool.wait_ge(rest_done, r - 1)
                            nc.gpsimd.tensor_tensor(turned[r % 2][:, :], with_cos[r % 2][:, :], with_sin[r % 2][:, :],
                                                    ALU.add).then_inc(turned_done, 1)
                        if n - 2 in number:
                            r = number[n - 2]
                            pool.wait_ge(p1_done, r + 1)
                            if r >= 2:
                                pool.wait_ge(p3_done, r - 1)
                            nc.gpsimd.tensor_tensor(rest[r % 2][:, :], turned[r % 2][:, :], part[r % NPB][:, 0, :],
                                                    ALU.subtract).then_inc(rest_done, 1)
                        if n - 3 in number:
                            r = number[n - 3]
                            pool.wait_ge(p2_done, r + 1)
                            nc.gpsimd.tensor_tensor(part[r % NPB][:, 2, :], rest[r % 2][:, :], part[r % NPB][:, 1, :],
                                                    ALU.subtract).then_inc(p3_done, 1)

                @block.tensor
                def _(pe):
                    for t in range(T):
                        transpose_tile(m, pe, nm, xp[t % 2], t)
                    pe.wait_ge(nm.xt_lo, T)
                    pe.wait_ge(w_ready, 1)
                    for n in range(UNITS + 1):
                        if n < UNITS:
                            j, c = divmod(n, NCH)
                            if n - 2 in number:
                                pe.wait_ge(cos_done, number[n - 2] + 1)
                            elif n >= 2:
                                pe.wait_ge(v_read, n - 2 - V_UNITS[0] + 1)
                            cols = slice(c * CH, (c + 1) * CH)
                            feats = slice(j * P, (j + 1) * P)
                            product(nc, pj[n % 2][:, :], [(w_hi[:, k, feats], w_lo[:, k, feats], m.xt_hi[:, k, cols],
                                                           m.xt_lo[:, k, cols]) for k in range(KT)]).then_inc(pj_done, 1)
                        if n - 1 in number:
                            r = number[n - 1]
                            pe.wait_ge(lo_done, r + 1)
                            if r >= 2:
                                pe.wait_ge(sin_done, r - 1)
                            nc.tensor.matmul(rot[r % 2][:, :], swap[:, :], q_hi[r % 2][:, :], start=True, stop=False)
                            nc.tensor.matmul(rot[r % 2][:, :], swap[:, :], q_lo[r % 2][:, :], start=False,
                                             stop=True).then_inc(rot_done, 1)
                        elif n == V_UNITS[1]:
                            pe.wait_ge(v_read, NCH)
                            for t in range(T):
                                last = nc.tensor.transpose(xp[t * P // CH][:, t * P % CH:t * P % CH + P],
                                                           vt[:, t * P:(t + 1) * P], m.ident[:, :])
                            last.then_inc(vt_done, 1)

                @block.scalar
                def _(act):
                    for t in range(T):
                        hi_tile(m, act, nm, xp[t % 2], t)
                    act.wait_ge(c_in, 48)
                    for n in range(UNITS + 4):
                        if n < UNITS:
                            j, c = divmod(n, NCH)
                            act.wait_ge(pj_done, n + 1)
                            if n in number:
                                r = number[n]
                                if r >= 2:
                                    act.wait_ge(rot_done, r - 1)
                                nc.scalar.activation(q_hi[r % 2][:, :], pj[n % 2][:, :], ACT.Identity,
                                                     bias=b_qkv[:, j:j + 1]).then_inc(hi_done, 1)
                            else:
                                nc.scalar.activation(vt[:, c * CH:(c + 1) * CH], pj[n % 2][:, :], ACT.Identity,
                                                     bias=b_qkv[:, j:j + 1]).then_inc(v_read, 1)
                        if n - 2 in number:
                            r = number[n - 2]
                            act.wait_ge(turned_done, r + 1)
                            if r >= NPB:
                                act.wait_ge(part_out[r % NPB], 16 * (r // NPB))
                            nc.scalar.copy(part[r % NPB][:, 0, :], turned[r % 2][:, :]).then_inc(p1_done, 1)
                        if n - 3 in number:
                            r = number[n - 3]
                            act.wait_ge(rest_done, r + 1)
                            nc.scalar.copy(part[r % NPB][:, 1, :], rest[r % 2][:, :]).then_inc(p2_done, 1)

                @block.vector
                def _(dve):
                    normalise_vector(m, dve, nm, lambda t: lo_tile(m, dve, nm, xp[t % 2], t))
                    dve.wait_ge(c_in, 48)
                    for n in range(UNITS + 1):
                        j, c = divmod(n, NCH)
                        cols = slice(c * CH, (c + 1) * CH)
                        if n in number:
                            r = number[n]
                            dve.wait_ge(hi_done, r + 1)
                            nc.vector.scalar_tensor_tensor(out=q_lo[r % 2][:, :], in0=pj[n % 2][:, :], scalar=b_qkv[:, j:j + 1],
                                                           in1=q_hi[r % 2][:, :].bitcast(F32), op0=ALU.add,
                                                           op1=ALU.subtract).then_inc(lo_done, 1)
                            if r >= 2:
                                dve.wait_ge(turned_done, r - 1)
                            nc.vector.scalar_tensor_tensor(out=with_cos[r % 2][:, :], in0=pj[n % 2][:, :],
                                                           scalar=b_qkv[:, j:j + 1], in1=cos[:, cols], op0=ALU.add,
                                                           op1=ALU.mult).then_inc(cos_done, 1)
                        if n - 1 in number:
                            r = number[n - 1]
                            c = (n - 1) % NCH
                            dve.wait_ge(rot_done, r + 1)
                            nc.vector.tensor_tensor(with_sin[r % 2][:, :], rot[r % 2][:, :], sin[:, c * CH:(c + 1) * CH],
                                                    ALU.mult).then_inc(sin_done, 1)
                        if n == V_UNITS[1] + 1:
                            dve.wait_ge(vt_done, 1)
                            dve.wait_ge(v_init, 2)
                            for c in range(NCH):
                                nc.vector.tensor_copy(v_all[:, c * (CH // P):(c + 1) * (CH // P), :, 0:HD],
                                                      xp[c][:, :].rearrange("p (t g d) -> p t g d", t=CH // P, g=KV)).then_inc(v_done, 1)

        with ExitStack() as ctx:
            def sb(what, shape, dt=F32):
                return ctx.enter_context(nc.sbuf_tensor(f"{name}_{what}", shape, dt))

            def pb(what, shape, dt=F32):
                return ctx.enter_context(nc.psum_tensor(f"{name}_{what}", shape, dt))

            QG = QPK * S
            TC = CH // P
            qs = sb("qs", [P, HEADS * S], BF16)
            v_now = sb("v_now", [P, T, 2 * HD])
            masks = sb("masks", [P, 2, P])
            mask_qk = sb("mask_qk", [P, P], BF16)
            mask_kq = sb("mask_kq", [P, P], BF16)
            ident = sb("ident", [P, P], BF16)
            warm = sb("warm", [1, 1])
            top = sb("top", [P, NCH, T, QPK])
            best = sb("best", [P, TC, QPK])
            neg = sb("neg", [P, TC, QPK])
            left = sb("left", [P, TC, QPK])
            neg_parts = [sb(f"neg_parts{h}", [P, TC, MROWS, QPK], BF16) for h in range(NCH)]
            neg_turned = [sb(f"neg_turned{h}", [MROWS * QPK, CH], BF16) for h in range(NCH)]
            prob = [sb(f"prob{s}", [P, QPK, CH]) for s in range(2)]
            out_t = sb("out_t", [P, CH])
            inv = sb("inv", [P, TC, QPK])
            sc = [pb(f"sc{s}", [P, CH]) for s in range(2)]
            mx = [pb(f"mx{s}", [P, 2, CH]) for s in range(2)]
            po = pb("po", [P, CH])
            small = pb("small", [P, 2 * CH], BF16)
            small_f = small[:, :].bitcast(F32)

            c_in2, consts, stack_in = sem("c_in2"), sem("consts"), sem("stack_in")
            mx_done, mx_read, neg_chain, neg_done, neg_turn, neg_read = (
                sem("mx_done"), sem("mx_read"), sem("neg_chain"), sem("neg_done"), sem("neg_turn"), sem("neg_read"))
            neg_in = [m.gpsimd_dma_semaphore(f"neg_in{h}", KV * MROWS * 16)[0] for h in range(NCH)]
            sc_done, exp_done, v_ready, pv_done = sem("sc_done"), sem("exp_done"), sem("v_ready"), sem("pv_done")
            po_read, out_turn, inv_done, ctx_done = sem("po_read"), sem("out_turn"), sem("inv_done"), sem("ctx_done")

            MAX_UNITS = [(t, kc, a) for t in range(T) for kc in range(t * P // CH + 1) for a in range(QPK // 2)]
            NMU = len(MAX_UNITS)
            HALF0 = sum(t < TC for t, _, _ in MAX_UNITS)
            STEPS = [(c, kb) for c in range(NCH) for kb in range((c + 1) * TC)]
            NS = len(STEPS)
            C0 = TC
            NEG_OPS = (4, 5)
            LOADS = 2 * len(Q_PART)

            with nc.Block() as block:
                @block.sync
                def _(sp):
                    sp.dma_start(masks[:, :, :], m.dram["masks"]).then_inc(c_in2, 16)

                    def load(g):
                        for a in range(len(Q_PART)):
                            rows = slice(a * HD, (a + 1) * HD)
                            sp.dma_start(ks[rows, bass.ds(g * S, S)],
                                         parts_dram[K_PART[a], bass.ds(g * HD, HD), :]).then_inc(stack_in, 16)
                            sp.dma_start(qs[rows, bass.ds(g * QG, QG)].rearrange("d (h s) -> d h s", h=QPK),
                                         parts_dram[Q_PART[a], bass.ds(g * (QPK * HD) + KV * HD, QPK * HD), :].rearrange(
                                             "(h d) s -> d h s", h=QPK)).then_inc(stack_in, 16)

                    load(0)
                    with sp.Fori(1, KV) as g:
                        sp.wait_ge(stack_in, g * (16 * LOADS))
                        load(g)

                @block.gpsimd
                def _(pool):
                    def put_maxima(gn, h):
                        pool.wait_ge(neg_read, gn * NCH + h + 1)
                        for a in range(MROWS):
                            pool.dma_start(qs[STACK + a:STACK + a + 1, bass.ds(gn * QG, QG)].rearrange(
                                "a (h s) -> a h s", h=QPK)[:, :, h * CH:(h + 1) * CH],
                                neg_turned[h][a * QPK:(a + 1) * QPK, :]).then_inc(neg_in[h], 16)

                    def values(g):
                        pool.wait_ge(pv_done, g * NS + 1)
                        nc.gpsimd.tensor_copy(v_now[:, :, :], v_all[:, :, bass.ds(g, 1), :].rearrange(
                            "p t a d -> p t (a d)")).then_inc(v_ready, 1)

                    for h in range(NCH):
                        put_maxima(0, h)
                    with pool.Fori(0, KV - 1) as g:
                        values(g)
                        for h in range(NCH):
                            put_maxima(g + 1, h)
                    values(KV - 1)

                @block.tensor
                def _(pe):
                    def maximum(gn, i):
                        t, kc, a = MAX_UNITS[i]
                        mu = gn * NMU + i
                        if i == 0:
                            pe.wait_ge(stack_in, gn * (16 * LOADS) + 16 * LOADS)
                        if not isinstance(mu, int) or mu >= 2:
                            pe.wait_ge(mx_read, mu - 1)
                        w = min(CH, (t + 1) * P - kc * CH)
                        diagonal = t * P < (kc + 1) * CH
                        for b in range(2):
                            at = gn * QG + ((2 * a + b) * S + t * P)
                            last = nc.tensor.matmul(mx[i % 2][:, b, 0:w], qs[0:STACK, bass.ds(at, P)],
                                                    ks[0:STACK, bass.ds(gn * S + kc * CH, w)], start=True, stop=not diagonal)
                            if diagonal:
                                last = nc.tensor.matmul(mx[i % 2][:, b, w - P:w], ident[:, :], mask_qk[:, :], start=False, stop=True)
                        last.then_inc(mx_done, 1)

                    def turn_maxima(gn, h):
                        pe.wait_ge(neg_done, gn * NCH + h + 1)
                        if not isinstance(gn, int) or gn * NCH + h >= 1:
                            pe.wait_ge(neg_read, gn * NCH + h)
                        for u in range(TC):
                            last = nc.tensor.transpose(small[0:MROWS * QPK, u * P:(u + 1) * P],
                                                       neg_parts[h][:, u, :, :].rearrange("p a h -> p (a h)"), ident[:, :])
                        last.then_inc(neg_turn, 1)

                    def scores(g, u, h):
                        c, kb = STEPS[u]
                        pe.wait_ge(exp_done, g * (NS * QPK) + (u * QPK + h + 1))
                        o = max(0, kb * P - c * CH)
                        diagonal = kb * P >= c * CH
                        b = (u * QPK + h) % 2
                        nc_last = nc.tensor.matmul(sc[b][:, o:CH], ks[0:STACK + MROWS, bass.ds(g * S + kb * P, P)],
                                                   qs[0:STACK + MROWS, bass.ds(g * QG + (h * S + c * CH + o), CH - o)],
                                                   start=True, stop=not diagonal)
                        if diagonal:
                            nc_last = nc.tensor.matmul(sc[b][:, o:o + P], ident[:, :], mask_kq[:, :], start=False, stop=True)
                        nc_last.then_inc(sc_done, 1)

                    def values(g, u):
                        c, kb = STEPS[u]
                        pe.wait_ge(exp_done, g * (NS * QPK) + ((u + 1) * QPK + 2))
                        if u == 0:
                            pe.wait_ge(v_ready, g + 1)
                        if kb == 0:
                            pe.wait_ge(po_read, g * NCH + (c + 1))
                        o = max(0, kb * P - c * CH)
                        for h in range(QPK):
                            last = nc.tensor.matmul(po[2 * HD * h:2 * HD * (h + 1), o:CH], v_now[:, kb, :],
                                                    prob[u % 2][:, h, o:CH], start=(kb == 0), stop=(kb == (c + 1) * TC - 1))
                        last.then_inc(pv_done, 1)

                    def turn_output(g, c):
                        pe.wait_ge(po_read, g * NCH + (c + 2))
                        for u in range(TC):
                            last = nc.tensor.transpose(small_f[:, u * P:(u + 1) * P], out_t[:, u * P:(u + 1) * P], m.ident[:, :])
                        last.then_inc(out_turn, 1)

                    def group(g, more):
                        for u in range(NS):
                            if u == 0 or u == C0:
                                pe.wait_ge(neg_in[STEPS[u][0]], g * (16 * MROWS) + 16 * MROWS)
                            scores(g, u, 0)
                            scores(g, u, 1)
                            if more:
                                maximum(g + 1, 2 * u)
                            scores(g, u, 2)
                            if u >= 1:
                                values(g, u - 1)
                            scores(g, u, 3)
                            if more:
                                maximum(g + 1, 2 * u + 1)
                            if u == C0 + 1 and more:
                                pe.wait_ge(ctx_done, g * NCH + 1)
                                turn_maxima(g + 1, 0)
                            if u == C0 + 4:
                                if more:
                                    pe.wait_ge(neg_read, g * NCH + NCH + 1)
                                turn_output(g, 0)
                        values(g, NS - 1)
                        pe.wait_ge(ctx_done, g * NCH + 2)
                        if more:
                            turn_maxima(g + 1, 1)
                            pe.wait_ge(neg_read, g * NCH + NCH + 2)
                        turn_output(g, 1)

                    pe.sem_inc(pv_done, 1)
                    pe.sem_inc(out_turn, 1)
                    pe.wait_ge(consts, 3)
                    for i in range(NMU):
                        maximum(0, i)
                        if i == HALF0 + 1:
                            turn_maxima(0, 0)
                    turn_maxima(0, 1)
                    with pe.Fori(0, KV - 1) as g:
                        group(g, True)
                    group(KV - 1, False)

                @block.scalar
                def _(act):
                    def read_maxima(gn, h):
                        act.wait_ge(neg_turn, gn * NCH + h + 1)
                        if not isinstance(gn, int) or gn:
                            act.wait_ge(neg_in[h], gn * (16 * MROWS))
                        nc.scalar.copy(neg_turned[h][:, :], small[0:MROWS * QPK, 0:CH]).then_inc(neg_read, 1)

                    def group(g, more):
                        for u in range(NS):
                            c, kb = STEPS[u]
                            o = max(0, kb * P - c * CH)
                            act.wait_ge(pv_done, g * NS + (max(0, u - 1) + 1))
                            for h in range(QPK):
                                act.wait_ge(sc_done, g * (NS * QPK) + (u * QPK + h + 1))
                                nc.scalar.activation(prob[u % 2][:, h, o:CH], sc[(u * QPK + h) % 2][:, o:CH], ACT.Exp,
                                                     scale=SCALE).then_inc(exp_done, 1)
                            if u == C0 + 2 and more:
                                read_maxima(g + 1, 0)
                        if more:
                            read_maxima(g + 1, 1)

                    nc.scalar.activation(warm[:, :], m.ident[0:1, 0:1], ACT.Exp).then_inc(exp_done, 2)
                    for h in range(NCH):
                        read_maxima(0, h)
                    with act.Fori(0, KV - 1) as g:
                        group(g, True)
                    group(KV - 1, False)

                @block.vector
                def _(dve):
                    def maximum(gn, i):
                        t, kc, a = MAX_UNITS[i]
                        w = min(CH, (t + 1) * P - kc * CH)
                        dve.wait_ge(mx_done, gn * NMU + (i + 1))
                        nc.vector.tensor_reduce(top[:, kc, t, 2 * a:2 * a + 2], mx[i % 2][:, :, 0:w], AX.X,
                                                ALU.max).then_inc(mx_read, 1)

                    def split_maxima(gn, h, units):
                        base = gn * sum(NEG_OPS) + sum(NEG_OPS[:h])
                        dve.wait_ge(mx_read, gn * NMU + units)
                        k = 0
                        source = top[:, 0, 0:TC, :]
                        if h:
                            nc.vector.tensor_tensor(best[:, :, :], top[:, 0, TC:T, :], top[:, 1, TC:T, :], ALU.max).then_inc(neg_chain, 1)
                            k += 1
                            dve.wait_ge(neg_chain, base + k)
                            source = best[:, :, :]
                        nc.vector.tensor_scalar(neg[:, :, :], source, -1.0, None, ALU.mult).then_inc(neg_chain, 1)
                        k += 1
                        dve.wait_ge(neg_chain, base + k)
                        if not isinstance(gn, int):
                            dve.wait_ge(neg_turn, gn * NCH + h - 1)
                        nc.vector.tensor_copy(neg_parts[h][:, :, 0, :], neg[:, :, :]).then_inc(neg_chain, 1)
                        k += 1
                        dve.wait_ge(neg_chain, base + k)
                        nc.vector.tensor_tensor(left[:, :, :], neg[:, :, :], neg_parts[h][:, :, 0, :], ALU.subtract).then_inc(neg_chain, 1)
                        k += 1
                        dve.wait_ge(neg_chain, base + k)
                        nc.vector.tensor_copy(neg_parts[h][:, :, 1, :], left[:, :, :]).then_inc(neg_chain, 1)
                        k += 1
                        dve.wait_ge(neg_chain, base + k)
                        nc.vector.tensor_tensor(neg_parts[h][:, :, 2, :], left[:, :, :], neg_parts[h][:, :, 1, :],
                                                ALU.subtract).then_inc(neg_done, 1)

                    def read_output(g, c):
                        dve.wait_ge(pv_done, g * NS + ((C0, NS)[c] + 1))
                        dve.wait_ge(out_turn, g * NCH + (c + 1))
                        nc.vector.tensor_copy(out_t[:, :], po[:, :]).then_inc(po_read, 1)

                    def normalise(g, c):
                        dve.wait_ge(out_turn, g * NCH + (c + 2))
                        o = small_f.rearrange("p (t h d) -> p t h d", t=TC, h=QPK)
                        nc.vector.reciprocal(inv[:, :, :], o[:, :, :, HD]).then_inc(inv_done, 1)
                        dve.wait_ge(inv_done, g * NCH + c + 1)
                        nc.vector.tensor_tensor(m.xn[:, c * TC:(c + 1) * TC, bass.ds(g * (QPK * HD), QPK * HD)].rearrange(
                            "p t (h d) -> p t h d", h=QPK), o[:, :, :, 0:HD],
                            inv[:, :, :].unsqueeze(3).broadcast_to([P, TC, QPK, HD]), ALU.mult).then_inc(ctx_done, 1)

                    def group(g, more):
                        for u in range(NS):
                            if more:
                                maximum(g + 1, 2 * u)
                            if u == C0:
                                read_output(g, 0)
                            if more:
                                maximum(g + 1, 2 * u + 1)
                                if 2 * u + 2 == HALF0:
                                    split_maxima(g + 1, 0, HALF0)
                            if u == C0 + 5:
                                normalise(g, 0)
                        if more:
                            split_maxima(g + 1, 1, NMU)
                        read_output(g, 1)
                        normalise(g, 1)

                    dve.sem_inc(po_read, 1)
                    dve.sem_inc(ctx_done, 1)
                    dve.wait_ge(c_in2, 16)
                    nc.vector.tensor_copy(mask_qk[:, :], masks[:, 0, :]).then_inc(consts, 1)
                    nc.vector.tensor_copy(mask_kq[:, :], masks[:, 1, :]).then_inc(consts, 1)
                    nc.vector.tensor_copy(ident[:, :], m.ident[:, :]).then_inc(consts, 1)
                    for i in range(NMU):
                        maximum(0, i)
                        if i + 1 == HALF0:
                            split_maxima(0, 0, HALF0)
                    split_maxima(0, 1, NMU)
                    with dve.Fori(0, KV - 1) as g:
                        group(g, True)
                    group(KV - 1, False)

        with ExitStack() as ctx:
            def sb(what, shape, dt=F32):
                return ctx.enter_context(nc.sbuf_tensor(f"{name}_{what}", shape, dt))

            def pb(what, shape, dt=F32):
                return ctx.enter_context(nc.psum_tensor(f"{name}_{what}", shape, dt))

            wd_raw = sb("wd_raw", [P, KT, H])
            wd_hi = sb("wd_hi", [P, KT, H], F32R)
            wd_lo = sb("wd_lo", [P, KT, H], F32R)
            b_out = sb("b_out", [P, H])
            xp = [pb(f"xpd{s}", [P, CH]) for s in range(2)]
            yp = [pb(f"yp{s}", [P, CH]) for s in range(2)]
            cm = NormSems(sem, "ctx")
            wd_in, wd_half, wd_ready, x_biased, y_done, x_done = (
                sem("wd_in"), sem("wd_half"), sem("wd_ready"), sem("x_biased"), sem("y_done"), sem("x_done"))

            with nc.Block() as block:
                @block.sync
                def _(sp):
                    sp.dma_start(wd_raw[:, :, :], m.dram["w_dense"]).then_inc(wd_in, 16)
                    sp.dma_start(b_out[:, :], m.dram["b_dense"].rearrange("(a h) -> a h", a=1).broadcast_to([P, H])).then_inc(wd_in, 16)

                @block.gpsimd
                def _(pool):
                    pool.wait_ge(wd_in, 32)
                    nc.gpsimd.tensor_copy(wd_hi[:, :, :], wd_raw[:, :, :]).then_inc(wd_half, 1)
                    pool.wait_ge(wd_half, 1)
                    nc.gpsimd.tensor_tensor(wd_lo[:, :, :], wd_raw[:, :, :], wd_hi[:, :, :].bitcast(F32),
                                            ALU.subtract).then_inc(wd_ready, 1)
                    nc.gpsimd.tensor_tensor(m.x[:, :, :], m.x[:, :, :], b_out[:, :].unsqueeze(1).broadcast_to([P, T, H]),
                                            ALU.add).then_inc(x_biased, 1)

                @block.tensor
                def _(pe):
                    for t in range(T):
                        transpose_tile(m, pe, cm, xp[t % 2], t, ready=False)
                    pe.wait_ge(wd_ready, 1)
                    for t in range(T):
                        pe.wait_ge(cm.xt_lo, t + 1)
                        if t >= 2:
                            pe.wait_ge(x_done, t - 1)
                        rows = slice(t * P, (t + 1) * P)
                        product(nc, yp[t % 2][:, :], [(m.xt_hi[:, k, rows], m.xt_lo[:, k, rows], wd_hi[:, k, :], wd_lo[:, k, :])
                                                      for k in range(KT)]).then_inc(y_done, 1)

                @block.scalar
                def _(act):
                    for t in range(T):
                        hi_tile(m, act, cm, xp[t % 2], t)

                @block.vector
                def _(dve):
                    for t in range(T):
                        lo_tile(m, dve, cm, xp[t % 2], t)
                    dve.wait_ge(x_biased, 1)
                    for t in range(T):
                        dve.wait_ge(y_done, t + 1)
                        nc.vector.tensor_tensor(m.x[:, t, :], yp[t % 2][:, :], m.x[:, t, :], ALU.add).then_inc(x_done, 1)



def program(nc, m_in, out, stages):
    m = Shared()
    m.nc = nc
    m.taken = []
    m.kept, m.counted = {}, {}
    m.dram = m_in
    layers = {"moe": moe_layer, "causal": causal_attention_layer, "butter": butterfly_layer, "full": full_attention_layer}
    with ExitStack() as ctx:
        def sb(what, shape, dt=F32):
            return ctx.enter_context(nc.sbuf_tensor(what, shape, dt))

        m.x = sb("x", [P, T, H])
        m.xn = sb("xn", [P, T, H])
        m.xt_hi = sb("xt_hi", [P, KT, S], F32R)
        m.xt_lo = sb("xt_lo", [P, KT, S], F32R)
        m.ident = sb("ident", [P, P])
        m.stats = sb("stats", [P, T, 6])
        m.mean_var = sb("mean_var", [P, T, 2])
        m.var_eps = sb("var_eps", [P, T])
        m.minus_half = sb("minus_half", [P, T])
        m.zero = sb("zero", [P, 1])
        m.rstd = sb("rstd", [P, T])
        x_in = ctx.enter_context(nc.semaphore("x_in"))
        x_out = ctx.enter_context(nc.semaphore("x_out"))
        with nc.Block() as block:
            @block.gpsimd
            def _(pool):
                nc.gpsimd.memset(m.minus_half[:, :], -0.5)
                nc.gpsimd.memset(m.zero[:, :], 0.0)

            @block.sync
            def _(sp):
                sp.dma_start(m.x[:, :, :], m.dram["hidden"].rearrange("(t p) h -> p t h", p=P)).then_inc(x_in, 16)
                sp.dma_start(m.ident[:, :], m.dram["identity"]).then_inc(x_in, 16)
                sp.wait_ge(x_in, 32)
        for n, stage in enumerate(stages):
            layers[stage](m, f"{stage}{n}")
            m.release()
        with nc.Block() as block:
            @block.sync
            def _(sp):
                sp.dma_start(out.rearrange("(t p) h -> p t h", p=P), m.x[:, :, :]).then_inc(x_out, 16)
                sp.wait_ge(x_out, 16)


STAGES = ("moe", "causal", "moe", "butter", "full", "butter")


def layout(inputs):
    import numpy as np

    f = np.ascontiguousarray
    i = {k: np.asarray(v) for k, v in inputs.items()}
    d = {}

    def by_partition(w):
        return f(w.reshape(w.shape[0] // P, P, w.shape[1]).transpose(1, 0, 2))

    d["hidden"] = f(i["L0_attn_hidden_states"].reshape(S, H))
    gate = np.concatenate([i["L0_ffn_Sg"][None], i["L0_ffn_Wg"]])
    up = np.concatenate([i["L0_ffn_Su"][None], i["L0_ffn_Wu"]])
    down = np.concatenate([i["L0_ffn_Sd"][None], i["L0_ffn_Wd"]])
    gu = np.concatenate([gate, up], axis=1).transpose(0, 2, 1)
    d["w_gu"] = f(gu.reshape(NE, KT, P, 2 * FI).transpose(0, 2, 1, 3).reshape(NE, P, GU_COLS))
    d["w_down"] = f(down.transpose(0, 2, 1).reshape(NE, IT, P, H).transpose(0, 2, 1, 3).reshape(NE, P, IT * H))
    router = np.zeros((H, P), np.float32)
    router[:, :E] = i["L0_ffn_gate_w"].T
    d["gate_w"] = by_partition(router)
    d["gate_bias"] = f(i["L0_ffn_bias"].reshape(E, 1))
    kv, hd, qpk = 8, 16, 4
    w = i["L0_attn_w_qkv"].reshape(kv, qpk + 2, hd, H)
    b = i["L0_attn_b_qkv"].reshape(kv, qpk + 2, hd)
    w = np.concatenate([w[:, qpk].reshape(-1, H), w[:, qpk + 1].reshape(-1, H), w[:, :qpk].reshape(-1, H)])
    b = np.concatenate([b[:, qpk].reshape(-1), b[:, qpk + 1].reshape(-1), b[:, :qpk].reshape(-1)])
    d["w_qkv"] = by_partition(w.T)
    d["b_qkv"] = f(b.reshape(-1, P).T)
    d["w_dense"] = by_partition(i["L0_attn_w_dense"].T)
    d["b_dense"] = f(i["L0_attn_b_dense"])
    d["perm"] = f(i["L1_ffn_perm"])
    d["perm_col"] = f(d["perm"].reshape(KT, P).T)
    d["up"] = f(i["L1_ffn_up"].reshape(KT, P, -1).transpose(1, 0, 2))
    d["down"] = f(i["L1_ffn_down"].transpose(1, 0, 2))
    d["w1_qkv"] = by_partition(i["L1_attn_Wqkv"])
    d["w1_out"] = f(i["L1_attn_Wo"])
    d["b1_qkv"] = f(i["L1_attn_bqkv"].reshape(-1, P).T)
    d["b1_out"] = f(i["L1_attn_bo"])
    d["identity"] = np.eye(P, dtype=np.float32)
    lower = (np.arange(E)[None, :] < np.arange(E)[:, None]).astype(np.float32)
    d["tie"] = f(np.broadcast_to(lower.reshape(1, -1), (P, E * E)))
    raw_at = np.arange(E) % RAW * W_COLS
    d["route"] = np.concatenate([P * np.arange(1, T), P * np.arange(T) - S, np.arange(TOPK),
                                 np.diff(raw_at, prepend=0)]).astype(np.float32)
    d["index_row"] = np.arange(H, dtype=np.float32)
    d["index_col"] = f(np.arange(H, dtype=np.float32).reshape(KT, P).T)
    inv_freq = np.float32(1) / np.power(np.float32(1e6), np.arange(0, hd, 2, dtype=np.float32) / np.float32(hd))
    angle = inv_freq.astype(np.float32)[:, None] * np.arange(S, dtype=np.float32)[None, :]
    d["cos"] = f(np.tile(np.cos(angle), (2 * P // hd, 1)).astype(np.float32))
    d["sin"] = f(np.tile(np.sin(angle), (2 * P // hd, 1)).astype(np.float32))
    swap = np.zeros((P, P), np.float32)
    for o in range(P):
        if o % hd < hd // 2:
            swap[o + hd // 2, o] = -1
        else:
            swap[o - hd // 2, o] = 1
    d["swap"] = swap
    later = np.where(np.arange(P)[None, :] > np.arange(P)[:, None], np.float32(-1e30), np.float32(0))
    d["masks"] = f(np.stack([later, later.T], axis=1).astype(np.float32))
    return d


def kernel(**inputs):
    import numpy as _np
    import concourse.bacc as _bacc
    from concourse import mybir as _mybir
    from concourse.bass_utils import run_bass_kernel_spmd as _run

    nc = _bacc.Bacc("TRN2", target_bir_lowering=False, num_devices=1)
    arrays, aps = {}, {}
    for name, a in layout(inputs).items():
        arrays[f"in_{name}"] = a
        aps[name] = nc.dram_tensor(f"in_{name}", a.shape, _mybir.dt.from_np(a.dtype), kind="ExternalInput").ap()
    out = nc.dram_tensor("out", (S, H), _mybir.dt.from_np(_np.dtype("float32")), kind="ExternalOutput").ap()
    program(nc, aps, out, STAGES)
    r = _run(nc, [arrays], core_ids=[0])
    return r.results[0]["out"].reshape(1, S, H)
```

```python
from contextlib import ExitStack

import concourse.bass as bass
from concourse import mybir

ALU = mybir.AluOpType
ACT = mybir.ActivationFunctionType
AX = mybir.AxisListType
F32 = mybir.dt.float32
F32R = mybir.dt.float32r
BF16 = mybir.dt.bfloat16
I32 = mybir.dt.int32
U32 = mybir.dt.uint32

P = 128
S = 1024
H = 512
T = S // P
KT = H // P
CH = 512
NCH = S // CH
EPS = 1e-5

E = 16
TOPK = 4
NE = E + 1
FI = 256
IT = FI // P
GU_COLS = KT * 2 * FI
W_COLS = GU_COLS + IT * H
RING = 4
NB = (S * TOPK + E * (P - 1)) // P
RAW = 5
EARLY = 3
DVE_COLS = GU_COLS * 5 // 8
ROW = H + E
ROUTE_COLS = 2 * T - 1 + TOPK + E


class Shared:

    def semaphore(self, name):
        self.taken.append(self.nc.alloc_semaphore(name=name))
        return self.taken[-1]

    def gpsimd_dma_semaphore(self, name, adds):
        if name not in self.kept:
            self.kept[name] = self.nc.alloc_semaphore(name=name)
            self.counted[name] = 0
        start = self.counted[name]
        self.counted[name] += adds
        return self.kept[name], start

    def clear_stale(self, sp):
        for s in self.stale:
            sp.sem_clear(s)

    def release(self):
        for s in self.stale:
            self.nc.release_semaphore(s)
        self.stale, self.taken = self.taken, []

    def load_x(self, sp, rows):
        self.x_loads += 1
        for t in range(T):
            sp.dma_start(self.x[:, t, :], rows[t * P:(t + 1) * P, :]).then_inc(self.x_tile[t], 16)


def next_stats(m, dve, sem, count, t):
    dve.wait_ge(sem, count)
    m.nc.vector.bn_stats(out=m.stats[:, t, :], in_=m.x[:, t, :]).then_inc(m.next_stats, 1)


RSTD_TILES = 1
NORM_LAG = 4


def normalise_vector(m, dve, nm, lo_of):
    nc = m.nc

    def moments(t):
        nc.vector.bn_aggr(out=m.mean_var[:, t, :], in_=m.stats[:, t, :]).then_inc(nm.moments, 1)

    def normalise(t):
        if t % RSTD_TILES == 0:
            dve.wait_ge(nm.rstd, t // RSTD_TILES + 1)
        nc.vector.tensor_scalar(m.xn[:, t, :], m.x[:, t, :], m.mean_var[:, t, 0:1], m.rstd[:, t:t + 1],
                                ALU.subtract, ALU.mult).then_inc(nm.xn, 1)
        if t >= 2:
            lo_of(t - 2)

    if m.have_stats:
        for t in range(T):
            moments(t)
        for t in range(T):
            normalise(t)
    else:
        for t in range(T + NORM_LAG):
            if t < T:
                dve.wait_ge(m.x_tile[t], 16 * m.x_loads)
                nc.vector.bn_stats(out=m.stats[:, t, :], in_=m.x[:, t, :]).then_inc(nm.stats, 1)
            if 0 < t <= T:
                dve.wait_ge(nm.stats, t)
                moments(t - 1)
            if t >= NORM_LAG:
                normalise(t - NORM_LAG)
    lo_of(T - 2)
    lo_of(T - 1)


def rstd_gpsimd(m, pool, nm):
    for g in range(T // RSTD_TILES):
        tiles = slice(g * RSTD_TILES, (g + 1) * RSTD_TILES)
        pool.wait_ge(nm.moments, (g + 1) * RSTD_TILES)
        m.nc.gpsimd.tensor_scalar(m.var_eps[:, tiles], m.mean_var[:, tiles, 1], EPS, None, ALU.add).then_inc(nm.var_eps, 1)
        pool.wait_ge(nm.var_eps, g + 1)
        m.nc.gpsimd.tensor_tensor(m.rstd[:, tiles], m.var_eps[:, tiles], m.minus_half[:, tiles], ALU.pow).then_inc(nm.rstd, 1)


class NormSems:
    def __init__(self, sem, name="norm"):
        self.stats = sem(f"{name}_stats")
        self.moments = sem(f"{name}_moments")
        self.var_eps = sem(f"{name}_var_eps")
        self.rstd = sem(f"{name}_rstd")
        self.xn = sem(f"{name}_xn")
        self.xt = sem(f"{name}_xt")
        self.xt_hi = sem(f"{name}_xt_hi")
        self.xt_lo = sem(f"{name}_xt_lo")


def transpose_tile(m, pe, nm, bank, t, ready=True):
    if ready:
        pe.wait_ge(nm.xn, t + 1)
    if t >= 2:
        pe.wait_ge(nm.xt_lo, t - 1)
    for k in range(KT):
        last = m.nc.tensor.transpose(bank[:, k * P:(k + 1) * P], m.xn[:, t, k * P:(k + 1) * P], m.ident[:, :])
    last.then_inc(nm.xt, 1)


def hi_tile(m, act, nm, bank, t):
    act.wait_ge(nm.xt, t + 1)
    m.nc.scalar.copy(m.xt_hi[:, :, t * P:(t + 1) * P],
                     bank[:, :].rearrange("p (k c) -> p k c", k=KT)).then_inc(nm.xt_hi, 1)


def lo_tile(m, dve, nm, bank, t):
    dve.wait_ge(nm.xt_hi, t + 1)
    m.nc.vector.tensor_tensor(m.xt_lo[:, :, t * P:(t + 1) * P], bank[:, :].rearrange("p (k c) -> p k c", k=KT),
                              m.xt_hi[:, :, t * P:(t + 1) * P].bitcast(F32), ALU.subtract).then_inc(nm.xt_lo, 1)


def product(nc, out, pairs):
    n = 0
    for a_hi, a_lo, b_hi, b_lo in pairs:
        for a, b in ((a_hi, b_hi), (a_hi, b_lo), (a_lo, b_hi)):
            last = nc.tensor.matmul(out, a, b, start=(n == 0), stop=(n == 3 * len(pairs) - 1))
            n += 1
    return last


def some(count):
    return not isinstance(count, int) or count > 0


def moe_layer(m, name):
    nc = m.nc
    xn_rows = nc.dram_tensor(f"{name}_xn_rows", (S + P, ROW), F32).ap()
    acc_rows = nc.dram_tensor(f"{name}_acc_rows", (S + P, H), F32).ap()
    with ExitStack() as ctx:
        def sb(what, shape, dt=F32):
            return ctx.enter_context(nc.sbuf_tensor(f"{name}_{what}", shape, dt))

        def sem(what):
            return m.semaphore(f"{name}_{what}")

        def gu_w(w, k):
            return w[:, k * 2 * FI:(k + 1) * 2 * FI]

        def down_w(w, i):
            return w[:, i, :]

        raw = sb("raw", [P, RAW * W_COLS])
        w_hi = [sb(f"w_hi{s}", [P, W_COLS], F32R) for s in range(2)]
        w_lo = [sb(f"w_lo{s}", [P, W_COLS], F32R) for s in range(2)]
        down_hi, down_lo = ([w[0][:, GU_COLS:W_COLS].rearrange("p (i h) -> p i h", i=IT)]
                            + [half[:, n * IT:(n + 1) * IT, S - H:S] for n in range(2)]
                            + [w[1][:, GU_COLS:W_COLS].rearrange("p (i h) -> p i h", i=IT)]
                            for w, half in ((w_hi, m.xt_hi), (w_lo, m.xt_lo)))
        silu = [sb(f"silu{s}", [P, FI]) for s in range(2)]
        z = [sb(f"z{s}", [P, FI]) for s in range(2)]
        zt_hi = [sb(f"zt_hi{s}", [P, FI], F32R) for s in range(2)]
        zt_lo = [sb(f"zt_lo{s}", [P, FI], F32R) for s in range(2)]
        token_of = sb("token_of", [P, NB], I32)
        expert_of = sb("expert_of", [1, NB], I32)
        raw_at = sb("raw_at", [1, NB], I32)
        first_of = sb("first_of", [1, E], I32)
        raw_in = [sem(f"raw_in{s}") for s in range(RAW)]

        def load_raw(eng, slot, e):
            at = slot * W_COLS
            eng.dma_start(raw[:, at:at + GU_COLS], m.dram["w_gu"][e]).then_inc(raw_in[slot], 16)
            eng.dma_start(raw[:, at + GU_COLS:at + W_COLS], m.dram["w_down"][e]).then_inc(raw_in[slot], 16)

        with ExitStack() as part:
            def sb(what, shape, dt=F32):
                return part.enter_context(nc.sbuf_tensor(f"{name}_{what}", shape, dt))

            def pb(what, shape, dt=F32):
                return part.enter_context(nc.psum_tensor(f"{name}_{what}", shape, dt))

            gate_raw = sb("gate_raw", [P, KT, P])
            gate_hi = sb("gate_hi", [P, KT, P], F32R)
            gate_lo = sb("gate_lo", [P, KT, P], F32R)
            gate_bias = sb("gate_bias", [E, 1])
            tie = sb("tie", [P, E * E])
            consts = sb("consts", [P, ROUTE_COLS])
            index_row = sb("index_row", [P, P])
            index_col = sb("index_col", [P, KT])
            score_t = sb("score_t", [E, S])
            score = sb("score", [P, T, E])
            spare = raw[:, EARLY * W_COLS:RAW * W_COLS].bitcast(BF16)
            beats = spare[:, 0:T * E * E].rearrange("p (t a b) -> p t a b", t=T, a=E)
            rank = sb("rank", [P, T, E])
            mask = sb("mask", [P, T, E], BF16)
            chosen = sb("chosen", [P, T, E])
            total = sb("total", [P, T])
            inv_total = sb("inv_total", [P, T])
            cw = sb("cw", [P, T, E])
            before = sb("before", [P, P], BF16)
            ones = sb("ones", [P, P], BF16)
            over = sb("over", [P, E, T - 1])
            blocks = sb("blocks", [P, E])
            ahead = sb("ahead", [P, E, E])
            first = sb("first", [P, E])
            place = sb("place", [P, T, E])
            pick = sb("pick", [P, T, TOPK, E])
            slot = sb("slot", [P, T, TOPK])
            slot_i = sb("slot_i", [P, T, TOPK], I32)
            block_i = sb("block_i", [P, T, TOPK], I32)
            block_f = sb("block_f", [P, T, TOPK])
            within = sb("within", [P, T, TOPK])
            at, n_place, n_block = T * E * E, T * TOPK * P, T * TOPK * NB
            at_place = spare[:, at:at + n_place].rearrange("p (t r c) -> p t r c", t=T, r=TOPK)
            at += n_place
            in_block, in_block_p, in_block_t = (spare[:, at + n * n_block:at + (n + 1) * n_block].rearrange(
                "p (t r c) -> p t r c", t=T, r=TOPK) for n in range(3))
            padding = sb("padding", [P, NB])
            begun = sb("begun", [1, NB, E], BF16)
            begun_at = sb("begun_at", [1, NB, E], BF16)
            expert_f = sb("expert_f", [1, NB])
            raw_f = sb("raw_f", [1, NB])

            turn = [pb(f"turn{s}", [P, CH]) for s in range(2)]
            gu = [pb(f"gu{s}", [P, CH]) for s in range(2)]
            y = [pb(f"y{s}", [P, CH]) for s in range(2)]
            logits = [pb(f"logits{c}", [P, CH]) for c in range(NCH)]
            counts = logits[1]

            nm = NormSems(sem)
            gate_in, gate_hi_done, gate_w, const_in = sem("gate_in"), sem("gate_hi_done"), sem("gate_w"), sem("const_in")
            w_hi_done, w_ready = sem("w_hi_done"), sem("w_ready")
            logits_done, sig_done, score_b, score_turned, score_done = (
                sem("logits_done"), sem("sig_done"), sem("score_b"), sem("score_turned"), sem("score_done"))
            compared, route, ready = sem("compared"), sem("route"), sem("ready")
            within_done, places_done = sem("within_done"), sem("places_done")
            mask_done, cw_done, counted, maps_done, mapped = (
                sem("mask_done"), sem("cw_done"), sem("counted"), sem("maps_done"), sem("mapped"))
            gu_done, silu_done, z_done = sem("gu_done"), sem("silu_done"), sem("z_done")
            zt_done, zt_hi_done, zt_lo_done = sem("zt_done"), sem("zt_hi_done"), sem("zt_lo_done")
            y_done, x_done, rows_out = sem("y_done"), sem("x_done"), sem("rows_out")
            table_done = sem("table_done")
            SHARED = 1
            POOL_TILES = 3
            w0_hi, w0_lo = sem("w0_hi"), sem("w0_lo")
            SHARED_RAW = EARLY - 1

            block = part.enter_context(nc.Block())

            @block.sync
            def _(sp):
                sp.dma_start(gate_raw[:, :, :], m.dram["gate_w"]).then_inc(gate_in, 16)
                load_raw(sp, SHARED_RAW, 0)
                sp.dma_start(gate_bias[:, :], m.dram["gate_bias"]).then_inc(const_in, 16)
                sp.dma_start(tie[:, :], m.dram["tie"]).then_inc(const_in, 16)
                sp.dma_start(index_row[:, :], m.dram["index_row"][0:P].rearrange("(a h) -> a h", a=1).broadcast_to([P, P])).then_inc(const_in, 16)
                sp.dma_start(index_col[:, :], m.dram["index_col"]).then_inc(const_in, 16)
                sp.dma_start(consts[:, :], m.dram["route"].rearrange("(a h) -> a h", a=1).broadcast_to([P, ROUTE_COLS])).then_inc(const_in, 16)
                for e in range(EARLY - 1):
                    load_raw(sp, e, e + 1)
                m.clear_stale(sp)
                sp.wait_ge(nm.xn, T)
                sp.dma_start(xn_rows[0:S, 0:H].rearrange("(t p) h -> p t h", p=P), m.xn[:, :, :]).then_inc(rows_out, 16)
                sp.dma_start(xn_rows[S:S + P, 0:H], m.xn[:, 0, :]).then_inc(rows_out, 16)
                sp.wait_ge(w_ready, 1)
                load_raw(sp, SHARED_RAW, EARLY)
                sp.wait_ge(cw_done, 1)
                sp.dma_start(xn_rows[0:S, H:ROW].rearrange("(t p) e -> p t e", p=P), cw[:, :, :]).then_inc(rows_out, 16)
                sp.dma_start(xn_rows[S:S + P, H:ROW], cw[:, 0, :]).then_inc(rows_out, 16)
                for t in range(T):
                    sp.wait_ge(x_done, t + 1)
                    sp.dma_start(acc_rows[t * P:(t + 1) * P, :], m.x[:, t, :]).then_inc(rows_out, 16)
                sp.dma_start(acc_rows[S:S + P, :], m.x[:, 0, :]).then_inc(rows_out, 16)
                sp.wait_ge(rows_out, 16 * (T + 5))

            @block.gpsimd
            def _(pool):
                rstd_gpsimd(m, pool, nm)
                shared = raw[:, SHARED_RAW * W_COLS:(SHARED_RAW + 1) * W_COLS]
                pool.wait_ge(w_hi_done, 1)
                nc.gpsimd.tensor_tensor(w_lo[SHARED][:, :], shared, w_hi[SHARED][:, :].bitcast(F32),
                                        ALU.subtract).then_inc(w_ready, 1)
                pool.wait_ge(w0_hi, 1)
                nc.gpsimd.tensor_tensor(w_lo[0][:, :], raw[:, 0:W_COLS], w_hi[0][:, :].bitcast(F32),
                                        ALU.subtract).then_inc(w0_lo, 1)
                pool.wait_ge(within_done, 1)
                for t in range(POOL_TILES):
                    for r in range(TOPK):
                        nc.gpsimd.tensor_scalar(at_place[:, t, r, :], index_row[:, :], within[:, t, r:r + 1], None,
                                                ALU.is_equal).then_inc(places_done, 1)

            @block.tensor
            def _(pe):
                def turn_z(b, s):
                    pe.wait_ge(z_done, b + 1)
                    if b >= 2:
                        pe.wait_ge(zt_lo_done, b - 1)
                    for j in range(IT):
                        last = nc.tensor.transpose(turn[s][:, j * P:(j + 1) * P], z[s][:, j * P:(j + 1) * P], m.ident[:, :])
                    last.then_inc(zt_done, 1)

                def gate_up(s, t):
                    product(nc, gu[s][:, :], [(m.xt_hi[:, k, t * P:(t + 1) * P], m.xt_lo[:, k, t * P:(t + 1) * P],
                                               gu_w(w_hi[SHARED], k), gu_w(w_lo[SHARED], k)) for k in range(KT)]).then_inc(gu_done, 1)

                def down(b, s):
                    pe.wait_ge(zt_lo_done, b + 1)
                    if b >= 2:
                        pe.wait_ge(x_done, b - 1)
                    product(nc, y[s][:, :], [(zt_hi[s][:, j * P:(j + 1) * P], zt_lo[s][:, j * P:(j + 1) * P],
                                              down_w(down_hi[-1], j), down_w(down_lo[-1], j)) for j in range(IT)]).then_inc(y_done, 1)

                for t in range(T):
                    transpose_tile(m, pe, nm, turn[t % 2], t)
                pe.wait_ge(nm.xt_lo, T)
                pe.wait_ge(gate_w, 1)
                for c in range(NCH):
                    cols = slice(c * CH, (c + 1) * CH)
                    product(nc, logits[c][:, :], [(gate_hi[:, k, :], gate_lo[:, k, :], m.xt_hi[:, k, cols], m.xt_lo[:, k, cols])
                                                  for k in range(KT)]).then_inc(logits_done, 1)

                def count():
                    pe.wait_ge(ready, 2)
                    pe.wait_ge(mask_done, 1)
                    taken = mask[:, :, :].rearrange("p t e -> p (t e)")
                    nc.tensor.matmul(counts[:, 0:T * E], before[:, :], taken, start=True, stop=False)
                    for d in range(1, T):
                        nc.tensor.matmul(counts[:, d * E:T * E], ones[:, :], taken[:, 0:(T - d) * E], start=False, stop=(d == T - 1))
                    for t in range(T):
                        last = nc.tensor.matmul(counts[:, T * E:(T + 1) * E], ones[:, :], mask[:, t, :], start=(t == 0), stop=(t == T - 1))
                    last.then_inc(counted, 1)

                pe.wait_ge(w_ready, 1)
                for t in range(T + 2):
                    if t < T:
                        if t >= 2:
                            pe.wait_ge(z_done, t - 1)
                        gate_up(t % 2, t)
                    if t == 0:
                        pe.wait_ge(score_b, 1)
                        for u in range(T):
                            last = nc.tensor.transpose(logits[0][:, u * E:(u + 1) * E], score_t[:, u * P:(u + 1) * P],
                                                       m.ident[0:E, 0:E])
                        last.then_inc(score_turned, 1)
                    if 1 <= t <= T:
                        turn_z(t - 1, (t - 1) % 2)
                    if t == 4:
                        count()
                    if t >= 2:
                        down(t - 2, t % 2)
                pe.wait_ge(maps_done, 3)
                pe.wait_ge(places_done, POOL_TILES * TOPK)
                for n in range(T * TOPK):
                    t, r = divmod(n, TOPK)
                    for half in (in_block_p, in_block_t):
                        last = nc.tensor.matmul(logits[0][:, 0:NB], at_place[:, t, r, :], half[:, t, r, :],
                                                start=(n == 0 and half is in_block_p),
                                                stop=(n == T * TOPK - 1 and half is in_block_t))
                last.then_inc(mapped, 1)

            @block.scalar
            def _(act):
                def silu_of(b, s):
                    act.wait_ge(gu_done, b + 1)
                    if b >= 2:
                        act.wait_ge(z_done, b - 1)
                    nc.scalar.activation(silu[s][:, :], gu[s][:, 0:FI], ACT.Silu).then_inc(silu_done, 1)

                def zt_hi_of(b, s):
                    act.wait_ge(zt_done, b + 1)
                    if b >= 2:
                        act.wait_ge(y_done, b - 1)
                    nc.scalar.copy(zt_hi[s][:, :], turn[s][:, 0:FI]).then_inc(zt_hi_done, 1)

                act.wait_ge(gate_in, 16)
                nc.scalar.copy(gate_hi[:, :, :], gate_raw[:, :, :]).then_inc(gate_hi_done, 1)
                for t in range(T):
                    hi_tile(m, act, nm, turn[t % 2], t)
                    if t == T - 1:
                        act.wait_ge(raw_in[SHARED_RAW], 32)
                        nc.scalar.copy(w_hi[SHARED][:, :], raw[:, SHARED_RAW * W_COLS:(SHARED_RAW + 1) * W_COLS]).then_inc(w_hi_done, 1)
                for c in range(NCH):
                    act.wait_ge(logits_done, c + 1)
                    nc.scalar.activation(score_t[:, c * CH:(c + 1) * CH], logits[c][0:E, :], ACT.Sigmoid).then_inc(sig_done, 1)
                for t in range(T + 2):
                    if t < T:
                        silu_of(t, t % 2)
                    if t == 0:
                        act.wait_ge(score_turned, 1)
                        nc.scalar.copy(score[:, :, :], logits[0][:, 0:T * E].rearrange("p (t e) -> p t e", t=T)).then_inc(score_done, 1)
                    if 1 <= t <= T:
                        zt_hi_of(t - 1, (t - 1) % 2)
                    if t == 2:
                        act.wait_ge(raw_in[0], 32)
                        nc.scalar.copy(w_hi[0][:, :], raw[:, 0:W_COLS]).then_inc(w0_hi, 1)

            @block.vector
            def _(dve):
                def z_of(b, s):
                    dve.wait_ge(silu_done, b + 1)
                    if b >= 2:
                        dve.wait_ge(zt_done, b - 1)
                    nc.vector.tensor_tensor(z[s][:, :], silu[s][:, :], gu[s][:, FI:2 * FI], ALU.mult).then_inc(z_done, 1)

                def zt_lo_of(b, s):
                    dve.wait_ge(zt_hi_done, b + 1)
                    nc.vector.tensor_tensor(zt_lo[s][:, :], turn[s][:, 0:FI], zt_hi[s][:, :].bitcast(F32),
                                            ALU.subtract).then_inc(zt_lo_done, 1)

                def add(t, s):
                    dve.wait_ge(y_done, t + 1)
                    nc.vector.scalar_tensor_tensor(out=m.x[:, t, :], in0=y[s][:, :], scalar=0.5, in1=m.x[:, t, :],
                                                   op0=ALU.mult, op1=ALU.add).then_inc(x_done, 1)

                row = index_row[:, :]
                thresholds = consts[:, 0:T - 1]
                tile_start = consts[:, T - 1:2 * T - 1]
                ranks = consts[:, 2 * T - 1:2 * T - 1 + TOPK]
                raw_step = consts[0:1, 2 * T - 1 + TOPK:2 * T - 1 + TOPK + E]

                def compare():
                    dve.wait_ge(score_done, 1)
                    for e in range(E):
                        if e:
                            nc.vector.tensor_tensor(beats[:, :, e, 0:e], score[:, :, 0:e],
                                                    score[:, :, e:e + 1].broadcast_to([P, T, e]), ALU.is_ge).then_inc(compared, 1)
                        nc.vector.tensor_tensor(beats[:, :, e, e:E], score[:, :, e:E],
                                                score[:, :, e:e + 1].broadcast_to([P, T, E - e]), ALU.is_gt).then_inc(compared, 1)

                def choose():
                    dve.wait_ge(compared, 2 * E - 1)
                    nc.vector.tensor_reduce(rank[:, :, :], beats[:, :, :, :], AX.X, ALU.add).then_inc(route, 1)
                    dve.wait_ge(route, 1)
                    nc.vector.tensor_scalar(mask[:, :, :], rank[:, :, :], float(TOPK) - 0.5, None, ALU.is_lt).then_inc(mask_done, 1)
                    nc.vector.scalar_tensor_tensor(out=chosen[:, :, :], in0=rank[:, :, :], scalar=float(TOPK) - 0.5,
                                                   in1=score[:, :, :], op0=ALU.is_lt, op1=ALU.mult).then_inc(route, 1)
                    nc.vector.tensor_tensor(pick[:, :, :, :], rank[:, :, :].unsqueeze(2).broadcast_to([P, T, TOPK, E]),
                                            ranks.unsqueeze(1).unsqueeze(3).broadcast_to([P, T, TOPK, E]),
                                            ALU.is_equal).then_inc(route, 1)
                    dve.wait_ge(route, 2)
                    nc.vector.tensor_reduce(total[:, :], chosen[:, :, :], AX.X, ALU.add).then_inc(route, 1)
                    dve.wait_ge(route, 4)
                    nc.vector.tensor_scalar(total[:, :], total[:, :], 1e-20, None, ALU.add).then_inc(route, 1)
                    dve.wait_ge(route, 5)
                    nc.vector.reciprocal(inv_total[:, :], total[:, :]).then_inc(route, 1)
                    dve.wait_ge(route, 6)
                    nc.vector.scalar_tensor_tensor(out=cw[:, :, :], in0=chosen[:, :, :], scalar=0.5,
                                                   in1=inv_total[:, :].unsqueeze(2).broadcast_to([P, T, E]),
                                                   op0=ALU.mult, op1=ALU.mult).then_inc(cw_done, 1)

                def place_tokens():
                    dve.wait_ge(counted, 1)
                    nc.vector.tensor_tensor(over[:, :, :], counts[:, T * E:(T + 1) * E].unsqueeze(2).broadcast_to([P, E, T - 1]),
                                            thresholds.unsqueeze(1).broadcast_to([P, E, T - 1]), ALU.is_gt).then_inc(route, 1)
                    dve.wait_ge(route, 7)
                    nc.vector.tensor_reduce(blocks[:, :], over[:, :, :], AX.X, ALU.add).then_inc(route, 1)
                    dve.wait_ge(route, 8)
                    nc.vector.scalar_tensor_tensor(out=ahead[:, :, :], in0=blocks[:, :].unsqueeze(1).broadcast_to([P, E, E]), scalar=1.0,
                                                   in1=tie[:, :].rearrange("p (a b) -> p a b", a=E),
                                                   op0=ALU.add, op1=ALU.mult).then_inc(route, 1)
                    dve.wait_ge(route, 9)
                    nc.vector.tensor_reduce(first[:, :], ahead[:, :, :], AX.X, ALU.add).then_inc(route, 1)
                    dve.wait_ge(route, 10)
                    nc.vector.scalar_tensor_tensor(out=place[:, :, :], in0=first[:, :].unsqueeze(1).broadcast_to([P, T, E]), scalar=float(P),
                                                   in1=counts[:, 0:T * E].rearrange("p (t e) -> p t e", t=T),
                                                   op0=ALU.mult, op1=ALU.add).then_inc(route, 1)
                    dve.wait_ge(route, 11)
                    nc.vector.tensor_tensor(pick[:, :, :, :], pick[:, :, :, :], place[:, :, :].unsqueeze(2).broadcast_to([P, T, TOPK, E]),
                                            ALU.mult).then_inc(route, 1)
                    dve.wait_ge(route, 12)
                    nc.vector.tensor_reduce(slot[:, :, :], pick[:, :, :, :], AX.X, ALU.add).then_inc(route, 1)
                    dve.wait_ge(route, 13)
                    nc.vector.tensor_copy(slot_i[:, :, :], slot[:, :, :]).then_inc(route, 1)
                    dve.wait_ge(route, 14)
                    nc.vector.tensor_scalar(block_i[:, :, :], slot_i[:, :, :], P.bit_length() - 1, None,
                                            ALU.logical_shift_right).then_inc(route, 1)
                    dve.wait_ge(route, 15)
                    nc.vector.tensor_copy(block_f[:, :, :], block_i[:, :, :]).then_inc(route, 1)
                    dve.wait_ge(route, 16)
                    nc.vector.scalar_tensor_tensor(out=within[:, :, :], in0=block_f[:, :, :], scalar=-float(P), in1=slot[:, :, :],
                                                   op0=ALU.mult, op1=ALU.add).then_inc(within_done, 1)

                def mark_blocks():
                    nc.vector.tensor_tensor(in_block[:, :, :, :], block_f[:, :, :].unsqueeze(3).broadcast_to([P, T, TOPK, NB]),
                                            row[:, 0:NB].unsqueeze(1).unsqueeze(1).broadcast_to([P, T, TOPK, NB]),
                                            ALU.is_equal).then_inc(route, 1)
                    dve.wait_ge(route, 17)
                    nc.vector.tensor_scalar(in_block_p[:, :, :, :], in_block[:, :, :, :], index_col[:, 0:1], None, ALU.mult).then_inc(maps_done, 1)
                    nc.vector.tensor_tensor(in_block_t[:, :, :, :], in_block[:, :, :, :],
                                            tile_start.unsqueeze(2).unsqueeze(3).broadcast_to([P, T, TOPK, NB]),
                                            ALU.mult).then_inc(maps_done, 1)

                def mark_places():
                    dve.wait_ge(within_done, 1)
                    rest = T - POOL_TILES
                    nc.vector.tensor_tensor(at_place[:, POOL_TILES:T, :, :], within[:, POOL_TILES:T, :].unsqueeze(3).broadcast_to([P, rest, TOPK, P]),
                                            row.unsqueeze(1).unsqueeze(1).broadcast_to([P, rest, TOPK, P]),
                                            ALU.is_equal).then_inc(maps_done, 1)

                def tables():
                    nc.vector.tensor_copy(first_of[:, :], first[0:1, :]).then_inc(table_done, 1)
                    nc.vector.tensor_tensor(begun[:, :, :], first[0:1, :].unsqueeze(1).broadcast_to([1, NB, E]),
                                            row[0:1, 0:NB].unsqueeze(2).broadcast_to([1, NB, E]), ALU.is_le).then_inc(route, 1)
                    dve.wait_ge(route, 18)
                    nc.vector.tensor_reduce(expert_f[:, :], begun[:, :, :], AX.X, ALU.add).then_inc(route, 1)
                    nc.vector.tensor_tensor(begun_at[:, :, :], begun[:, :, :], raw_step.unsqueeze(1).broadcast_to([1, NB, E]),
                                            ALU.mult).then_inc(route, 1)
                    dve.wait_ge(route, 19)
                    nc.vector.tensor_copy(expert_of[:, :], expert_f[:, :]).then_inc(table_done, 1)
                    dve.wait_ge(route, 20)
                    nc.vector.tensor_reduce(raw_f[:, :], begun_at[:, :, :], AX.X, ALU.add).then_inc(route, 1)
                    dve.wait_ge(route, 21)
                    nc.vector.tensor_copy(raw_at[:, :], raw_f[:, :]).then_inc(table_done, 1)

                nc.vector.memset(ones[:, :], 1.0).then_inc(ready, 1)
                normalise_vector(m, dve, nm, lambda t: lo_tile(m, dve, nm, turn[t % 2], t))
                dve.wait_ge(gate_hi_done, 1)
                nc.vector.tensor_tensor(gate_lo[:, :, :], gate_raw[:, :, :], gate_hi[:, :, :].bitcast(F32),
                                        ALU.subtract).then_inc(gate_w, 1)
                dve.wait_ge(const_in, 80)
                nc.vector.tensor_scalar(before[:, :], row, index_col[:, 0:1], None, ALU.is_gt).then_inc(ready, 1)
                dve.wait_ge(sig_done, NCH)
                nc.vector.tensor_scalar(score_t[:, :], score_t[:, :], gate_bias[:, 0:1], None, ALU.add).then_inc(score_b, 1)
                routing = {1: compare, 2: choose, 4: place_tokens, 5: mark_blocks, 6: mark_places, 7: tables}
                for t in range(T + 2):
                    if t < T:
                        z_of(t, t % 2)
                    if 1 <= t <= T:
                        zt_lo_of(t - 1, (t - 1) % 2)
                    if t >= 2:
                        add(t - 2, t % 2)
                    if t in routing:
                        routing[t]()
                dve.wait_ge(mapped, 1)
                nc.vector.tensor_scalar(padding[:, :], logits[0][:, 0:NB], 0.0, index_col[:, 0:1], ALU.is_equal, ALU.mult).then_inc(route, 1)
                dve.wait_ge(route, 22)
                nc.vector.scalar_tensor_tensor(out=token_of[:, :], in0=logits[0][:, 0:NB], scalar=float(S), in1=padding[:, :],
                                               op0=ALU.add, op1=ALU.add).then_inc(route, 1)

        routed_blocks(m, name, sb, sem, xn_rows, acc_rows, raw, raw_in, load_raw, w_hi, w_lo, down_hi, down_lo, gu_w, down_w,
                      silu, z, zt_hi, zt_lo, token_of, expert_of, raw_at, first_of)


def routed_blocks(m, name, sb, sem, xn_rows, acc_rows, raw, raw_in, load_raw, w_hi, w_lo, down_hi, down_lo, gu_w, down_w,
                  silu, z, zt_hi, zt_lo, token_of, expert_of, raw_at, first_of):
    nc = m.nc
    with ExitStack() as ctx:
        def sb(what, shape, dt=F32):
            return ctx.enter_context(nc.sbuf_tensor(f"{name}_{what}", shape, dt))

        def pb(what, shape, dt=F32):
            return ctx.enter_context(nc.psum_tensor(f"{name}_{what}", shape, dt))

        rows = [sb(f"rows{s}", [P, ROW]) for s in range(RING)]
        out_rows = [sb(f"out_rows{s}", [P, H]) for s in range(2)]
        from_row = [sb(f"from_row{s}", [P, 1], I32) for s in range(RING)]
        to_row = sb("to_row", [P, 1], I32)
        gu = [pb(f"gu_{s}", [P, CH]) for s in range(2)]
        y = [pb(f"y_{s}", [P, CH]) for s in range(2)]
        tx = [pb(f"tx{s}", [P, CH]) for s in range(2)]
        tz = [pb(f"tz{s}", [P, CH]) for s in range(2)]

        raw_ready, act_go, pool_go = sem("raw_ready"), sem("act_go"), sem("pool_go")
        hi_gu, hi_down, lo_gu, lo_gu_pool, lo_down = sem("hi_gu"), sem("hi_down"), sem("lo_gu"), sem("lo_gu_pool"), sem("lo_down")
        from_ready, to_ready = sem("from_ready"), sem("to_ready")
        gathered, gathered_start = zip(*[m.gpsimd_dma_semaphore(f"gathered{s}", 16 * len(range(s, NB, RING))) for s in range(RING)])
        scattered, scattered_start = m.gpsimd_dma_semaphore("scattered", NB * 16)
        tx_done, tx_hi, tx_lo = sem("tx_done"), sem("tx_hi"), sem("tx_lo")
        gu_done, silu_done, z_done = sem("b_gu_done"), sem("b_silu_done"), sem("b_z_done")
        tz_done, tz_hi, tz_lo = sem("tz_done"), sem("tz_hi"), sem("tz_lo")
        y_done, y_out = sem("b_y_done"), sem("y_out")

        def there(b):
            return not isinstance(b, int) or 0 <= b < NB

        def split(b):
            return not isinstance(b, int) or 0 < b < NB

        def run(eng, step):
            for b in range(-3, 2 * RING):
                step(b, b)
            full = (NB - 3) // RING
            with eng.Fori(2, full) as i:
                for c in range(RING):
                    step(i * RING + c, c)
            for b in range(full * RING, NB + 3):
                step(b, b)

        def xt(half, s, k):
            return half[:, k, s * P:(s + 1) * P]

        block = ctx.enter_context(nc.Block())

        @block.sync
        def _(sp):
            def announce(slot, loads):
                sp.wait_ge(raw_in[slot], loads)
                sp.sem_inc(raw_ready, 1)

            def refill(e, slot, loads):
                end = sp.value_load(first_of[0:1, bass.ds(e - RAW + 1, 1)], min_val=0, max_val=NB)
                sp.wait_ge(lo_down, end)
                sp.wait_ge(lo_gu_pool, end)
                load_raw(sp, slot, e + 1)
                announce(slot, loads)

            sp.wait_ge(gathered[2], 16 + gathered_start[2])
            for e in range(EARLY, RAW):
                load_raw(sp, e, e + 1)
            for e in range(RAW):
                announce(e, 64 if e == EARLY - 1 else 32)
            with sp.Fori(1, E // RAW) as i:
                for s in range(RAW):
                    refill(i * RAW + s, s, i * 32 + (64 if s == EARLY - 1 else 32))
            for e in range(E // RAW * RAW, E):
                refill(e, e % RAW, 32 * (e // RAW + 1) + (32 if e % RAW == EARLY - 1 else 0))
            sp.wait_ge(scattered, 16 * NB + scattered_start)
            m.load_x(sp, acc_rows)

        @block.gpsimd
        def _(pool):
            def step(b, c):
                if split(b + 1):
                    at = pool.value_load(raw_at[0:1, bass.ds(b + 1, 1)], min_val=0, max_val=(RAW - 1) * W_COLS)
                if there(b + 3):
                    if some(b):
                        pool.wait_ge(z_done, b)
                    pool.sem_inc(pool_go, 1)
                    s = (c + 3) % RING
                    nc.gpsimd.tensor_copy(from_row[s][:, :], token_of[:, bass.ds(b + 3, 1)]).then_inc(from_ready, 1)
                    pool.wait_ge(from_ready, b + 4)
                    pool.sem_inc(pool_go, 1)
                    pool.indirect_dma_start(rows[s][:, :], None, xn_rows, bass.IndirectOffsetOnAxis(
                        ap=from_row[s][:, :].bitcast(U32), axis=0)).then_inc(gathered[s], 16)
                if split(b + 1):
                    pool.wait_ge(hi_gu, b + 1)
                    pool.sem_inc(pool_go, 1)
                    s = (c + 1) % 2
                    nc.gpsimd.tensor_tensor(w_lo[s][:, DVE_COLS:GU_COLS], raw[:, bass.ds(at + DVE_COLS, GU_COLS - DVE_COLS)],
                                            w_hi[s][:, DVE_COLS:GU_COLS].bitcast(F32), ALU.subtract).then_inc(lo_gu_pool, 1)
                if there(b - 3):
                    if some(b - 3):
                        pool.wait_ge(scattered, (b - 3) * 16 + scattered_start)
                    pool.sem_inc(pool_go, 1)
                    nc.gpsimd.tensor_copy(to_row[:, :], token_of[:, bass.ds(b - 3, 1)]).then_inc(to_ready, 1)
                    pool.wait_ge(to_ready, b - 2)
                    pool.wait_ge(y_out, b - 2)
                    pool.sem_inc(pool_go, 1)
                    pool.indirect_dma_start(acc_rows, bass.IndirectOffsetOnAxis(ap=to_row[:, :].bitcast(U32), axis=0),
                                            out_rows[(c - 3) % 2][:, :], None, compute_op=ALU.add).then_inc(scattered, 16)

            pool.sem_inc(lo_gu_pool, 1)
            run(pool, step)

        @block.tensor
        def _(pe):
            def step(b, c):
                s = c % 2
                if there(b):
                    pe.wait_ge(tx_lo, b + 1)
                    if split(b):
                        pe.wait_ge(lo_gu, b)
                        pe.wait_ge(lo_gu_pool, b + 1)
                    if some(b - 1):
                        pe.wait_ge(z_done, b - 1)
                    product(nc, gu[s][:, :], [(xt(m.xt_hi, s, k), xt(m.xt_lo, s, k), gu_w(w_hi[s], k), gu_w(w_lo[s], k))
                                              for k in range(KT)]).then_inc(gu_done, 1)
                if there(b + 2):
                    r = (c + 2) % RING
                    pe.wait_ge(gathered[r], gather_count(b, c))
                    if some(b + 1):
                        pe.wait_ge(tx_lo, b + 1)
                    for k in range(KT):
                        last = nc.tensor.transpose(tx[s][:, k * P:(k + 1) * P], rows[r][:, k * P:(k + 1) * P], m.ident[:, :])
                    last.then_inc(tx_done, 1)
                if there(b - 1):
                    pe.wait_ge(z_done, b)
                    if some(b - 2):
                        pe.wait_ge(tz_lo, b - 2)
                    for j in range(IT):
                        last = nc.tensor.transpose(tz[1 - s][:, j * P:(j + 1) * P], z[1 - s][:, j * P:(j + 1) * P], m.ident[:, :])
                    last.then_inc(tz_done, 1)
                if there(b - 2):
                    pe.wait_ge(tz_lo, b - 1)
                    if split(b - 2):
                        pe.wait_ge(lo_down, b - 1)
                    if some(b - 3):
                        pe.wait_ge(y_out, b - 3)
                    product(nc, y[s][:, :], [(zt_hi[s][:, j * P:(j + 1) * P], zt_lo[s][:, j * P:(j + 1) * P],
                                              down_w(down_hi[(c - 2) % 4], j), down_w(down_lo[(c - 2) % 4], j)) for j in range(IT)]).then_inc(y_done, 1)

            def gather_count(b, c):
                return (b + 2 - (c + 2) % RING) * (16 // RING) + (16 + gathered_start[(c + 2) % RING])

            run(pe, step)

        @block.scalar
        def _(act):
            def step(b, c):
                s = c % 2
                if split(b + 1):
                    expert = act.value_load(expert_of[0:1, bass.ds(b + 1, 1)], min_val=1, max_val=E)
                    at = act.value_load(raw_at[0:1, bass.ds(b + 1, 1)], min_val=0, max_val=(RAW - 1) * W_COLS)
                if split(b + 1):
                    act.wait_ge(raw_ready, expert)
                    if some(b):
                        act.wait_ge(gu_done, b)
                    act.sem_inc(act_go, 1)
                    nc.scalar.copy(w_hi[1 - s][:, 0:GU_COLS], raw[:, bass.ds(at, GU_COLS)]).then_inc(hi_gu, 1)
                    if some(b - 2):
                        act.wait_ge(y_done, b - 2)
                    act.sem_inc(act_go, 1)
                    nc.scalar.copy(down_hi[(c + 1) % 4], raw[:, bass.ds(at + GU_COLS, W_COLS - GU_COLS)].rearrange("p (i h) -> p i h", i=IT)).then_inc(hi_down, 1)
                if there(b - 3):
                    act.wait_ge(y_done, b - 2)
                    if some(b - 4):
                        act.wait_ge(scattered, (b - 4) * 16 + scattered_start)
                    nc.scalar.copy(out_rows[1 - s][:, :], y[1 - s][:, :]).then_inc(y_out, 1)
                if there(b):
                    act.wait_ge(gu_done, b + 1)
                    if some(b - 1):
                        act.wait_ge(z_done, b - 1)
                    nc.scalar.activation(silu[s][:, :], gu[s][:, 0:FI], ACT.Silu).then_inc(silu_done, 1)
                if there(b + 2):
                    act.wait_ge(tx_done, b + 3)
                    if some(b + 1):
                        act.wait_ge(gu_done, b + 1)
                    nc.scalar.copy(m.xt_hi[:, :, s * P:(s + 1) * P], tx[s][:, :].rearrange("p (k c) -> p k c", k=KT)).then_inc(tx_hi, 1)
                if there(b - 1):
                    act.wait_ge(tz_done, b)
                    if some(b - 2):
                        act.wait_ge(y_done, b - 2)
                    nc.scalar.copy(zt_hi[1 - s][:, :], tz[1 - s][:, 0:FI]).then_inc(tz_hi, 1)

            run(act, step)

        @block.vector
        def _(dve):
            def step(b, c):
                s = c % 2
                if there(b):
                    column = dve.value_load(expert_of[0:1, bass.ds(b, 1)], min_val=1, max_val=E)
                if split(b + 1):
                    at = dve.value_load(raw_at[0:1, bass.ds(b + 1, 1)], min_val=0, max_val=(RAW - 1) * W_COLS)
                if split(b + 1):
                    dve.wait_ge(hi_gu, b + 1)
                    nc.vector.tensor_tensor(w_lo[1 - s][:, 0:DVE_COLS], raw[:, bass.ds(at, DVE_COLS)],
                                            w_hi[1 - s][:, 0:DVE_COLS].bitcast(F32), ALU.subtract).then_inc(lo_gu, 1)
                    dve.wait_ge(hi_down, b + 1)
                    nc.vector.tensor_tensor(down_lo[(c + 1) % 4], raw[:, bass.ds(at + GU_COLS, W_COLS - GU_COLS)].rearrange("p (i h) -> p i h", i=IT),
                                            down_hi[(c + 1) % 4].bitcast(F32), ALU.subtract).then_inc(lo_down, 1)
                if there(b):
                    dve.wait_ge(silu_done, b + 1)
                    if some(b - 1):
                        dve.wait_ge(tz_done, b - 1)
                    nc.vector.scalar_tensor_tensor(out=z[s][:, :], in0=silu[s][:, :], scalar=rows[c % RING][:, bass.ds(column + (H - 1), 1)],
                                                   in1=gu[s][:, FI:2 * FI], op0=ALU.mult, op1=ALU.mult).then_inc(z_done, 1)
                if there(b + 2):
                    dve.wait_ge(tx_hi, b + 3)
                    nc.vector.tensor_tensor(m.xt_lo[:, :, s * P:(s + 1) * P], tx[s][:, :].rearrange("p (k c) -> p k c", k=KT),
                                            m.xt_hi[:, :, s * P:(s + 1) * P].bitcast(F32), ALU.subtract).then_inc(tx_lo, 1)
                if there(b - 1):
                    dve.wait_ge(tz_hi, b)
                    nc.vector.tensor_tensor(zt_lo[1 - s][:, :], tz[1 - s][:, 0:FI], zt_hi[1 - s][:, :].bitcast(F32),
                                            ALU.subtract).then_inc(tz_lo, 1)

            dve.sem_inc(lo_down, 1)
            run(dve, step)


def butterfly_layer(m, name, out):
    nc = m.nc
    HEADS, DH, M = 16, 32, 128
    QH = P // DH
    TC = CH // P
    with ExitStack() as ctx:
        def sb(what, shape, dt=F32):
            return ctx.enter_context(nc.sbuf_tensor(f"{name}_{what}", shape, dt))

        def pb(what, shape, dt=F32):
            return ctx.enter_context(nc.psum_tensor(f"{name}_{what}", shape, dt))

        def sem(what):
            return m.semaphore(f"{name}_{what}")

        perm_row_i = sb("perm_row_i", [P, H], I32)
        perm_row = sb("perm_row", [P, H])
        perm_col_i = sb("perm_col_i", [P, KT], I32)
        perm_col = sb("perm_col", [P, KT])
        index_row = sb("index_row", [P, H])
        index_col = sb("index_col", [P, KT])
        gather = sb("gather", [P, KT, H], F32R)
        spread = sb("spread", [P, KT, H], F32R)
        up = sb("up", [P, KT, M])
        down = sb("down", [P, HEADS, DH])
        t_in = sb("t_in", [P, KT, S])
        hid = [sb(f"hid{s}", [P, QH, CH]) for s in range(2)]
        d_hi = sb("d_hi", [P, KT, S], F32R)
        d_lo = sb("d_lo", [P, KT, S], F32R)
        ups = [pb(f"ups{s}", [P, 2, CH]) for s in range(2)]
        io = [pb(f"io{s}", [P, CH]) for s in range(2)]
        dn = [pb(f"dn{s}", [P, CH]) for s in range(2)]

        nm = NormSems(sem)
        perm_in, w_in, perm_f = sem("perm_in"), sem("w_in"), sem("perm_f")
        gather_done, spread_done, out_done = sem("gather_done"), sem("spread_done"), sem("out_done")
        io_done, io_read = sem("io_done"), sem("io_read")
        up_done, gelu_done, dn_done, d_hi_done, d_lo_done = (
            sem("up_done"), sem("gelu_done"), sem("dn_done"), sem("d_hi_done"), sem("d_lo_done"))

        UNITS = NCH * KT

        def around(u):
            return KT + u - 1 if 1 <= u <= 2 * KT else None

        block = ctx.enter_context(nc.Block())

        @block.sync
        def _(sp):
            sp.dma_start(perm_row_i[:, :], m.dram["perm"].rearrange("(a h) -> a h", a=1).broadcast_to([P, H])).then_inc(perm_in, 16)
            sp.dma_start(perm_col_i[:, :], m.dram["perm_col"]).then_inc(perm_in, 16)
            sp.dma_start(index_row[:, :], m.dram["index_row"].rearrange("(a h) -> a h", a=1).broadcast_to([P, H])).then_inc(perm_in, 16)
            sp.dma_start(index_col[:, :], m.dram["index_col"]).then_inc(perm_in, 16)
            sp.dma_start(up[:, :, :], m.dram["up"]).then_inc(w_in, 16)
            sp.dma_start(down[:, :, :], m.dram["down"]).then_inc(w_in, 16)
            m.clear_stale(sp)
            if out is not None:
                for t in range(T):
                    sp.wait_ge(io_read, UNITS + t + 1)
                    sp.dma_start(out[t * P:(t + 1) * P, :], m.x[:, t, :]).then_inc(out_done, 16)
                sp.wait_ge(out_done, 16 * T)

        @block.gpsimd
        def _(pool):
            rstd_gpsimd(m, pool, nm)
            pool.wait_ge(perm_in, 64)
            nc.gpsimd.tensor_copy(perm_row[:, :], perm_row_i[:, :]).then_inc(perm_f, 1)
            nc.gpsimd.tensor_copy(perm_col[:, :], perm_col_i[:, :]).then_inc(perm_f, 1)
            pool.wait_ge(perm_f, 2)
            for k in range(KT):
                nc.gpsimd.tensor_scalar(gather[:, k, :], perm_row[:, :], index_col[:, k:k + 1], None,
                                        ALU.is_equal).then_inc(gather_done, 1)

        @block.tensor
        def _(pe):
            def columns(n):
                c, j = divmod(n, KT)
                if n >= 2:
                    pe.wait_ge(io_read, n - 1)
                for k in range(KT):
                    for half in (m.xt_hi, m.xt_lo):
                        last = nc.tensor.matmul(io[n % 2][:, :], gather[:, k, j * P:(j + 1) * P],
                                                half[:, k, c * CH:(c + 1) * CH],
                                                start=(k == 0 and half is m.xt_hi), stop=(k == KT - 1 and half is m.xt_lo))
                last.then_inc(io_done, 1)

            def outputs(n):
                t = n - UNITS
                pe.wait_ge(io_read, n - 1)
                pe.wait_ge(spread_done, KT)
                pe.wait_ge(d_lo_done, (t // TC + 1) * KT)
                for k in range(KT):
                    for half in (d_hi, d_lo):
                        last = nc.tensor.matmul(io[n % 2][:, :], half[:, k, t * P:(t + 1) * P], spread[:, k, :],
                                                start=(k == 0 and half is d_hi), stop=(k == KT - 1 and half is d_lo))
                last.then_inc(io_done, 1)

            for t in range(T):
                transpose_tile(m, pe, nm, dn[t % 2], t)
            pe.wait_ge(nm.xt_lo, T)
            pe.wait_ge(gather_done, KT)
            pe.wait_ge(w_in, 32)
            for n in range(KT):
                columns(n)
            for u in range(UNITS + 1):
                n = around(u)
                if n is not None:
                    columns(n) if n < UNITS else outputs(n)
                if u < UNITS:
                    c, j = divmod(u, KT)
                    pe.wait_ge(io_read, u + 1)
                    for r in range(QH):
                        if u >= 1 and r % 2 == 0:
                            pe.wait_ge(gelu_done, 2 * u - 1 + r // 2)
                        rows = slice(DH * r, DH * (r + 1))
                        last = nc.tensor.matmul(ups[r // 2][:, r % 2, :], up[rows, j, :], t_in[rows, j, c * CH:(c + 1) * CH],
                                                start=True, stop=True)
                        if r % 2:
                            last.then_inc(up_done, 1)
                if u >= 1:
                    v = u - 1
                    pe.wait_ge(gelu_done, 2 * v + 2)
                    if v >= 2:
                        pe.wait_ge(d_lo_done, v - 1)
                    for r in range(QH):
                        last = nc.tensor.matmul(dn[v % 2][DH * r:DH * (r + 1), :], down[:, QH * (v % KT) + r, :],
                                                hid[v % 2][:, r, :], start=True, stop=True)
                    last.then_inc(dn_done, 1)
            for n in range(UNITS + TC, UNITS + T):
                outputs(n)

        @block.scalar
        def _(act):
            for t in range(T):
                hi_tile(m, act, nm, dn[t % 2], t)
            for u in range(UNITS + 1):
                if u < UNITS:
                    for a in range(2):
                        act.wait_ge(up_done, 2 * u + a + 1)
                        if u >= 2:
                            act.wait_ge(dn_done, u - 1)
                        nc.scalar.activation(hid[u % 2][:, 2 * a:2 * a + 2, :], ups[a][:, :, :], ACT.Gelu).then_inc(gelu_done, 1)
                if u >= 1:
                    c, j = divmod(u - 1, KT)
                    act.wait_ge(dn_done, u)
                    nc.scalar.copy(d_hi[:, j, c * CH:(c + 1) * CH], dn[(u - 1) % 2][:, :]).then_inc(d_hi_done, 1)

        @block.vector
        def _(dve):
            def read(n):
                dve.wait_ge(io_done, n + 1)
                if n < UNITS:
                    c, j = divmod(n, KT)
                    nc.vector.tensor_copy(t_in[:, j, c * CH:(c + 1) * CH], io[n % 2][:, :]).then_inc(io_read, 1)
                else:
                    t = n - UNITS
                    nc.vector.scalar_tensor_tensor(out=m.x[:, t, :], in0=io[n % 2][:, :], scalar=0.5, in1=m.x[:, t, :],
                                                   op0=ALU.mult, op1=ALU.add).then_inc(io_read, 1)
                    if out is None:
                        next_stats(m, dve, io_read, n + 1, t)

            normalise_vector(m, dve, nm, lambda t: lo_tile(m, dve, nm, dn[t % 2], t))
            dve.wait_ge(perm_in, 64)
            dve.wait_ge(perm_f, 2)
            for k in range(KT):
                nc.vector.tensor_scalar(spread[:, k, :], index_row[:, :], perm_col[:, k:k + 1], None,
                                        ALU.is_equal).then_inc(spread_done, 1)
            for n in range(KT):
                read(n)
            for u in range(UNITS + 1):
                n = around(u)
                if n is not None:
                    read(n)
                if u >= 1:
                    c, j = divmod(u - 1, KT)
                    dve.wait_ge(d_hi_done, u)
                    nc.vector.tensor_tensor(d_lo[:, j, c * CH:(c + 1) * CH], dn[(u - 1) % 2][:, :],
                                            d_hi[:, j, c * CH:(c + 1) * CH].bitcast(F32), ALU.subtract).then_inc(d_lo_done, 1)
            for n in range(UNITS + TC, UNITS + T):
                read(n)


def full_attention_layer(m, name):
    nc = m.nc
    D = H // 4
    SCALE = float(D) ** -0.5
    with ExitStack() as ctx:
        def sb(what, shape, dt=F32):
            return ctx.enter_context(nc.sbuf_tensor(f"{name}_{what}", shape, dt))

        def pb(what, shape, dt=F32):
            return ctx.enter_context(nc.psum_tensor(f"{name}_{what}", shape, dt))

        def sem(what):
            return m.semaphore(f"{name}_{what}")

        w_raw = sb("w_raw", [P, KT, 3 * D])
        w_hi = sb("w_hi", [P, KT, 3 * D], F32R)
        w_lo = sb("w_lo", [P, KT, 3 * D], F32R)
        wo_raw = sb("wo_raw", [P, H])
        wo_hi = sb("wo_hi", [P, H], F32R)
        wo_lo = sb("wo_lo", [P, H], F32R)
        b_qkv = sb("b_qkv", [P, 3])
        b_out = sb("b_out", [P, H])
        qk_hi = [sb(f"{a}_hi", [P, S], F32R) for a in "qk"]
        qk_lo = [sb(f"{a}_lo", [P, S], F32R) for a in "qk"]
        vt = sb("vt", [P, S])
        v_hi = sb("v_hi", [P, S], F32R)
        v_lo = sb("v_lo", [P, S], F32R)
        top = sb("top", [P, T])
        bias = sb("bias", [P, T])
        total = sb("total", [P, T])
        inv_total = sb("inv_total", [P, T])
        prob = [sb(f"prob{s}", [P, S]) for s in range(2)]
        pt_hi = sb("pt_hi", [P, T, S], F32R)
        pt_lo = sb("pt_lo", [P, T, S], F32R)
        o_hi = sb("o_hi", [P, S], F32R)
        o_lo = sb("o_lo", [P, S], F32R)

        sc = [pb(f"sc{s}", [P, S]) for s in range(2)]
        pt = pb("pt", [P, S])
        pj = [pb(f"pj{s}", [P, CH]) for s in range(2)]

        nm = NormSems(sem)
        w_in, b_in, w_half, w_ready, x_biased = sem("w_in"), sem("b_in"), sem("w_half"), sem("w_ready"), sem("x_biased")
        pj_done, qk_hi_done, qk_read, vt_read = sem("pj_done"), sem("qk_hi_done"), sem("qk_read"), sem("vt_read")
        o_hi_done, o_read, x_done = sem("o_hi_done"), sem("o_read"), sem("x_done")
        vt_done, v_hi_done, v_lo_done = sem("vt_done"), sem("v_hi_done"), sem("v_lo_done")
        sc_done, top_done, bias_done, prob_done = sem("sc_done"), sem("top_done"), sem("bias_done"), sem("prob_done")
        pt_done, pt_hi_done, pt_lo_done = sem("pt_done"), sem("pt_hi_done"), sem("pt_lo_done")
        inv_done = sem("inv_done")
        TC = CH // P
        PROJ = 3 * NCH

        block = ctx.enter_context(nc.Block())

        @block.sync
        def _(sp):
            sp.dma_start(w_raw[:, :, :], m.dram["w1_qkv"]).then_inc(w_in, 16)
            sp.dma_start(wo_raw[:, :], m.dram["w1_out"]).then_inc(w_in, 16)
            sp.dma_start(b_qkv[:, :], m.dram["b1_qkv"]).then_inc(b_in, 16)
            sp.dma_start(b_out[:, :], m.dram["b1_out"].rearrange("(a h) -> a h", a=1).broadcast_to([P, H])).then_inc(b_in, 16)
            m.clear_stale(sp)

        @block.gpsimd
        def _(pool):
            rstd_gpsimd(m, pool, nm)
            pool.wait_ge(w_half, 2)
            nc.gpsimd.tensor_tensor(w_lo[:, :, :], w_raw[:, :, :], w_hi[:, :, :].bitcast(F32), ALU.subtract).then_inc(w_ready, 1)
            nc.gpsimd.tensor_tensor(wo_lo[:, :], wo_raw[:, :], wo_hi[:, :].bitcast(F32), ALU.subtract).then_inc(w_ready, 1)
            pool.wait_ge(b_in, 32)
            pool.wait_ge(nm.xn, T)
            nc.gpsimd.tensor_tensor(m.x[:, :, :], m.x[:, :, :], b_out[:, :].unsqueeze(1).broadcast_to([P, T, H]),
                                    ALU.add).then_inc(x_biased, 1)

        @block.tensor
        def _(pe):
            for t in range(T):
                transpose_tile(m, pe, nm, sc[t % 2][:, 0:CH], t)
            pe.wait_ge(nm.xt_lo, T)
            pe.wait_ge(w_ready, 2)
            for u in range(PROJ):
                a, c = divmod(u, NCH)
                if u >= 2:
                    pe.wait_ge(qk_read, u - 1)
                cols = slice(c * CH, (c + 1) * CH)
                product(nc, pj[u % 2][:, :], [(w_hi[:, k, a * D:(a + 1) * D], w_lo[:, k, a * D:(a + 1) * D],
                                               m.xt_hi[:, k, cols], m.xt_lo[:, k, cols]) for k in range(KT)]).then_inc(pj_done, 1)

            def scores(t):
                if t >= 2:
                    pe.wait_ge(prob_done, t - 1)
                rows = slice(t * P, (t + 1) * P)
                for c in range(NCH):
                    cols = slice(c * CH, (c + 1) * CH)
                    last = product(nc, sc[t % 2][:, cols], [(qk_hi[0][:, rows], qk_lo[0][:, rows],
                                                             qk_hi[1][:, cols], qk_lo[1][:, cols])])
                last.then_inc(sc_done, 1)

            def turn_prob(t):
                pe.wait_ge(prob_done, t + 1)
                for c in range(NCH):
                    if t >= 1:
                        pe.wait_ge(pt_lo_done, NCH * (t - 1) + c + 1)
                    for k in range(c * TC, (c + 1) * TC):
                        last = nc.tensor.transpose(pt[:, k * P:(k + 1) * P], prob[t % 2][:, k * P:(k + 1) * P], m.ident[:, :])
                    last.then_inc(pt_done, 1)

            def attend(c):
                pe.wait_ge(pt_lo_done, NCH * TC * (c + 1))
                cols = slice(c * CH, (c + 1) * CH)
                product(nc, pj[c][:, :], [(v_hi[:, k * D:(k + 1) * D], v_lo[:, k * D:(k + 1) * D],
                                           pt_hi[:, k, cols], pt_lo[:, k, cols]) for k in range(T)]).then_inc(pj_done, 1)

            pe.wait_ge(qk_read, 2 * NCH)
            scores(0)
            pe.wait_ge(vt_read, NCH)
            for t in range(T):
                last = nc.tensor.transpose(pt[:, t * P:(t + 1) * P], vt[:, t * P:(t + 1) * P], m.ident[:, :])
            last.then_inc(vt_done, 1)
            for t in range(1, T):
                scores(t)
                if t == 1:
                    pe.wait_ge(v_lo_done, 1)
                turn_prob(t - 1)
                if t == TC + 2:
                    attend(0)
            turn_prob(T - 1)
            attend(1)
            for t in range(T):
                if t == 0:
                    pe.wait_ge(o_read, NCH)
                if t >= 2:
                    pe.wait_ge(x_done, t - 1)
                rows = slice(t * P, (t + 1) * P)
                product(nc, pj[t % 2][:, :], [(o_hi[:, rows], o_lo[:, rows], wo_hi[:, :], wo_lo[:, :])]).then_inc(pj_done, 1)

        @block.scalar
        def _(act):
            for t in range(T):
                hi_tile(m, act, nm, sc[t % 2][:, 0:CH], t)
                if t == 1:
                    act.wait_ge(w_in, 32)
                    nc.scalar.copy(w_hi[:, :, :], w_raw[:, :, :]).then_inc(w_half, 1)
                if t == 2:
                    nc.scalar.copy(wo_hi[:, :], wo_raw[:, :]).then_inc(w_half, 1)
            act.wait_ge(b_in, 32)
            for u in range(PROJ):
                a, c = divmod(u, NCH)
                act.wait_ge(pj_done, u + 1)
                cols = slice(c * CH, (c + 1) * CH)
                if a < 2:
                    nc.scalar.activation(qk_hi[a][:, cols], pj[u % 2][:, :], ACT.Identity, bias=b_qkv[:, a:a + 1]).then_inc(qk_hi_done, 1)
                else:
                    nc.scalar.activation(vt[:, cols], pj[u % 2][:, :], ACT.Identity, bias=b_qkv[:, a:a + 1]).then_inc(vt_read, 1)

            def probabilities(t):
                act.wait_ge(bias_done, t + 1)
                if t >= 2:
                    act.wait_ge(pt_done, NCH * (t - 1))
                nc.scalar.activation(prob[t % 2][:, :], sc[t % 2][:, :], ACT.Exp, bias=bias[:, t:t + 1], scale=SCALE,
                                     accum_out=total[:, t:t + 1]).then_inc(prob_done, 1)

            def upper(t):
                for c in range(NCH):
                    act.wait_ge(pt_done, NCH * t + c + 1)
                    nc.scalar.copy(pt_hi[:, c * TC:(c + 1) * TC, t * P:(t + 1) * P],
                                   pt[:, c * CH:(c + 1) * CH].rearrange("p (k c) -> p k c", k=TC)).then_inc(pt_hi_done, 1)

            act.wait_ge(vt_done, 1)
            nc.scalar.copy(v_hi[:, :], pt[:, :]).then_inc(v_hi_done, 1)
            probabilities(0)
            for t in range(1, T):
                probabilities(t)
                upper(t - 1)
            upper(T - 1)
            for c in range(NCH):
                act.wait_ge(pj_done, PROJ + c + 1)
                nc.scalar.copy(o_hi[:, c * CH:(c + 1) * CH], pj[c][:, :]).then_inc(o_hi_done, 1)

        @block.vector
        def _(dve):
            normalise_vector(m, dve, nm, lambda t: lo_tile(m, dve, nm, sc[t % 2][:, 0:CH], t))
            for u in range(2 * NCH):
                a, c = divmod(u, NCH)
                dve.wait_ge(qk_hi_done, u + 1)
                cols = slice(c * CH, (c + 1) * CH)
                nc.vector.scalar_tensor_tensor(out=qk_lo[a][:, cols], in0=pj[u % 2][:, :], scalar=b_qkv[:, a:a + 1],
                                               in1=qk_hi[a][:, cols].bitcast(F32), op0=ALU.add, op1=ALU.subtract).then_inc(qk_read, 1)

            def maximum(t):
                dve.wait_ge(sc_done, t + 1)
                nc.vector.tensor_reduce(top[:, t:t + 1], sc[t % 2][:, :], AX.X, ALU.max).then_inc(top_done, 1)
                dve.wait_ge(top_done, t + 1)
                nc.vector.tensor_scalar(bias[:, t:t + 1], top[:, t:t + 1], -SCALE, None, ALU.mult).then_inc(bias_done, 1)

            def lower(t):
                cols = slice(t * P, (t + 1) * P)
                for c in range(NCH):
                    dve.wait_ge(pt_hi_done, NCH * t + c + 1)
                    keys = slice(c * TC, (c + 1) * TC)
                    nc.vector.tensor_tensor(pt_lo[:, keys, cols], pt[:, c * CH:(c + 1) * CH].rearrange("p (k c) -> p k c", k=TC),
                                            pt_hi[:, keys, cols].bitcast(F32), ALU.subtract).then_inc(pt_lo_done, 1)

            maximum(0)
            dve.wait_ge(v_hi_done, 1)
            nc.vector.tensor_tensor(v_lo[:, :], pt[:, :], v_hi[:, :].bitcast(F32), ALU.subtract).then_inc(v_lo_done, 1)
            for t in range(1, T):
                maximum(t)
                lower(t - 1)
            lower(T - 1)
            dve.wait_ge(prob_done, T)
            nc.vector.reciprocal(inv_total[:, :], total[:, :]).then_inc(inv_done, 1)
            for c in range(NCH):
                dve.wait_ge(o_hi_done, c + 1)
                cols = slice(c * CH, (c + 1) * CH)
                nc.vector.tensor_tensor(o_lo[:, cols], pj[c][:, :], o_hi[:, cols].bitcast(F32), ALU.subtract).then_inc(o_read, 1)
            dve.wait_ge(inv_done, 1)
            dve.wait_ge(x_biased, 1)
            for t in range(T):
                dve.wait_ge(pj_done, PROJ + NCH + t + 1)
                nc.vector.scalar_tensor_tensor(out=m.x[:, t, :], in0=pj[t % 2][:, :], scalar=inv_total[:, t:t + 1],
                                               in1=m.x[:, t, :], op0=ALU.mult, op1=ALU.add).then_inc(x_done, 1)
                next_stats(m, dve, x_done, t + 1, t)


def causal_attention_layer(m, name):
    nc = m.nc
    HD, KV, QPK = 16, 8, 4
    HEADS = KV * QPK
    SCALE = 1.0 / HD
    QK_ROWS = (KV + HEADS) * HD
    Q_PART = (0, 0, 1, 0, 1, 2)
    K_PART = (0, 1, 0, 2, 1, 0)
    STACK = len(Q_PART) * HD
    MROWS = 3
    with ExitStack() as outer:
        def sem(what):
            return m.semaphore(f"{name}_{what}")

        parts_dram = nc.dram_tensor(f"{name}_parts", [3, QK_ROWS, S], BF16, kind="Internal").ap()
        v_all = outer.enter_context(nc.sbuf_tensor(f"{name}_v_all", [P, T, KV, 2 * HD], F32))
        ks = outer.enter_context(nc.sbuf_tensor(f"{name}_ks", [P, KV * S], BF16))

        with ExitStack() as ctx:
            def sb(what, shape, dt=F32):
                return ctx.enter_context(nc.sbuf_tensor(f"{name}_{what}", shape, dt))

            def pb(what, shape, dt=F32):
                return ctx.enter_context(nc.psum_tensor(f"{name}_{what}", shape, dt))

            WQ = (HEADS + 2 * KV) * HD
            w_raw = sb("w_raw", [P, KT, WQ])
            w_hi = sb("w_hi", [P, KT, WQ], F32R)
            w_lo = sb("w_lo", [P, KT, WQ], F32R)
            b_qkv = sb("b_qkv", [P, WQ // P])
            cos = sb("cos", [P, S])
            sin = sb("sin", [P, S])
            swap_raw = sb("swap_raw", [P, P])
            swap = sb("swap", [P, P], F32R)
            q_hi = [sb(f"q_hi{s}", [P, CH], F32R) for s in range(2)]
            q_lo = [sb(f"q_lo{s}", [P, CH], F32R) for s in range(2)]
            with_cos = [sb(f"with_cos{s}", [P, CH]) for s in range(2)]
            with_sin = [sb(f"with_sin{s}", [P, CH]) for s in range(2)]
            turned = [sb(f"turned{s}", [P, CH]) for s in range(2)]
            rest = [sb(f"rest{s}", [P, CH]) for s in range(2)]
            NPB = 4
            part = [sb(f"part{s}", [P, 3, CH], BF16) for s in range(NPB)]
            vt = sb("vt", [P, S])
            xp = [pb(f"xp{s}", [P, CH]) for s in range(2)]
            pj = [pb(f"pj{s}", [P, CH]) for s in range(2)]
            rot = [pb(f"rot{s}", [P, CH]) for s in range(2)]

            nm = NormSems(sem)
            w_in, c_in, w_half, w_ready, v_init = sem("w_in"), sem("c_in"), sem("w_half"), sem("w_ready"), sem("v_init")
            pj_done, hi_done, lo_done, cos_done, rot_done, sin_done = (
                sem("pj_done"), sem("hi_done"), sem("lo_done"), sem("cos_done"), sem("rot_done"), sem("sin_done"))
            turned_done, p1_done, rest_done, p2_done, p3_done = (
                sem("turned_done"), sem("p1_done"), sem("rest_done"), sem("p2_done"), sem("p3_done"))
            v_read, vt_done, v_done = sem("v_read"), sem("vt_done"), sem("v_done")
            part_out = [sem(f"part_out{s}") for s in range(NPB)]

            UNITS = WQ // P * NCH
            V_UNITS = (UNITS - NCH, UNITS)
            TURN = [n for n in range(UNITS) if not V_UNITS[0] <= n < V_UNITS[1]]
            number = {n: r for r, n in enumerate(TURN)}

            with nc.Block() as block:
                @block.sync
                def _(sp):
                    sp.dma_start(w_raw[:, :, :], m.dram["w_qkv"]).then_inc(w_in, 16)
                    sp.dma_start(swap_raw[:, :], m.dram["swap"]).then_inc(w_in, 16)
                    sp.dma_start(b_qkv[:, :], m.dram["b_qkv"]).then_inc(c_in, 16)
                    sp.dma_start(cos[:, :], m.dram["cos"]).then_inc(c_in, 16)
                    sp.dma_start(sin[:, :], m.dram["sin"]).then_inc(c_in, 16)
                    m.clear_stale(sp)
                    for n in TURN:
                        j, c = divmod(n, NCH)
                        r = number[n]
                        row = j * P
                        sp.wait_ge(p3_done, r + 1)
                        sp.dma_start(parts_dram[:, row:row + P, c * CH:(c + 1) * CH].rearrange("a p s -> p a s"),
                                     part[r % NPB][:, :, :]).then_inc(part_out[r % NPB], 16)
                    for s in range(NPB):
                        sp.wait_ge(part_out[s], 16 * len(range(s, len(TURN), NPB)))

                @block.gpsimd
                def _(pool):
                    rstd_gpsimd(m, pool, nm)
                    nc.gpsimd.memset(v_all[:, :, :, :], 0.0).then_inc(v_init, 1)
                    for k in range(KT):
                        pool.wait_ge(w_half, k + 1)
                        nc.gpsimd.tensor_tensor(w_lo[:, k, :], w_raw[:, k, :], w_hi[:, k, :].bitcast(F32),
                                                ALU.subtract).then_inc(w_ready, 1)
                    pool.wait_ge(v_init, 1)
                    nc.gpsimd.memset(v_all[:, :, :, HD:HD + 1], 1.0).then_inc(v_init, 1)
                    pool.wait_ge(v_init, 2)
                    nc.gpsimd.memset(ks[STACK:STACK + MROWS, :], 1.0).then_inc(v_init, 1)
                    pool.wait_ge(v_init, 3)
                    for n in range(UNITS + 3):
                        if n - 1 in number:
                            r = number[n - 1]
                            pool.wait_ge(sin_done, r + 1)
                            if r >= 2:
                                pool.wait_ge(rest_done, r - 1)
                            nc.gpsimd.tensor_tensor(turned[r % 2][:, :], with_cos[r % 2][:, :], with_sin[r % 2][:, :],
                                                    ALU.add).then_inc(turned_done, 1)
                        if n - 2 in number:
                            r = number[n - 2]
                            pool.wait_ge(p1_done, r + 1)
                            if r >= 2:
                                pool.wait_ge(p3_done, r - 1)
                            nc.gpsimd.tensor_tensor(rest[r % 2][:, :], turned[r % 2][:, :], part[r % NPB][:, 0, :],
                                                    ALU.subtract).then_inc(rest_done, 1)

                @block.tensor
                def _(pe):
                    for t in range(T):
                        transpose_tile(m, pe, nm, xp[t % 2], t)
                    pe.wait_ge(nm.xt_lo, T)
                    pe.wait_ge(w_ready, KT)
                    pe.wait_ge(w_half, KT + 1)
                    for n in range(UNITS + 1):
                        if n < UNITS:
                            j, c = divmod(n, NCH)
                            if n - 2 in number:
                                pe.wait_ge(cos_done, number[n - 2] + 1)
                            elif n >= 2:
                                pe.wait_ge(v_read, n - 2 - V_UNITS[0] + 1)
                            cols = slice(c * CH, (c + 1) * CH)
                            feats = slice(j * P, (j + 1) * P)
                            product(nc, pj[n % 2][:, :], [(w_hi[:, k, feats], w_lo[:, k, feats], m.xt_hi[:, k, cols],
                                                           m.xt_lo[:, k, cols]) for k in range(KT)]).then_inc(pj_done, 1)
                        if n - 1 in number:
                            r = number[n - 1]
                            pe.wait_ge(lo_done, r + 1)
                            if r >= 2:
                                pe.wait_ge(sin_done, r - 1)
                            nc.tensor.matmul(rot[r % 2][:, :], swap[:, :], q_hi[r % 2][:, :], start=True, stop=False)
                            nc.tensor.matmul(rot[r % 2][:, :], swap[:, :], q_lo[r % 2][:, :], start=False,
                                             stop=True).then_inc(rot_done, 1)
                        elif n == V_UNITS[1]:
                            pe.wait_ge(v_read, NCH)
                            for t in range(T):
                                last = nc.tensor.transpose(xp[t * P // CH][:, t * P % CH:t * P % CH + P],
                                                           vt[:, t * P:(t + 1) * P], m.ident[:, :])
                            last.then_inc(vt_done, 1)

                @block.scalar
                def _(act):
                    for t in range(T):
                        hi_tile(m, act, nm, xp[t % 2], t)
                        if 1 <= t <= KT:
                            if t == 1:
                                act.wait_ge(w_in, 32)
                            nc.scalar.copy(w_hi[:, t - 1, :], w_raw[:, t - 1, :]).then_inc(w_half, 1)
                    nc.scalar.copy(swap[:, :], swap_raw[:, :]).then_inc(w_half, 1)
                    act.wait_ge(c_in, 48)
                    for n in range(UNITS + 4):
                        if n < UNITS:
                            j, c = divmod(n, NCH)
                            act.wait_ge(pj_done, n + 1)
                            if n in number:
                                r = number[n]
                                if r >= 2:
                                    act.wait_ge(rot_done, r - 1)
                                nc.scalar.activation(q_hi[r % 2][:, :], pj[n % 2][:, :], ACT.Identity,
                                                     bias=b_qkv[:, j:j + 1]).then_inc(hi_done, 1)
                            else:
                                nc.scalar.activation(vt[:, c * CH:(c + 1) * CH], pj[n % 2][:, :], ACT.Identity,
                                                     bias=b_qkv[:, j:j + 1]).then_inc(v_read, 1)
                        if n - 2 in number:
                            r = number[n - 2]
                            act.wait_ge(turned_done, r + 1)
                            if r >= NPB:
                                act.wait_ge(part_out[r % NPB], 16 * (r // NPB))
                            nc.scalar.copy(part[r % NPB][:, 0, :], turned[r % 2][:, :]).then_inc(p1_done, 1)
                        if n - 3 in number:
                            r = number[n - 3]
                            act.wait_ge(rest_done, r + 1)
                            nc.scalar.copy(part[r % NPB][:, 1, :], rest[r % 2][:, :]).then_inc(p2_done, 1)

                @block.vector
                def _(dve):
                    normalise_vector(m, dve, nm, lambda t: lo_tile(m, dve, nm, xp[t % 2], t))
                    dve.wait_ge(c_in, 48)
                    for n in range(UNITS + 4):
                        j, c = divmod(n, NCH)
                        cols = slice(c * CH, (c + 1) * CH)
                        if n in number:
                            r = number[n]
                            dve.wait_ge(hi_done, r + 1)
                            nc.vector.scalar_tensor_tensor(out=q_lo[r % 2][:, :], in0=pj[n % 2][:, :], scalar=b_qkv[:, j:j + 1],
                                                           in1=q_hi[r % 2][:, :].bitcast(F32), op0=ALU.add,
                                                           op1=ALU.subtract).then_inc(lo_done, 1)
                            if r >= 2:
                                dve.wait_ge(turned_done, r - 1)
                            nc.vector.scalar_tensor_tensor(out=with_cos[r % 2][:, :], in0=pj[n % 2][:, :],
                                                           scalar=b_qkv[:, j:j + 1], in1=cos[:, cols], op0=ALU.add,
                                                           op1=ALU.mult).then_inc(cos_done, 1)
                        if n - 1 in number:
                            r = number[n - 1]
                            c = (n - 1) % NCH
                            dve.wait_ge(rot_done, r + 1)
                            nc.vector.tensor_tensor(with_sin[r % 2][:, :], rot[r % 2][:, :], sin[:, c * CH:(c + 1) * CH],
                                                    ALU.mult).then_inc(sin_done, 1)
                        if n - 3 in number:
                            r = number[n - 3]
                            dve.wait_ge(p2_done, r + 1)
                            nc.vector.tensor_tensor(part[r % NPB][:, 2, :], rest[r % 2][:, :], part[r % NPB][:, 1, :],
                                                    ALU.subtract).then_inc(p3_done, 1)
                        if n == V_UNITS[1] + 1:
                            dve.wait_ge(vt_done, 1)
                            dve.wait_ge(v_init, 2)
                            for c in range(NCH):
                                nc.vector.tensor_copy(v_all[:, c * (CH // P):(c + 1) * (CH // P), :, 0:HD],
                                                      xp[c][:, :].rearrange("p (t g d) -> p t g d", t=CH // P, g=KV)).then_inc(v_done, 1)

        with ExitStack() as ctx:
            def sb(what, shape, dt=F32):
                return ctx.enter_context(nc.sbuf_tensor(f"{name}_{what}", shape, dt))

            def pb(what, shape, dt=F32):
                return ctx.enter_context(nc.psum_tensor(f"{name}_{what}", shape, dt))

            BANKS = 3
            QG = QPK * S
            TC = CH // P
            qs = sb("qs", [P, HEADS * S], BF16)
            v_now = sb("v_now", [P, T, 2 * HD])
            masks = sb("masks", [P, 2, P])
            mask_qk = sb("mask_qk", [P, P], BF16)
            mask_kq = sb("mask_kq", [P, P], BF16)
            ident = sb("ident", [P, P], BF16)
            warm = sb("warm", [1, 1])
            top = sb("top", [P, NCH, T, QPK])
            best = sb("best", [P, TC, QPK])
            neg = sb("neg", [P, TC, QPK])
            left = sb("left", [P, TC, QPK])
            neg_parts = [sb(f"neg_parts{h}", [P, TC, MROWS, QPK], BF16) for h in range(NCH)]
            neg_turned = [sb(f"neg_turned{h}", [MROWS * QPK, CH], BF16) for h in range(NCH)]
            prob = [sb(f"prob{s}", [P, QPK, CH]) for s in range(2)]
            out_t = sb("out_t", [P, CH])
            inv = sb("inv", [P, TC, QPK])
            sc = [pb(f"sc{s}", [P, CH]) for s in range(BANKS)]
            mx = [pb(f"mx{s}", [P, CH]) for s in range(BANKS)]
            po = pb("po", [P, CH])
            small = pb("small", [P, 2 * CH], BF16)
            small_f = small[:, :].bitcast(F32)

            c_in2, consts, stack_in, first_q_in = sem("c_in2"), sem("consts"), sem("stack_in"), sem("first_q_in")
            mx_done, mx_read, neg_chain, neg_done, neg_turn, neg_read = (
                sem("mx_done"), sem("mx_read"), sem("neg_chain"), sem("neg_done"), sem("neg_turn"), sem("neg_read"))
            neg_in = [m.gpsimd_dma_semaphore(f"neg_in{h}", KV * MROWS * 16)[0] for h in range(NCH)]
            sc_done, exp_done, v_ready, pv_done = sem("sc_done"), sem("exp_done"), sem("v_ready"), sem("pv_done")
            po_read, out_turn, inv_done, ctx_done = sem("po_read"), sem("out_turn"), sem("inv_done"), sem("ctx_done")

            MAX_UNITS = [(t, kc, h) for t in range(T) for h in range(QPK) for kc in range(t * P // CH + 1)]
            NMU = len(MAX_UNITS)
            HALF0 = sum(t < TC for t, _, _ in MAX_UNITS)
            STEPS = [(0, kb) for kb in range(TC)] + [(1, half * TC + kb) for kb in range(TC) for half in range(2)]
            NS = len(STEPS)
            UPS = NMU // NS
            C0 = TC
            NEG_OPS = (4, 5)
            LOADS = 2 * len(Q_PART)

            with nc.Block() as block:
                @block.sync
                def _(sp):
                    def load(g):
                        for a in range(len(Q_PART)):
                            rows = slice(a * HD, (a + 1) * HD)
                            sp.dma_start(ks[rows, bass.ds(g * S, S)],
                                         parts_dram[K_PART[a], bass.ds(g * HD, HD), :]).then_inc(stack_in, 16)
                            sp.dma_start(qs[rows, bass.ds(g * QG, QG)].rearrange("d (h s) -> d h s", h=QPK),
                                         parts_dram[Q_PART[a], bass.ds(g * (QPK * HD) + KV * HD, QPK * HD), :].rearrange(
                                             "(h d) s -> d h s", h=QPK)).then_inc(stack_in, 16)

                    for a in range(len(Q_PART)):
                        sp.dma_start(ks[a * HD:(a + 1) * HD, 0:S], parts_dram[K_PART[a], 0:HD, :]).then_inc(stack_in, 16)
                    with sp.Fori(1, KV) as g:
                        sp.wait_ge(stack_in, g * (16 * LOADS) - 16 * LOADS // 2)
                        load(g)

                @block.gpsimd
                def _(pool):
                    def put_maxima(gn, h):
                        pool.wait_ge(neg_read, gn * NCH + h + 1)
                        for a in range(MROWS):
                            pool.dma_start(qs[STACK + a:STACK + a + 1, bass.ds(gn * QG, QG)].rearrange(
                                "a (h s) -> a h s", h=QPK)[:, :, h * CH:(h + 1) * CH],
                                neg_turned[h][a * QPK:(a + 1) * QPK, :]).then_inc(neg_in[h], 16)

                    def values(g):
                        pool.wait_ge(pv_done, g * NS + 1)
                        nc.gpsimd.tensor_copy(v_now[:, :, :], v_all[:, :, bass.ds(g, 1), :].rearrange(
                            "p t a d -> p t (a d)")).then_inc(v_ready, 1)

                    for h in range(NCH):
                        put_maxima(0, h)
                    values(0)
                    put_maxima(1, 0)
                    with pool.Fori(1, KV - 1) as g:
                        values(g)
                        put_maxima(g, 1)
                        put_maxima(g + 1, 0)
                    values(KV - 1)
                    put_maxima(KV - 1, 1)

                @block.tensor
                def _(pe):
                    def maximum(gn, i):
                        t, kc, h = MAX_UNITS[i]
                        mu = gn * NMU + i
                        if i == 0:
                            pe.wait_ge(stack_in, gn * (16 * LOADS) + 16 * LOADS // 2)
                            if isinstance(gn, int):
                                pe.wait_ge(first_q_in, 16 * LOADS // 2)
                        if some(mu - (BANKS - 1)):
                            pe.wait_ge(mx_read, mu - (BANKS - 1))
                        w = min(CH, (t + 1) * P - kc * CH)
                        diagonal = t * P < (kc + 1) * CH
                        at = gn * QG + (h * S + t * P)
                        last = nc.tensor.matmul(mx[i % BANKS][:, 0:w], qs[0:STACK, bass.ds(at, P)],
                                                ks[0:STACK, bass.ds(gn * S + kc * CH, w)], start=True, stop=not diagonal)
                        if diagonal:
                            last = nc.tensor.matmul(mx[i % BANKS][:, w - P:w], ident[:, :], mask_qk[:, :], start=False, stop=True)
                        last.then_inc(mx_done, 1)

                    def turn_maxima(gn, h):
                        pe.wait_ge(neg_done, gn * NCH + h + 1)
                        if not isinstance(gn, int) or gn * NCH + h >= 1:
                            pe.wait_ge(neg_read, gn * NCH + h)
                        for u in range(TC):
                            last = nc.tensor.transpose(small[0:MROWS * QPK, u * P:(u + 1) * P],
                                                       neg_parts[h][:, u, :, :].rearrange("p a h -> p (a h)"), ident[:, :])
                        last.then_inc(neg_turn, 1)

                    def scores(g, u, h):
                        c, kb = STEPS[u]
                        pe.wait_ge(exp_done, g * (NS * QPK) + (u * QPK + h + 1))
                        o = max(0, kb * P - c * CH)
                        diagonal = kb * P >= c * CH
                        b = (u * QPK + h) % BANKS
                        nc_last = nc.tensor.matmul(sc[b][:, o:CH], ks[0:STACK + MROWS, bass.ds(g * S + kb * P, P)],
                                                   qs[0:STACK + MROWS, bass.ds(g * QG + (h * S + c * CH + o), CH - o)],
                                                   start=True, stop=not diagonal)
                        if diagonal:
                            nc_last = nc.tensor.matmul(sc[b][:, o:o + P], ident[:, :], mask_kq[:, :], start=False, stop=True)
                        nc_last.then_inc(sc_done, 1)

                    def values(g, u):
                        c, kb = STEPS[u]
                        pe.wait_ge(exp_done, g * (NS * QPK) + ((u + 1) * QPK + BANKS))
                        if u == 0:
                            pe.wait_ge(v_ready, g + 1)
                        if kb == 0:
                            pe.wait_ge(po_read, g * NCH + (c + 1))
                        o = max(0, kb * P - c * CH)
                        for h in range(QPK):
                            last = nc.tensor.matmul(po[2 * HD * h:2 * HD * (h + 1), o:CH], v_now[:, kb, :],
                                                    prob[u % 2][:, h, o:CH], start=(kb == 0), stop=(kb == (c + 1) * TC - 1))
                        last.then_inc(pv_done, 1)

                    def turn_output(g, c):
                        pe.wait_ge(po_read, g * NCH + (c + 2))
                        for u in range(TC):
                            last = nc.tensor.transpose(small_f[:, u * P:(u + 1) * P], out_t[:, u * P:(u + 1) * P], m.ident[:, :])
                        last.then_inc(out_turn, 1)

                    def group(g, first, more):
                        for u in range(NS):
                            if u == 0 or u == C0:
                                pe.wait_ge(neg_in[STEPS[u][0]], g * (16 * MROWS) + 16 * MROWS)
                            for h in range(QPK):
                                scores(g, u, h)
                                if more:
                                    maximum(g + 1, UPS * u + h)
                                if h == 2 and u >= 1:
                                    values(g, u - 1)
                                elif h == 2 and not first:
                                    values(g - 1, NS - 1)
                            if u == 0 and not first:
                                pe.wait_ge(ctx_done, g * NCH)
                                turn_maxima(g, 1)
                            if u == 1 and not first:
                                pe.wait_ge(neg_read, g * NCH + 2)
                                turn_output(g - 1, 1)
                            if u == C0 + 1 and more:
                                pe.wait_ge(ctx_done, g * NCH + 1)
                                turn_maxima(g + 1, 0)
                            if u == C0 + 4:
                                if more:
                                    pe.wait_ge(neg_read, g * NCH + NCH + 1)
                                turn_output(g, 0)

                    pe.sem_inc(pv_done, 1)
                    pe.sem_inc(out_turn, 1)
                    pe.wait_ge(consts, 3)
                    for i in range(NMU):
                        maximum(0, i)
                        if i == HALF0 + 1:
                            turn_maxima(0, 0)
                    turn_maxima(0, 1)
                    group(0, True, True)
                    with pe.Fori(1, KV - 1) as g:
                        group(g, False, True)
                    group(KV - 1, False, False)
                    values(KV - 1, NS - 1)
                    pe.wait_ge(ctx_done, KV * NCH)
                    turn_output(KV - 1, 1)

                @block.scalar
                def _(act):
                    def read_maxima(gn, h):
                        act.wait_ge(neg_turn, gn * NCH + h + 1)
                        if not isinstance(gn, int) or gn:
                            act.wait_ge(neg_in[h], gn * (16 * MROWS))
                        nc.scalar.copy(neg_turned[h][:, :], small[0:MROWS * QPK, 0:CH]).then_inc(neg_read, 1)

                    def group(g, first, more):
                        for u in range(NS):
                            c, kb = STEPS[u]
                            o = max(0, kb * P - c * CH)
                            if some(g * NS + u):
                                act.wait_ge(pv_done, g * NS + u)
                            for h in range(QPK):
                                act.wait_ge(sc_done, g * (NS * QPK) + (u * QPK + h + 1))
                                nc.scalar.activation(prob[u % 2][:, h, o:CH], sc[(u * QPK + h) % BANKS][:, o:CH], ACT.Exp,
                                                     scale=SCALE).then_inc(exp_done, 1)
                                if u == 1 and h == 0 and not first:
                                    read_maxima(g, 1)
                            if u == C0 + 2 and more:
                                read_maxima(g + 1, 0)

                    act.dma_start(masks[:, :, :], m.dram["masks"]).then_inc(c_in2, 16)
                    for a in range(len(Q_PART)):
                        act.dma_start(qs[a * HD:(a + 1) * HD, 0:QG].rearrange("d (h s) -> d h s", h=QPK),
                                      parts_dram[Q_PART[a], KV * HD:KV * HD + QPK * HD, :].rearrange(
                                          "(h d) s -> d h s", h=QPK)).then_inc(first_q_in, 16)
                    nc.scalar.activation(warm[:, :], m.ident[0:1, 0:1], ACT.Exp).then_inc(exp_done, BANKS)
                    for h in range(NCH):
                        read_maxima(0, h)
                    group(0, True, True)
                    with act.Fori(1, KV - 1) as g:
                        group(g, False, True)
                    group(KV - 1, False, False)

                @block.vector
                def _(dve):
                    def maximum(gn, i):
                        t, kc, h = MAX_UNITS[i]
                        w = min(CH, (t + 1) * P - kc * CH)
                        dve.wait_ge(mx_done, gn * NMU + (i + 1))
                        nc.vector.tensor_reduce(top[:, kc, t, h:h + 1], mx[i % BANKS][:, 0:w], AX.X, ALU.max).then_inc(mx_read, 1)

                    def split_maxima(gn, h, units):
                        base = gn * sum(NEG_OPS) + sum(NEG_OPS[:h])
                        dve.wait_ge(mx_read, gn * NMU + units)
                        k = 0
                        source = top[:, 0, 0:TC, :]
                        if h:
                            nc.vector.tensor_tensor(best[:, :, :], top[:, 0, TC:T, :], top[:, 1, TC:T, :], ALU.max).then_inc(neg_chain, 1)
                            k += 1
                            dve.wait_ge(neg_chain, base + k)
                            source = best[:, :, :]
                        nc.vector.tensor_scalar(neg[:, :, :], source, -1.0, None, ALU.mult).then_inc(neg_chain, 1)
                        k += 1
                        dve.wait_ge(neg_chain, base + k)
                        if some(gn * NCH + h - 1):
                            dve.wait_ge(neg_turn, gn * NCH + h - 1)
                        nc.vector.tensor_copy(neg_parts[h][:, :, 0, :], neg[:, :, :]).then_inc(neg_chain, 1)
                        k += 1
                        dve.wait_ge(neg_chain, base + k)
                        nc.vector.tensor_tensor(left[:, :, :], neg[:, :, :], neg_parts[h][:, :, 0, :], ALU.subtract).then_inc(neg_chain, 1)
                        k += 1
                        dve.wait_ge(neg_chain, base + k)
                        nc.vector.tensor_copy(neg_parts[h][:, :, 1, :], left[:, :, :]).then_inc(neg_chain, 1)
                        k += 1
                        dve.wait_ge(neg_chain, base + k)
                        nc.vector.tensor_tensor(neg_parts[h][:, :, 2, :], left[:, :, :], neg_parts[h][:, :, 1, :],
                                                ALU.subtract).then_inc(neg_done, 1)

                    def read_output(g, c):
                        dve.wait_ge(pv_done, g * NS + ((C0, NS)[c] + 1))
                        dve.wait_ge(out_turn, g * NCH + (c + 1))
                        nc.vector.tensor_copy(out_t[:, :], po[:, :]).then_inc(po_read, 1)

                    def normalise(g, c):
                        dve.wait_ge(out_turn, g * NCH + (c + 2))
                        o = small_f.rearrange("p (t h d) -> p t h d", t=TC, h=QPK)
                        nc.vector.reciprocal(inv[:, :, :], o[:, :, :, HD]).then_inc(inv_done, 1)
                        dve.wait_ge(inv_done, g * NCH + c + 1)
                        nc.vector.tensor_tensor(m.xn[:, c * TC:(c + 1) * TC, bass.ds(g * (QPK * HD), QPK * HD)].rearrange(
                            "p t (h d) -> p t h d", h=QPK), o[:, :, :, 0:HD],
                            inv[:, :, :].unsqueeze(3).broadcast_to([P, TC, QPK, HD]), ALU.mult).then_inc(ctx_done, 1)

                    def group(g, first, more):
                        for u in range(NS):
                            if more:
                                for i in range(UPS - 1):
                                    maximum(g + 1, UPS * u + i)
                            if u == 0 and not first:
                                read_output(g - 1, 1)
                            if u == 2 and not first:
                                normalise(g - 1, 1)
                            if u == C0:
                                read_output(g, 0)
                            if more:
                                maximum(g + 1, UPS * u + UPS - 1)
                                if UPS * (u + 1) == HALF0:
                                    split_maxima(g + 1, 0, HALF0)
                            if u == C0 + 5:
                                normalise(g, 0)
                        if more:
                            split_maxima(g + 1, 1, NMU)

                    dve.sem_inc(po_read, 1)
                    dve.sem_inc(ctx_done, 1)
                    dve.wait_ge(c_in2, 16)
                    nc.vector.tensor_copy(mask_qk[:, :], masks[:, 0, :]).then_inc(consts, 1)
                    nc.vector.tensor_copy(mask_kq[:, :], masks[:, 1, :]).then_inc(consts, 1)
                    nc.vector.tensor_copy(ident[:, :], m.ident[:, :]).then_inc(consts, 1)
                    for i in range(NMU):
                        maximum(0, i)
                        if i + 1 == HALF0:
                            split_maxima(0, 0, HALF0)
                    split_maxima(0, 1, NMU)
                    group(0, True, True)
                    with dve.Fori(1, KV - 1) as g:
                        group(g, False, True)
                    group(KV - 1, False, False)
                    read_output(KV - 1, 1)
                    normalise(KV - 1, 1)

        with ExitStack() as ctx:
            def sb(what, shape, dt=F32):
                return ctx.enter_context(nc.sbuf_tensor(f"{name}_{what}", shape, dt))

            def pb(what, shape, dt=F32):
                return ctx.enter_context(nc.psum_tensor(f"{name}_{what}", shape, dt))

            wd_raw = sb("wd_raw", [P, KT, H])
            wd_hi = sb("wd_hi", [P, KT, H], F32R)
            wd_lo = sb("wd_lo", [P, KT, H], F32R)
            b_out = sb("b_out", [P, H])
            xp = [pb(f"xpd{s}", [P, CH]) for s in range(2)]
            yp = [pb(f"yp{s}", [P, CH]) for s in range(2)]
            cm = NormSems(sem, "ctx")
            wd_in, wd_half, wd_ready, x_biased, y_done, x_done = (
                sem("wd_in"), sem("wd_half"), sem("wd_ready"), sem("x_biased"), sem("y_done"), sem("x_done"))

            with nc.Block() as block:
                @block.sync
                def _(sp):
                    sp.dma_start(wd_raw[:, :, :], m.dram["w_dense"]).then_inc(wd_in, 16)
                    sp.dma_start(b_out[:, :], m.dram["b_dense"].rearrange("(a h) -> a h", a=1).broadcast_to([P, H])).then_inc(wd_in, 16)

                @block.gpsimd
                def _(pool):
                    pool.wait_ge(wd_half, 1)
                    nc.gpsimd.tensor_tensor(wd_lo[:, :, :], wd_raw[:, :, :], wd_hi[:, :, :].bitcast(F32),
                                            ALU.subtract).then_inc(wd_ready, 1)
                    nc.gpsimd.tensor_tensor(m.x[:, :, :], m.x[:, :, :], b_out[:, :].unsqueeze(1).broadcast_to([P, T, H]),
                                            ALU.add).then_inc(x_biased, 1)

                @block.tensor
                def _(pe):
                    for t in range(T):
                        transpose_tile(m, pe, cm, xp[t % 2], t, ready=False)
                    pe.wait_ge(wd_ready, 1)
                    for t in range(T):
                        pe.wait_ge(cm.xt_lo, t + 1)
                        if t >= 2:
                            pe.wait_ge(x_done, t - 1)
                        rows = slice(t * P, (t + 1) * P)
                        product(nc, yp[t % 2][:, :], [(m.xt_hi[:, k, rows], m.xt_lo[:, k, rows], wd_hi[:, k, :], wd_lo[:, k, :])
                                                      for k in range(KT)]).then_inc(y_done, 1)

                @block.scalar
                def _(act):
                    for t in range(2):
                        hi_tile(m, act, cm, xp[t % 2], t)
                    act.wait_ge(wd_in, 32)
                    nc.scalar.copy(wd_hi[:, :, :], wd_raw[:, :, :]).then_inc(wd_half, 1)
                    for t in range(2, T):
                        hi_tile(m, act, cm, xp[t % 2], t)

                @block.vector
                def _(dve):
                    for t in range(T):
                        lo_tile(m, dve, cm, xp[t % 2], t)
                    dve.wait_ge(x_biased, 1)
                    for t in range(T):
                        dve.wait_ge(y_done, t + 1)
                        nc.vector.tensor_tensor(m.x[:, t, :], yp[t % 2][:, :], m.x[:, t, :], ALU.add).then_inc(x_done, 1)
                        next_stats(m, dve, x_done, t + 1, t)



def program(nc, m_in, out, stages):
    m = Shared()
    m.nc = nc
    m.taken, m.stale = [], []
    m.x_loads = 0
    m.kept, m.counted = {}, {}
    m.dram = m_in
    layers = {"moe": moe_layer, "causal": causal_attention_layer, "full": full_attention_layer}
    with ExitStack() as ctx:
        def sb(what, shape, dt=F32):
            return ctx.enter_context(nc.sbuf_tensor(what, shape, dt))

        m.x = sb("x", [P, T, H])
        m.xn = sb("xn", [P, T, H])
        m.xt_hi = sb("xt_hi", [P, KT, S], F32R)
        m.xt_lo = sb("xt_lo", [P, KT, S], F32R)
        m.ident = sb("ident", [P, P])
        m.stats = sb("stats", [P, T, 6])
        m.mean_var = sb("mean_var", [P, T, 2])
        m.var_eps = sb("var_eps", [P, T])
        m.minus_half = sb("minus_half", [P, T])
        m.zero = sb("zero", [P, 1])
        m.rstd = sb("rstd", [P, T])
        m.next_stats = nc.alloc_semaphore(name="next_stats")
        m.x_tile = [nc.alloc_semaphore(name=f"x_tile{t}") for t in range(T)]
        ident_in = nc.alloc_semaphore(name="ident_in")
        x_out = nc.alloc_semaphore(name="x_out")
        with nc.Block() as block:
            @block.gpsimd
            def _(pool):
                nc.gpsimd.memset(m.minus_half[:, :], -0.5)
                nc.gpsimd.memset(m.zero[:, :], 0.0)

            @block.sync
            def _(sp):
                sp.dma_start(m.ident[:, :], m.dram["identity"]).then_inc(ident_in, 16)
                m.load_x(sp, m.dram["hidden"])
                sp.wait_ge(ident_in, 16)
        m.have_stats = False
        for n, stage in enumerate(stages):
            if stage == "butter":
                butterfly_layer(m, f"{stage}{n}", out if n == len(stages) - 1 else None)
            else:
                layers[stage](m, f"{stage}{n}")
            m.release()
            m.have_stats = stage != "moe"
        if stages[-1] != "butter":
            with nc.Block() as block:
                @block.sync
                def _(sp):
                    for t in range(T):
                        sp.wait_ge(m.x_tile[t], 16 * m.x_loads)
                    sp.dma_start(out.rearrange("(t p) h -> p t h", p=P), m.x[:, :, :]).then_inc(x_out, 16)
                    sp.wait_ge(x_out, 16)


STAGES = ("moe", "causal", "moe", "butter", "full", "butter")


def layout(inputs):
    import numpy as np

    f = np.ascontiguousarray
    i = {k: np.asarray(v) for k, v in inputs.items()}
    d = {}

    def by_partition(w):
        return f(w.reshape(w.shape[0] // P, P, w.shape[1]).transpose(1, 0, 2))

    d["hidden"] = f(i["L0_attn_hidden_states"].reshape(S, H))
    gate = np.concatenate([i["L0_ffn_Sg"][None], i["L0_ffn_Wg"]])
    up = np.concatenate([i["L0_ffn_Su"][None], i["L0_ffn_Wu"]])
    down = np.concatenate([i["L0_ffn_Sd"][None], i["L0_ffn_Wd"]])
    gu = np.concatenate([gate, up], axis=1).transpose(0, 2, 1)
    d["w_gu"] = f(gu.reshape(NE, KT, P, 2 * FI).transpose(0, 2, 1, 3).reshape(NE, P, GU_COLS))
    d["w_down"] = f(down.transpose(0, 2, 1).reshape(NE, IT, P, H).transpose(0, 2, 1, 3).reshape(NE, P, IT * H))
    router = np.zeros((H, P), np.float32)
    router[:, :E] = i["L0_ffn_gate_w"].T
    d["gate_w"] = by_partition(router)
    d["gate_bias"] = f(i["L0_ffn_bias"].reshape(E, 1))
    kv, hd, qpk = 8, 16, 4
    w = i["L0_attn_w_qkv"].reshape(kv, qpk + 2, hd, H)
    b = i["L0_attn_b_qkv"].reshape(kv, qpk + 2, hd)
    w = np.concatenate([w[:, qpk].reshape(-1, H), w[:, :qpk].reshape(-1, H), w[:, qpk + 1].reshape(-1, H)])
    b = np.concatenate([b[:, qpk].reshape(-1), b[:, :qpk].reshape(-1), b[:, qpk + 1].reshape(-1)])
    d["w_qkv"] = by_partition(w.T)
    d["b_qkv"] = f(b.reshape(-1, P).T)
    d["w_dense"] = by_partition(i["L0_attn_w_dense"].T)
    d["b_dense"] = f(i["L0_attn_b_dense"])
    d["perm"] = f(i["L1_ffn_perm"])
    d["perm_col"] = f(d["perm"].reshape(KT, P).T)
    d["up"] = f(i["L1_ffn_up"].reshape(KT, P, -1).transpose(1, 0, 2))
    d["down"] = f(i["L1_ffn_down"].transpose(1, 0, 2))
    d["w1_qkv"] = by_partition(i["L1_attn_Wqkv"])
    d["w1_out"] = f(i["L1_attn_Wo"])
    d["b1_qkv"] = f(i["L1_attn_bqkv"].reshape(-1, P).T)
    d["b1_out"] = f(i["L1_attn_bo"])
    d["identity"] = np.eye(P, dtype=np.float32)
    lower = (np.arange(E)[None, :] < np.arange(E)[:, None]).astype(np.float32)
    d["tie"] = f(np.broadcast_to(lower.reshape(1, -1), (P, E * E)))
    raw_at = np.arange(E) % RAW * W_COLS
    d["route"] = np.concatenate([P * np.arange(1, T), P * np.arange(T) - S, np.arange(TOPK),
                                 np.diff(raw_at, prepend=0)]).astype(np.float32)
    d["index_row"] = np.arange(H, dtype=np.float32)
    d["index_col"] = f(np.arange(H, dtype=np.float32).reshape(KT, P).T)
    inv_freq = np.float32(1) / np.power(np.float32(1e6), np.arange(0, hd, 2, dtype=np.float32) / np.float32(hd))
    angle = inv_freq.astype(np.float32)[:, None] * np.arange(S, dtype=np.float32)[None, :]
    d["cos"] = f(np.tile(np.cos(angle), (2 * P // hd, 1)).astype(np.float32))
    d["sin"] = f(np.tile(np.sin(angle), (2 * P // hd, 1)).astype(np.float32))
    swap = np.zeros((P, P), np.float32)
    for o in range(P):
        if o % hd < hd // 2:
            swap[o + hd // 2, o] = -1
        else:
            swap[o - hd // 2, o] = 1
    d["swap"] = swap
    later = np.where(np.arange(P)[None, :] > np.arange(P)[:, None], np.float32(-1e30), np.float32(0))
    d["masks"] = f(np.stack([later, later.T], axis=1).astype(np.float32))
    return d


def kernel(**inputs):
    import numpy as _np
    import concourse.bacc as _bacc
    from concourse import mybir as _mybir
    from concourse.bass_utils import run_bass_kernel_spmd as _run

    nc = _bacc.Bacc("TRN2", target_bir_lowering=False, num_devices=1)
    arrays, aps = {}, {}
    for name, a in layout(inputs).items():
        arrays[f"in_{name}"] = a
        aps[name] = nc.dram_tensor(f"in_{name}", a.shape, _mybir.dt.from_np(a.dtype), kind="ExternalInput").ap()
    out = nc.dram_tensor("out", (S, H), _mybir.dt.from_np(_np.dtype("float32")), kind="ExternalOutput").ap()
    program(nc, aps, out, STAGES)
    r = _run(nc, [arrays], core_ids=[0])
    return r.results[0]["out"].reshape(1, S, H)
```
